# Optimizing a Trainium2 kernel written in Bass

```python
import numpy as np
import jax
import jax.numpy as jnp

def _softmax(x, axis=-1):
    return jax.nn.softmax(x, axis=axis)

def _gelu(x):
    return jax.nn.gelu(x, approximate=True)

def _silu(x):
    return jax.nn.silu(x)

def _sigmoid(x):
    return jax.nn.sigmoid(x)

def _layernorm(x, axis=-1, eps=1e-05):
    m = jnp.mean(x, axis=axis, keepdims=True)
    v = jnp.var(x, axis=axis, keepdims=True)
    return (x - m) / jnp.sqrt(v + eps)

def _scatter_add(tgt, idx, src, axis=0):
    return tgt.at[idx].add(src)

def _segment_sum(src, seg, n):
    return jax.ops.segment_sum(src, seg, n)
kernel_name = 'mk_flamingo_gated_d2_seqx_r8_c36bc8'

def setup_inputs(seed: int=0):
    np.random.seed(seed)
    _w = jnp.asarray

    def _rec_inputs():
        import jax
        import jax.numpy as jnp
        _rk = jax.random.key(seed)
        x = 7.22e-05 + 1 * jax.random.normal(jax.random.fold_in(_rk, 1), (8, 56, 128), jnp.float32)
        _lenS = 56 - jax.random.randint(jax.random.fold_in(_rk, 7), (8,), 0, max(1, 56 // 4) + 1, jnp.int32)
        _lenS2 = 1500 - jax.random.randint(jax.random.fold_in(_rk, 8), (8,), 0, max(1, 1500 // 4) + 1, jnp.int32)
        _ctx_1024P = jax.random.normal(jax.random.fold_in(_rk, 11), (8, 16, 128), jnp.float32)
        _ctx_1024c = jax.random.dirichlet(jax.random.fold_in(_rk, 511), 0.3 * jnp.ones((16,), jnp.float32), (8, 1500))
        _ctx_1024t = jnp.einsum('bsk,bkd->bsd', _ctx_1024c, _ctx_1024P)
        _ctx_1024t = _ctx_1024t * jax.lax.rsqrt(jnp.mean(jnp.square(_ctx_1024t)) + 1e-12) * 0.953939
        ctx_1024 = 4.13588e-05 + 0.999923 * (_ctx_1024t + 0.3 * jax.random.normal(jax.random.fold_in(_rk, 611), (8, 1500, 128), jnp.float32))
        _g = jax.random.normal(jax.random.fold_in(_rk, 9001), (2, 2), jnp.float32)
        _g = jnp.sign(_g) * jnp.maximum(jnp.abs(_g), 1.0) + (_g == 0) * 1.0
        g_xattn = _g[0]
        g_ffn = _g[1]
        return (x, ctx_1024, g_xattn, g_ffn)
    x, ctx_1024, g_xattn, g_ffn = _rec_inputs()

    def _L0_xattn_setup():
        import jax, jax.numpy as jnp
        import numpy as np
        B, S, D, H = (4, 256, 128, 16)
        DH = D // H

        def _split_heads(x):
            b, s, _ = x.shape
            return x.reshape(b, s, H, DH).transpose(0, 2, 1, 3)
        key = jax.random.key(seed)
        ks = jax.random.split(key, 11)
        scale = 1.0 / np.sqrt(D)
        inp = {'Q': jax.random.normal(ks[0], (B, S, D), jnp.float32), 'K': jax.random.normal(ks[1], (B, S, D), jnp.float32), 'V': jax.random.normal(ks[2], (B, S, D), jnp.float32), 'Wq': jax.random.normal(ks[3], (D, D), jnp.float32) * scale, 'bq': jnp.zeros((D,), jnp.float32), 'Wk': jax.random.normal(ks[4], (D, D), jnp.float32) * scale, 'bk': jnp.zeros((D,), jnp.float32), 'Wv': jax.random.normal(ks[5], (D, D), jnp.float32) * scale, 'bv': jnp.zeros((D,), jnp.float32), 'Wo': jax.random.normal(ks[6], (D, D), jnp.float32) * scale, 'bo': jnp.zeros((D,), jnp.float32)}
        return inp
    _L0_xattn_all = _L0_xattn_setup()
    _L0_xattn_in = {k: v for k, v in _L0_xattn_all.items() if k in ('Wq', 'bq', 'Wk', 'bk', 'Wv', 'bv', 'Wo', 'bo')}
    del _L0_xattn_all

    def _L0_ffn_setup():
        import jax, jax.numpy as jnp
        import numpy as np
        B, S, D, E, F = (2, 256, 128, 8, 512)
        key = jax.random.key(seed)
        ks = jax.random.split(key, 4)
        return {'hidden_states': jax.random.normal(ks[0], (B, S, D), dtype=jnp.float32), 'Wr': jax.random.normal(ks[1], (D, E), dtype=jnp.float32) * (1.0 / np.sqrt(D)), 'W1': jax.random.normal(ks[2], (E, D, F), dtype=jnp.float32) * (1.0 / np.sqrt(D)), 'b1': jnp.zeros((E, F), dtype=jnp.float32), 'W2': jax.random.normal(ks[3], (E, F, D), dtype=jnp.float32) * (1.0 / np.sqrt(F)), 'b2': jnp.zeros((E, D), dtype=jnp.float32)}
    _L0_ffn_all = _L0_ffn_setup()
    _L0_ffn_in = {k: v for k, v in _L0_ffn_all.items() if k in ('Wr', 'W1', 'b1', 'W2', 'b2')}
    del _L0_ffn_all

    def _L1_xattn_setup():
        import jax, jax.numpy as jnp
        import numpy as np
        D_MODEL = 128
        B, S = (4, 256)
        key = jax.random.key(seed)
        ks = jax.random.split(key, 10)
        s = 1.0 / np.sqrt(D_MODEL)
        return {'k': jax.random.normal(ks[0], (B, S, D_MODEL), jnp.float32), 'v': jax.random.normal(ks[1], (B, S, D_MODEL), jnp.float32), 'q': jax.random.normal(ks[2], (B, S, D_MODEL), jnp.float32), 'Wk': jax.random.normal(ks[3], (D_MODEL, D_MODEL), jnp.float32) * s, 'Wv': jax.random.normal(ks[4], (D_MODEL, D_MODEL), jnp.float32) * s, 'bv': jnp.zeros((D_MODEL,), jnp.float32), 'Wq': jax.random.normal(ks[5], (D_MODEL, D_MODEL), jnp.float32) * s, 'bq': jnp.zeros((D_MODEL,), jnp.float32), 'Wo': jax.random.normal(ks[6], (D_MODEL, D_MODEL), jnp.float32) * s, 'bo': jnp.zeros((D_MODEL,), jnp.float32)}
    _L1_xattn_all = _L1_xattn_setup()
    _L1_xattn_in = {k: v for k, v in _L1_xattn_all.items() if k in ('Wk', 'Wv', 'bv', 'Wq', 'bq', 'Wo', 'bo')}
    del _L1_xattn_all

    def _L1_ffn_setup():
        import jax, jax.numpy as jnp
        import numpy as np
        B, S, D_MODEL, D_HIDDEN = (4, 256, 128, 512)

        def act_quant(x):
            scale = 127.0 / jnp.clip(jnp.max(jnp.abs(x), axis=-1, keepdims=True), 1e-05)
            return jnp.clip(jnp.round(x * scale), -128, 127) / scale

        def weight_quant(w):
            scale = 1.0 / jnp.clip(jnp.mean(jnp.abs(w)), 1e-05)
            return jnp.clip(jnp.round(w * scale), -1, 1) / scale

        def bit_linear(x, w):
            xq = x + jax.lax.stop_gradient(act_quant(x) - x)
            wq = w + jax.lax.stop_gradient(weight_quant(w) - w)
            return jnp.einsum('bsd,hd->bsh', xq, wq)

        def depthwise_conv1d(x_bcl, w, b):
            y = jax.lax.conv_general_dilated(x_bcl, w, window_strides=(1,), padding=[(1, 1)], dimension_numbers=('NCH', 'OIH', 'NCH'), feature_group_count=x_bcl.shape[1])
            return y + b[None, :, None]
        key = jax.random.key(seed)
        ks = jax.random.split(key, 5)
        lim1 = 1.0 / np.sqrt(D_MODEL)
        lim2 = 1.0 / np.sqrt(D_HIDDEN)
        limc = 1.0 / np.sqrt(3.0)
        return {'x': jax.random.normal(ks[0], (B, S, D_MODEL), dtype=jnp.float32), 'w1': jax.random.uniform(ks[1], (D_HIDDEN, D_MODEL), jnp.float32, -lim1, lim1), 'conv_w': jax.random.uniform(ks[2], (D_HIDDEN, 1, 3), jnp.float32, -limc, limc), 'conv_b': jax.random.uniform(ks[3], (D_HIDDEN,), jnp.float32, -limc, limc), 'w2': jax.random.uniform(ks[4], (D_MODEL, D_HIDDEN), jnp.float32, -lim2, lim2)}
    _L1_ffn_all = _L1_ffn_setup()
    _L1_ffn_in = {k: v for k, v in _L1_ffn_all.items() if k in ('w1', 'conv_w', 'conv_b', 'w2')}
    del _L1_ffn_all
    return {'x': x, 'ctx_1024': ctx_1024, 'g_xattn': g_xattn, 'g_ffn': g_ffn, 'L0_xattn_Wq': _L0_xattn_in['Wq'], 'L0_xattn_bq': _L0_xattn_in['bq'], 'L0_xattn_Wk': _L0_xattn_in['Wk'], 'L0_xattn_bk': _L0_xattn_in['bk'], 'L0_xattn_Wv': _L0_xattn_in['Wv'], 'L0_xattn_bv': _L0_xattn_in['bv'], 'L0_xattn_Wo': _L0_xattn_in['Wo'], 'L0_xattn_bo': _L0_xattn_in['bo'], 'L0_ffn_Wr': _L0_ffn_in['Wr'], 'L0_ffn_W1': _L0_ffn_in['W1'], 'L0_ffn_b1': _L0_ffn_in['b1'], 'L0_ffn_W2': _L0_ffn_in['W2'], 'L0_ffn_b2': _L0_ffn_in['b2'], 'L1_xattn_Wk': _L1_xattn_in['Wk'], 'L1_xattn_Wv': _L1_xattn_in['Wv'], 'L1_xattn_bv': _L1_xattn_in['bv'], 'L1_xattn_Wq': _L1_xattn_in['Wq'], 'L1_xattn_bq': _L1_xattn_in['bq'], 'L1_xattn_Wo': _L1_xattn_in['Wo'], 'L1_xattn_bo': _L1_xattn_in['bo'], 'L1_ffn_w1': _L1_ffn_in['w1'], 'L1_ffn_conv_w': _L1_ffn_in['conv_w'], 'L1_ffn_conv_b': _L1_ffn_in['conv_b'], 'L1_ffn_w2': _L1_ffn_in['w2']}

def reference(x, ctx_1024, g_xattn, g_ffn, L0_xattn_Wq, L0_xattn_bq, L0_xattn_Wk, L0_xattn_bk, L0_xattn_Wv, L0_xattn_bv, L0_xattn_Wo, L0_xattn_bo, L0_ffn_Wr, L0_ffn_W1, L0_ffn_b1, L0_ffn_W2, L0_ffn_b2, L1_xattn_Wk, L1_xattn_Wv, L1_xattn_bv, L1_xattn_Wq, L1_xattn_bq, L1_xattn_Wo, L1_xattn_bo, L1_ffn_w1, L1_ffn_conv_w, L1_ffn_conv_b, L1_ffn_w2):
    import jax
    import jax.numpy as jnp

    def _L0_xattn_ref(Q, K, V, Wq, bq, Wk, bk, Wv, bv, Wo, bo):
        import jax, jax.numpy as jnp
        import numpy as np
        B, S, D, H = (4, 256, 128, 16)
        DH = D // H

        def _split_heads(x):
            b, s, _ = x.shape
            return x.reshape(b, s, H, DH).transpose(0, 2, 1, 3)
        q = _split_heads(Q @ Wq + bq)
        k = _split_heads(K @ Wk + bk)
        v = _split_heads(V @ Wv + bv)
        scores = jnp.einsum('bhqd,bhkd->bhqk', q, k) / jnp.sqrt(jnp.float32(DH))
        attn = jax.nn.softmax(scores, axis=-1)
        out = jnp.einsum('bhqk,bhkd->bhqd', attn, v)
        out = out.transpose(0, 2, 1, 3).reshape(Q.shape[0], -1, D)
        return out @ Wo + bo

    def _L0_ffn_ref(hidden_states, Wr, W1, b1, W2, b2):
        import jax, jax.numpy as jnp
        import numpy as np
        B, S, D, E, F = (2, 256, 128, 8, 512)
        b, s, d = hidden_states.shape
        e = Wr.shape[1]
        x = hidden_states.reshape(b * s, d)
        router_logits = x @ Wr
        router_probs = jax.nn.softmax(router_logits, axis=-1)
        expert_idx = jnp.argmax(router_probs, axis=-1)
        p_max = jnp.max(router_probs, axis=-1, keepdims=True)

        def expert_mlp(w1, bb1, w2, bb2):
            h = jax.nn.gelu(x @ w1 + bb1, approximate=False)
            return h @ w2 + bb2
        outs = jax.vmap(expert_mlp)(W1, b1, W2, b2)
        onehot = jax.nn.one_hot(expert_idx, e, dtype=x.dtype)
        next_states = jnp.einsum('te,etd->td', onehot, outs)
        out = p_max * next_states
        return out.reshape(b, s, d)

    def _L1_xattn_ref(k, v, q, Wk, Wv, bv, Wq, bq, Wo, bo):
        import jax, jax.numpy as jnp
        import numpy as np
        D_MODEL = 128
        B, S = (4, 256)
        kp = jnp.einsum('bsd,ed->bse', k, Wk)
        vp = jnp.einsum('bsd,ed->bse', v, Wv) + bv
        qp = jnp.einsum('bsd,ed->bse', q, Wq) + bq
        scale = 1.0 / jnp.sqrt(jnp.float32(kp.shape[-1]))
        scores = jnp.einsum('bqd,bkd->bqk', qp, kp) * scale
        probs = jax.nn.softmax(scores, axis=-1)
        ctx = jnp.einsum('bqk,bkd->bqd', probs, vp)
        return jnp.einsum('bqd,ed->bqe', ctx, Wo) + bo

    def _L1_ffn_ref(x, w1, conv_w, conv_b, w2):
        import jax, jax.numpy as jnp
        import numpy as np
        B, S, D_MODEL, D_HIDDEN = (4, 256, 128, 512)

        def act_quant(x):
            scale = 127.0 / jnp.clip(jnp.max(jnp.abs(x), axis=-1, keepdims=True), 1e-05)
            return jnp.clip(jnp.round(x * scale), -128, 127) / scale

        def weight_quant(w):
            scale = 1.0 / jnp.clip(jnp.mean(jnp.abs(w)), 1e-05)
            return jnp.clip(jnp.round(w * scale), -1, 1) / scale

        def bit_linear(x, w):
            xq = x + jax.lax.stop_gradient(act_quant(x) - x)
            wq = w + jax.lax.stop_gradient(weight_quant(w) - w)
            return jnp.einsum('bsd,hd->bsh', xq, wq)

        def depthwise_conv1d(x_bcl, w, b):
            y = jax.lax.conv_general_dilated(x_bcl, w, window_strides=(1,), padding=[(1, 1)], dimension_numbers=('NCH', 'OIH', 'NCH'), feature_group_count=x_bcl.shape[1])
            return y + b[None, :, None]
        h = bit_linear(x, w1)
        h = depthwise_conv1d(h.transpose(0, 2, 1), conv_w, conv_b)
        h = h.transpose(0, 2, 1)
        h = jax.nn.silu(h)
        return bit_linear(h, w2)
    x = x + jnp.tanh(g_xattn[0]) * _L0_xattn_ref(_layernorm(x, axis=-1), ctx_1024, ctx_1024, L0_xattn_Wq, L0_xattn_bq, L0_xattn_Wk, L0_xattn_bk, L0_xattn_Wv, L0_xattn_bv, L0_xattn_Wo, L0_xattn_bo)
    x = x + jnp.tanh(g_ffn[0]) * _L0_ffn_ref(_layernorm(x, axis=-1), L0_ffn_Wr, L0_ffn_W1, L0_ffn_b1, L0_ffn_W2, L0_ffn_b2)
    x = x + jnp.tanh(g_xattn[1]) * _L1_xattn_ref(ctx_1024, ctx_1024, _layernorm(x, axis=-1), L1_xattn_Wk, L1_xattn_Wv, L1_xattn_bv, L1_xattn_Wq, L1_xattn_bq, L1_xattn_Wo, L1_xattn_bo)
    x = x + jnp.tanh(g_ffn[1]) * _L1_ffn_ref(_layernorm(x, axis=-1), L1_ffn_w1, L1_ffn_conv_w, L1_ffn_conv_b, L1_ffn_w2)
    return x

_drawn_inputs = setup_inputs


def setup_inputs(seed=0):
    import zlib

    import numpy as np

    out = dict(_drawn_inputs(seed))
    spreads = {'g_ffn': (-1.0, 0.6),
     'L0_xattn_bq': (0.0, 0.1),
     'L0_xattn_bk': (0.0, 0.8),
     'L0_xattn_bv': (0.0, 0.1),
     'L0_xattn_bo': (0.0, 0.1),
     'L0_ffn_b1': (0.0, 0.479),
     'L0_ffn_b2': (0.0, 0.33),
     'L1_xattn_bv': (0.0, 0.1),
     'L1_xattn_bq': (0.0, 0.449),
     'L1_xattn_bo': (0.0, 0.1)}
    factors = {}
    for name, (base, spread) in spreads.items():
        noise = np.random.default_rng([zlib.crc32(name.encode()), seed]).standard_normal(out[name].shape)
        drawn = base * np.exp(spread * noise) if base else spread * noise
        out[name] = jnp.asarray(drawn.astype(out[name].dtype))
    for name, factor in factors.items():
        out[name] = (out[name] * factor).astype(out[name].dtype)
    return out
```

```python
import concourse.bass as bass
from concourse import mybir
from contextlib import ExitStack

NB, SQ, D = 8, 56, 128
SK = 1500
NTOK = NB * SQ
H, DH = 16, 8
KT, NT = 125, 12
CH, NCH = 500, 3
TPC = NT // NCH
HQ = H * SQ
QG, GC = 4, 224
RT = HQ // 128
VG, VC = 6, 168
OC = 2 * VC
DEN = 24
TT, NTT = 112, 4
E, F, FC = 8, 512, 4
SP1 = SQ + 2
MAGIC = 12582912.0

EARLY = {}
LATE = {}


def _offsets(table, parts):
    at = 0
    for name, n in parts:
        table[name] = (at, n)
        at += n
    return at


EARLY_N = _offsets(EARLY, [("ident", 128), ("sel", 128), ("sel2", 128), ("mask", H), ("first", E), ("wq", D), ("wk", D),
                           ("wv", D), ("bq", 1), ("bk", 1), ("bv", 1), ("bo", 1), ("gates", 4)])
LATE_N = _offsets(LATE, [("wo", D), ("woslot", 6 * D), ("wr", E), ("wq1", D), ("wk1", D), ("wv1", D),
                         ("wo1", D), ("bq1", 1), ("bv1", 1), ("bo1", 1), ("convw", FC * 3), ("convb", FC),
                         ("b1", E * FC), ("b2", D), ("fw1", F), ("fw2", F)])


def flamingo_kernel(nc, x_d, ctx_d, early_d, late_d, w1_d, w2_d, out_d):
    fp32, f32r, bf16 = mybir.dt.float32, mybir.dt.float32r, mybir.dt.bfloat16
    ALU, ACT, AX = mybir.AluOpType, mybir.ActivationFunctionType, mybir.AxisListType

    with ExitStack() as ctx:
        def sb(name, shape, dt=fp32):
            return ctx.enter_context(nc.sbuf_tensor(name, shape, dt))

        sems = {}

        def sem(name):
            if name not in sems:
                sems[name] = ctx.enter_context(nc.semaphore(name))
            return sems[name]

        early = sb("early", [128, EARLY_N])
        late = sb("late", [128, LATE_N])

        def ea(name):
            a, n = EARLY[name]
            return early[:, a:a + n]

        def la(name):
            a, n = LATE[name]
            return late[:, a:a + n]

        ident = ea("ident")
        ctx_nat = sb("ctx_nat", [128, 2, NT * D])
        ctx_T = sb("ctx_T", [128, 2, SK])
        k_hi = sb("k_hi", [128, 2, SK], f32r)
        k_lo = sb("k_lo", [128, 2, SK], f32r)
        k_st = sb("k_st", [128, 2, QG, SK], f32r)
        v_aug = sb("v_aug", [128, 2, NT, VG, 32])
        probs = sb("probs", [128, 3, HQ])
        q_f = sb("q_f", [128, NTOK])
        q_hi = sb("q_hi", [128, NTOK], f32r)
        q_lo = sb("q_lo", [128, NTOK], f32r)
        qd_hi = sb("qd_hi", [128, 2, HQ], f32r)
        qd_lo = sb("qd_lo", [128, 2, HQ], f32r)
        q_st = sb("q_st", [128, 2, HQ], f32r)
        rowmax = sb("rowmax", [128, RT * NCH])
        negmax = sb("negmax", [128, RT])
        negrow = sb("negrow", [RT, 128], f32r)
        o_all = sb("o_all", [128, NB, OC])
        recip = sb("recip", [128, OC])
        o_cur = sb("o_cur", [128, 2, OC])
        w1_sb = sb("w1_sb", [128, E * F])
        x_tok = sb("x_tok", [TT, NTT, D])
        xn = sb("xn", [TT, NTT, D])
        x_T = sb("x_T", [128, NTOK])
        stats = sb("stats", [TT, NTT, 6])
        meanvar = sb("meanvar", [TT, NTT, 2])
        rstd = sb("rstd", [TT, NTT])
        minus_half = sb("minus_half", [TT, NTT])
        tgate = sb("tgate", [128, 4])
        c0 = sb("c0", [128, 1])
        ones = sb("ones", [128, 128])
        small = sb("small", [TT, 8, NTT])
        rt = sb("rt", [TT, 4, NTT, E])
        gate_T = sb("gate_T", [E, NTOK])
        den1 = sb("den1", [128, 3])
        wsc = sb("wsc", [128, 8])
        ident_bf = sb("ident_bf", [128, 128], bf16)
        fw1_q = sb("fw1_q", [128, F], bf16)
        fw2_q = sb("fw2_q", [128, F], bf16)

        y_T = q_f
        w2_sb = v_aug[:, :, :, :, :].rearrange("p a t g c -> p (a t g c)")[:, 0:E * F]
        hid = [probs[:, 0:2, :].rearrange("p a c -> p (a c)"),
               o_all[:, :, :].rearrange("p b c -> p (b c)")[:, 0:FC * NTOK]]
        v_flat = v_aug[:, :, :, :, :].rearrange("p a t g c -> p (a t g c)")
        p_row = v_flat[:, 0:SK]
        p_T = v_flat[:, 1536:3072]
        ctx_pair = [ctx_nat[:, :, :], w1_sb[:, 0:2 * NT * D].rearrange("p (b c) -> p b c", b=2)]
        qt_pad = hid[1][:, 0:NB * 64].rearrange("p (b q) -> p b q", q=64)
        qp_T = hid[0][:, 0:NTOK]
        c_nat = hid[0][:, 448:576]
        c_T = hid[0][:, 576:1024].rearrange("p (b q) -> p b q", q=SQ)
        v1_T = hid[0][:, 1024:1472]
        hconv = v_flat[:, 0:FC * NB * SP1].rearrange("p (c b s) -> p c b s", c=FC, b=NB)

        ps = [ctx.enter_context(nc.psum_tensor(f"bank{i}", [128, 512], fp32)) for i in range(4, 8)]
        ps_all = ctx.enter_context(nc.psum_tensor("banks", [128, 4, 512], fp32))
        bank = [ps_all[:, i, :] for i in range(4)] + [p[:, :] for p in ps]
        SBANK, OBANK, MBANK = 4, 6, 7

        bank_bf = [b.bitcast(bf16) for b in bank]
        xq_view = ctx_nat[0:TT, 0, 0:NTT * D // 2].bitcast(bf16).rearrange("p (k d) -> p k d", k=NTT)
        xqT_view = ctx_nat[:, 0, 512:512 + NTOK // 2].bitcast(bf16)
        hq_view = ctx_T[0:TT, 0, 0:NTT * F // 2].bitcast(bf16)
        hqT_view = ctx_T[:, 1, 0:FC * NTOK // 2].bitcast(bf16)

        x_v = x_d.rearrange("(k p) d -> p k d", p=TT)
        out_v = out_d.rearrange("(k p) d -> p k d", p=TT)
        ctx_v = ctx_d.rearrange("b (p t) d -> b p (t d)", t=NT)
        w1_v = w1_d.rearrange("e d f -> d e f")
        w2_v = w2_d.rearrange("e (c p) d -> p e c d", p=128)

        PIECES = [("T", 0), ("K", 0), ("V", 0), ("T", 1), ("K", 1), ("V", 1), ("T", 2), ("K", 2), ("V", 2)]
        PER_T = [2, 2, 3, 2, 2, 3, 2, 2, 3]
        FIRST = [sum(PER_T[:t]) for t in range(len(PER_T))]
        SROWS = RT * NCH

        def piece_bank(b, kind, j):
            if isinstance(b, int) and b < 0:
                i = PIECES.index((kind, j))
                return i % 4 if b == -1 else (2 * j + (kind == "K")) % 4
            return MBANK

        def steps(eng, body, queries=lambda: None):
            body(-1, 0, False, False, True)
            queries()
            body(-1, 1, False, True, True)
            body(0, 0, True, True, True)
            body(0, 1, True, True, True)
            with eng.Fori(1, NB // 2 - 1) as r:
                body(r, 0, True, True, True)
                body(r, 1, True, True, True)
            body(NB // 2 - 1, 0, True, True, False)
            body(NB // 2 - 1, 1, True, False, False)

        def wait(eng, s, n):
            if isinstance(n, int) and n <= 0:
                return
            eng.wait_ge(s, n)

        block = ctx.enter_context(nc.Block())

        @block.sync
        def _(sp):
            sp.dma_start(x_tok[:, :, :], x_v).then_inc(sem("x_loaded"), 16)
            sp.dma_start(early[:, :], early_d).then_inc(sem("early_loaded"), 16)
            for n in range(2):
                sp.dma_start(ctx_nat[0:KT, n, :], ctx_v[n, :, :]).then_inc(sem(f"ctx_loaded{n}"), 16)
            sp.wait_ge(sem("ones"), 1)
            n = 2 * QG * SK // KT
            sp.dma_start(k_st[96:97, :, :, :].bitcast(fp32).rearrange("p a g (t k) -> p (a g t) k", k=KT), ones[0:n, 0:KT])\
                .then_inc(sem("k_ones"), 16)

            def body(r, par, attn, rows, keys):
                b = 2 * r + par
                o = 1 - par
                n = b + 4 if isinstance(b, int) else 3 * (NB // 2) + par - (NB // 2 + 2) * r
                load = keys and (not isinstance(b, int) or b + 4 < NB)
                if rows:
                    wait(sp, sem("st_done"), NT * b)
                    sp.wait_ge(sem("k_lo_done"), NCH * (b + 2))
                    for g in range(QG):
                        for blk, part in enumerate((k_hi, k_hi, k_lo)):
                            sp.dma_start(k_st[32 * blk:32 * blk + 32, o, g, :].bitcast(fp32),
                                         part[32 * g:32 * g + 32, o, :].bitcast(fp32)).then_inc(sem(f"k_stacked{o}"), 16)
                if rows:
                    sp.wait_ge(sem("qd_done"), b + 2)
                    for g in range(QG):
                        for blk, part in enumerate((qd_hi, qd_lo, qd_hi)):
                            if load and (g, blk) == (QG - 1, 2):
                                sp.wait_ge(sem("t_done"), NCH * (b + 3))
                            sp.dma_start(q_st[32 * blk:32 * blk + 32, o, GC * g:GC * g + GC].bitcast(fp32),
                                         part[32 * g:32 * g + 32, o, GC * g:GC * g + GC].bitcast(fp32))\
                                .then_inc(sem(f"q_stacked{o}"), 16)
                if load:
                    if not rows:
                        sp.wait_ge(sem("t_done"), NCH * (b + 3))
                    sp.dma_start(ctx_nat[0:KT, par, :], ctx_v[n, :, :]).then_inc(sem(f"ctx_loaded{par}"), 16)
                if rows:
                    sp.wait_ge(sem("negrow_done"), b + 2)
                    sp.dma_start(q_st[96:97, o, :].bitcast(fp32).rearrange("a (m c) -> a m c", m=RT),
                                 negrow[:, :].bitcast(fp32)).then_inc(sem(f"q_stacked{o}"), 16)

            steps(sp, body)

            sp.wait_ge(sem("pv_done"), NT * NB)
            sp.dma_start(w2_sb.rearrange("p (e c d) -> p e c d", e=E, c=FC), w2_v).then_inc(sem("w2_loaded"), 16)
            for p in range(1, NB // 2):
                if p == 1:
                    sp.wait_ge(sem("up_mm"), FC * E)
                if p >= 2:
                    sp.wait_ge(sem("pv1_done"), p - 1)
                for bb in range(2):
                    sp.dma_start(ctx_pair[p % 2][0:KT, bb, :], ctx_v[2 * p + bb, :, :]).then_inc(sem(f"pair_loaded{p % 2}"), 16)
            sp.wait_ge(sem("x4_done"), NTT)
            sp.dma_start(out_v, x_tok[:, :, :]).then_inc(sem("stored"), 16)
            sp.wait_ge(sem("stored"), 16)

        @block.tensor
        def _(pe):
            mm, tp = nc.tensor.matmul, nc.tensor.transpose

            def transpose_x(name):
                pe.wait_ge(sem(f"{name}_xn"), 1)
                for k in range(NTT):
                    last = tp(bank[MBANK][:, TT * k:TT * k + TT], xn[:, k, :], ident[0:TT, 0:TT])
                last.then_inc(sem(f"{name}_xnT"), 1)

            def back_to_tokens(name, src):
                pe.wait_ge(sem(f"{name}_y"), 1)
                for k in range(NTT):
                    last = tp(bank[MBANK][0:TT, D * k:D * k + D], src[:, TT * k:TT * k + TT], ident)
                last.then_inc(sem(f"{name}_yT"), 1)

            pe.wait_ge(sem("early_loaded"), 16)

            def queries():
                transpose_x("ln0")
                pe.wait_ge(sem("ln0_xT"), 1)
                mm(bank[OBANK][:, 0:NTOK], ea("wq"), x_T[:, :], start=True, stop=True).then_inc(sem("q_mm"), 1)

            def piece(b, r, par, kind, j, rows, keys):
                n, rn = b + 2, r + 1
                o = 1 - par
                m = bank[piece_bank(b, kind, j)]
                early_step = isinstance(b, int) and b < 0
                if kind == "T" and keys:
                    if j == 0:
                        pe.wait_ge(sem(f"ctx_loaded{par}"), 16 * (rn + 1))
                        if not early_step:
                            wait(pe, sem("recip_done"), b - 1)
                    if not early_step:
                        wait(pe, sem("v_done"), NCH * (b + 1) + j)
                    elif b == -1 and j == 2:
                        pe.wait_ge(sem("v_done"), 1)
                    for i in range(TPC):
                        t = TPC * j + i
                        last = tp(m[:, KT * i:KT * i + KT], ctx_nat[0:KT, par, D * t:D * t + D], ident[0:KT, 0:KT])
                    last.then_inc(sem("t_done"), 1)
                if kind == "K" and keys:
                    pe.wait_ge(sem("ctx_T_done"), NCH * n + j + 1)
                    if early_step and (b, j) == (-2, 2):
                        pe.wait_ge(sem("k_lo_done"), 1)
                    if early_step and (b, j) == (-1, 0):
                        pe.wait_ge(sem("k_lo_done"), NCH)
                    mm(m[:, 0:CH], ea("wk"), ctx_T[:, par, CH * j:CH * j + CH], start=True, stop=True)\
                        .then_inc(sem("k_mm"), 1)
                if kind == "V" and rows:
                    if keys:
                        pe.wait_ge(sem("k_lo_done"), NCH * n + j + 1)
                    else:
                        wait(pe, sem("v_done"), NCH * (b + 1) + j)
                        if j == 0:
                            wait(pe, sem("recip_done"), b - 1)
                    for i in range(TPC):
                        t = TPC * j + i
                        last = mm(m[0:KT, D * i:D * i + D], ctx_T[:, o, KT * t:KT * t + KT], ea("wv"), start=True, stop=True)
                    last.then_inc(sem("v_mm"), 1)

            def values(b, par, t):
                pe.wait_ge(sem("exp_done"), NT * b + t + 1)
                if t == 0:
                    pe.wait_ge(sem("v_done"), NCH * (b + 1))
                    wait(pe, sem("o_done"), b)
                work = [(t, g, g, VC * g) for g in range(4)]
                if t % 2:
                    work += [(t + j // 2 - 1, 4 + j % 2, j, (VC * 4, HQ - VC)[j % 2]) for j in range(4)]
                for tile, g, j, at in work:
                    second = int(g >= 4)
                    last = mm(bank[OBANK][32 * j:32 * j + 32, VC * second:VC * second + VC], v_aug[0:KT, par, tile, g, :],
                              probs[0:KT, tile % 3, at:at + VC], start=(t == 0 and not second), stop=(t == NT - 1),
                              skip_group_check=True)
                last.then_inc(sem("pv_done"), 1)

            def denominators(b, par):
                pe.wait_ge(sem("o_done"), b + 1)
                mm(bank[MBANK][:, 0:VC], ea("sel"), o_cur[:, par, 0:VC], start=True, stop=True)
                mm(bank[MBANK][:, VC:OC], ea("sel2"), o_cur[:, par, VC:OC], start=True, stop=True)\
                    .then_inc(sem("den_mm"), 1)

            def body(r, par, attn, rows, keys):
                b = 2 * r + par
                o, ro = 1 - par, r + par
                later = attn and not (isinstance(b, int) and b == 0)
                for t in range(NT):
                    rows_t = iter(range(FIRST[t], FIRST[t] + PER_T[t]) if rows and t < len(PER_T) else ())

                    def row_chunk():
                        u = next(rows_t, None)
                        if u is None:
                            return
                        c, m = u // NCH, u % NCH
                        if u == 0:
                            pe.wait_ge(sem("k_hi_done"), NCH * (b + 2))
                            pe.wait_ge(sem("qd_done"), b + 2)
                            wait(pe, sem("negrow_done"), b + 1)
                        wait(pe, sem("row_done"), SROWS * (b + 1) + u - 1)
                        mm(bank[SBANK + u % 2][:, 0:CH], qd_hi[:, o, 128 * c:128 * c + 128],
                           k_hi[:, o, CH * m:CH * m + CH], start=True, stop=True).then_inc(sem("row_mm"), 1)

                    if attn:
                        if t == 0:
                            if isinstance(b, int) and b == 0:
                                pe.wait_ge(sem("k_ones"), 16)
                                pe.wait_ge(sem("v_done"), NCH)
                                pe.wait_ge(sem("k_lo_done"), 2 * NCH)
                            pe.wait_ge(sem(f"k_stacked{par}"), 16 * 12 * (r + 1))
                            pe.wait_ge(sem(f"q_stacked{par}"), 16 * 13 * (r + 1))
                        wait(pe, sem("exp_done"), NT * b + t - 1)
                        for g in range(QG):
                            last = mm(bank[2 * (t % 2) + g // 2][0:KT, GC * (g % 2):GC * (g % 2) + GC],
                                      k_st[0:97, par, g, KT * t:KT * t + KT], q_st[0:97, par, GC * g:GC * g + GC],
                                      start=True, stop=True)
                        last.then_inc(sem("st_done"), 1)
                    row_chunk()
                    if attn and t >= 1:
                        values(b, par, t - 1)
                    elif later:
                        values(b - 1, o, NT - 1)
                    row_chunk()
                    if t < len(PIECES):
                        piece(b, r, par, *PIECES[t], rows, keys)
                    row_chunk()
                    if rows and t == 9:
                        pe.wait_ge(sem("max_done"), b + 2)
                        tp(bank[SBANK][0:RT, 0:128], negmax[:, :], ident).then_inc(sem("max_T"), 1)
                    if later and t == 10:
                        if rows:
                            pe.wait_ge(sem("v_done"), NCH * (b + 2))
                        else:
                            pe.wait_ge(sem("recip_done"), b - 1)
                        denominators(b - 1, o)

            steps(pe, body, queries)

            values(NB - 1, 1, NT - 1)
            pe.wait_ge(sem("recip_done"), NB - 1)
            denominators(NB - 1, 1)
            pe.wait_ge(sem("late_loaded"), 16)
            mm(bank[4][:, 0:1], la("wo"), ea("bv"), start=True, stop=True).then_inc(sem("c0_mm"), 1)
            pe.wait_ge(sem("norm_done"), NB)
            for s in range(6):
                a = VC * (s // 3) + SQ * (s % 3)
                last = mm(bank[5][:, 0:NTOK], la("woslot")[:, D * s:D * s + D], o_all[:, :, a:a + SQ],
                          start=(s == 0), stop=(s == 5))
            last.then_inc(sem("att0_mm"), 1)
            back_to_tokens("att0", y_T)

            transpose_x("ln1")
            pe.wait_ge(sem("ln1_xT"), 1)
            for k in range(NTT):
                last = mm(bank[6][0:TT, E * k:E * k + E], x_T[:, TT * k:TT * k + TT], la("wr"), start=True, stop=True)
            last.then_inc(sem("logits"), 1)
            pe.wait_ge(sem("w1_loaded"), 16)

            def up(e):
                for c in range(FC):
                    if e >= 1:
                        pe.wait_ge(sem("gelu_done"), FC * (e - 1) + c + 1)
                    mm(bank[c][:, 0:NTOK], w1_sb[:, F * e + 128 * c:F * e + 128 * c + 128], x_T[:, :],
                       start=True, stop=True).then_inc(sem("up_mm"), 1)

            def down(e):
                if e >= 2:
                    pe.wait_ge(sem("mix_done"), e - 1)
                pe.wait_ge(sem("gelu_done"), FC * (e + 1))
                h = hid[e % 2]
                for k in range(NTT):
                    for c in range(FC):
                        last = mm(bank[4 + e % 2][0:TT, D * k:D * k + D], h[:, NTOK * c + TT * k:NTOK * c + TT * k + TT],
                                  w2_sb[:, F * e + D * c:F * e + D * c + D], start=(c == 0), stop=(c == FC - 1))
                last.then_inc(sem("down_mm"), 1)

            up(0)
            pe.wait_ge(sem("gates"), 1)
            for k in range(NTT):
                last = tp(bank[7][0:E, TT * k:TT * k + TT], rt[:, 3, k, :], ident[0:TT, 0:TT])
            last.then_inc(sem("gates_T"), 1)
            pe.wait_ge(sem("gate_T"), 1)
            for k in range(NTT):
                last = mm(bank[6][0:TT, D * k:D * k + D], gate_T[:, TT * k:TT * k + TT], la("b2")[0:E, :], start=True, stop=True)
            last.then_inc(sem("b2_mm"), 1)
            pe.wait_ge(sem("w2_loaded"), 16)
            for e in range(1, E):
                up(e)
                down(e - 1)
            down(E - 1)

            transpose_x("ln2")
            pe.wait_ge(sem("ln2_xT"), 1)
            mm(bank[6][:, 0:NTOK], la("wq1"), x_T[:, :], start=True, stop=True).then_inc(sem("qp_mm"), 1)
            pe.wait_ge(sem("qp_T"), 1)
            mm(bank[7][:, 0:NTOK], la("wk1"), qp_T, start=True, stop=True).then_inc(sem("qt_mm"), 1)

            def pair_transposes(p):
                for bb in range(2):
                    for j in range(NCH):
                        n = 6 * p + 3 * bb + j
                        if bb == 0 and j == 0:
                            if p == 0:
                                pe.wait_ge(sem("ctx_loaded0"), 16 * (NB // 2 + 1))
                                pe.wait_ge(sem("ctx_loaded1"), 16 * (NB // 2 + 1))
                            else:
                                pe.wait_ge(sem(f"pair_loaded{p % 2}"), 32 * ((p + 1) // 2))
                            if p == 0:
                                pe.wait_ge(sem("qt_pad"), 1)
                        if n >= 2:
                            pe.wait_ge(sem("ctx1_T"), n - 1)
                        for i in range(TPC):
                            t = TPC * j + i
                            last = tp(bank[6 + n % 2][:, KT * i:KT * i + KT], ctx_pair[p % 2][0:KT, bb, D * t:D * t + D],
                                      ident[0:KT, 0:KT])
                        last.then_inc(sem("t1_done"), 1)

            def pair_scores(p):
                if p >= 1:
                    pe.wait_ge(sem("exp1_done"), p)
                else:
                    pe.wait_ge(sem("qt_pad"), 1)
                for j in range(NCH):
                    for bb in range(2):
                        pe.wait_ge(sem("ctx1_T"), 6 * p + 3 * bb + j + 1)
                        last = mm(bank[j][64 * bb:64 * bb + 64, 0:CH], qt_pad[:, 2 * p + bb, :], ctx_T[:, bb, CH * j:CH * j + CH],
                                  start=True, stop=True)
                last.then_inc(sem("s1_mm"), 1)

            pair_transposes(0)
            for p in range(NB // 2):
                pair_scores(p)
                if p + 1 < NB // 2:
                    pair_transposes(p + 1)
                pe.wait_ge(sem("exp1_done"), p + 1)
                for j in range(NCH):
                    n = NCH * p + j
                    if n >= 2:
                        pe.wait_ge(sem("p_T"), n - 1)
                    for i in range(TPC):
                        t = TPC * j + i
                        last = tp(bank[3 + n % 2][0:KT, 128 * i:128 * i + 128], p_row[:, KT * t:KT * t + KT], ident)
                    last.then_inc(sem("pt_done"), 1)
                if p >= 1:
                    pe.wait_ge(sem("c_T"), p)
                for t in range(NT):
                    if t % TPC == 0:
                        pe.wait_ge(sem("p_T"), NCH * p + t // TPC + 1)
                    for bb in range(2):
                        last = mm(bank[5][64 * bb:64 * bb + 64, 0:D], p_T[0:KT, 128 * t + 64 * bb:128 * t + 64 * bb + 64],
                                  ctx_pair[p % 2][0:KT, bb, D * t:D * t + D], start=(t == 0), stop=(t == NT - 1))
                last.then_inc(sem("pv1_done"), 1)
                pe.wait_ge(sem("c_nat"), p + 1)
                tp(bank[5][:, 0:128], c_nat, ident).then_inc(sem("c_tp"), 1)
            pe.wait_ge(sem("c_T"), NB // 2)
            mm(bank[0][:, 0:NTOK], la("wv1"), c_T, start=True, stop=True).then_inc(sem("v1_mm"), 1)
            pe.wait_ge(sem("v1_T"), 1)
            mm(bank[1][:, 0:NTOK], la("wo1"), v1_T, start=True, stop=True).then_inc(sem("att1_mm"), 1)
            back_to_tokens("att1", y_T)

            pe.wait_ge(sem("xq_done"), 1)
            pe.wait_ge(sem("ident_bf"), 1)
            for k in range(NTT):
                last = tp(bank_bf[2][:, TT * k:TT * k + TT], xq_view[:, k, :], ident_bf[0:TT, 0:TT])
            last.then_inc(sem("xq_tp"), 1)
            pe.wait_ge(sem("xs_diag"), 1)
            pe.wait_ge(sem("ones"), 1)
            for k in range(NTT):
                last = mm(bank[3][:, TT * k:TT * k + TT], ones[0:TT, :], xn[:, k, 0:TT], start=True, stop=True)
            last.then_inc(sem("xs_mm"), 1)
            pe.wait_ge(sem("xq_T"), 1)
            pe.wait_ge(sem("fw1_q"), 1)
            for c in range(FC):
                mm(bank[4 + c][:, 0:NTOK], fw1_q[:, 128 * c:128 * c + 128], xqT_view, start=True, stop=True)\
                    .then_inc(sem("h1_mm"), 1)
            for k in range(NTT):
                if k == 0:
                    pe.wait_ge(sem("silu_done"), FC)
                    pe.wait_ge(sem("h1_read"), FC)
                for c in range(FC):
                    last = tp(bank[4 + k][0:TT, 128 * c:128 * c + 128], hid[1][:, NTOK * c + TT * k:NTOK * c + TT * k + TT], ident)
                last.then_inc(sem("h_tok"), 1)
            for c in range(FC):
                if c == 0:
                    pe.wait_ge(sem("hq_done"), NTT)
                for k in range(NTT):
                    last = tp(bank_bf[c][:, TT * k:TT * k + TT], hq_view[:, F * k + 128 * c:F * k + 128 * c + 128],
                              ident_bf[0:TT, 0:TT])
                last.then_inc(sem("hq_tp"), 1)
            pe.wait_ge(sem("fw2_q"), 1)
            pe.wait_ge(sem("hq_T"), FC)
            for k in range(NTT):
                for c in range(FC):
                    last = mm(bank[4][0:TT, D * k:D * k + D], hqT_view[:, NTOK * c + TT * k:NTOK * c + TT * k + TT],
                              fw2_q[:, D * c:D * c + D], start=(c == 0), stop=(c == FC - 1))
            last.then_inc(sem("y2_mm"), 1)

        @block.scalar
        def _(act):
            A = nc.scalar.activation
            act.wait_ge(sem("early_loaded"), 16)
            A(tgate[:, :], ea("gates"), ACT.Tanh).then_inc(sem("tgate"), 1)

            def queries():
                act.wait_ge(sem("ln0_xnT"), 1)
                A(x_T[:, :], bank[MBANK][:, 0:NTOK], ACT.Copy).then_inc(sem("ln0_xT"), 1)

            def piece(b, r, par, kind, j, rows, keys):
                n = b + 2
                o = 1 - par
                m = bank[piece_bank(b, kind, j)]
                if kind == "T" and keys:
                    act.wait_ge(sem("t_done"), NCH * n + j + 1)
                    A(ctx_T[:, par, CH * j:CH * j + CH], m[:, 0:CH], ACT.Copy).then_inc(sem("ctx_T_done"), 1)
                if kind == "K" and keys:
                    act.wait_ge(sem("k_mm"), NCH * n + j + 1)
                    if j == 0:
                        if not isinstance(b, int) or b >= 0:
                            act.wait_ge(sem(f"k_stacked{par}"), 16 * 12 * (r + 1))
                            act.wait_ge(sem("row_mm"), SROWS * (b + 1))
                    A(k_hi[:, par, CH * j:CH * j + CH], m[:, 0:CH], ACT.Identity, bias=ea("bk")).then_inc(sem("k_hi_done"), 1)
                if kind == "V" and rows:
                    act.wait_ge(sem("v_mm"), NCH * (b + 1) + j + 1)
                    if j == 0:
                        wait(act, sem("pv_done"), NT * b)
                        if isinstance(b, int) and b == -1:
                            act.wait_ge(sem("v_const"), 1)
                    mv = m[0:KT, :].rearrange("p (t c) -> p t c", t=TPC)
                    for i in range(0, TPC, 2):
                        pass
                    dst = v_aug[0:KT, o, TPC * j:TPC * j + TPC, :, :]
                    A(dst[:, :, 0:5, 0:24], mv[:, :, 0:120].rearrange("p t (g c) -> p t g c", g=5), ACT.Copy)
                    A(dst[:, :, 5, 0:8], mv[:, :, 120:128], ACT.Copy).then_inc(sem("v_done"), 1)

            def body(r, par, attn, rows, keys):
                b = 2 * r + par
                for t in range(NT):
                    if attn:
                        act.wait_ge(sem("st_done"), NT * b + t + 1)
                        wait(act, sem("pv_done"), NT * b + t - 2 + t % 2)
                        A(probs[0:KT, t % 3, :].rearrange("p (a c) -> p a c", a=2),
                          ps_all[0:KT, 2 * (t % 2):2 * (t % 2) + 2, 0:2 * GC], ACT.Exp).then_inc(sem("exp_done"), 1)
                    if t < len(PIECES):
                        piece(b, r, par, *PIECES[t], rows, keys)
                    if rows and t == 9:
                        act.wait_ge(sem("max_T"), b + 2)
                        if not isinstance(b, int) or b >= 0:
                            act.wait_ge(sem(f"q_stacked{par}"), 16 * 13 * (r + 1))
                        A(negrow[:, :], bank[SBANK][0:RT, 0:128], ACT.Copy).then_inc(sem("negrow_done"), 1)

            steps(act, body, queries)

            act.wait_ge(sem("c0_mm"), 1)
            A(c0[:, :], bank[4][:, 0:1], ACT.Identity, bias=ea("bo")).then_inc(sem("c0_done"), 1)
            act.wait_ge(sem("c0_done"), 1)
            act.wait_ge(sem("att0_mm"), 1)
            A(y_T[:, :], bank[5][:, 0:NTOK], ACT.Identity, bias=c0[:, :]).then_inc(sem("att0_y"), 1)

            act.wait_ge(sem("ln1_xnT"), 1)
            A(x_T[:, :], bank[MBANK][:, 0:NTOK], ACT.Copy).then_inc(sem("ln1_xT"), 1)
            act.wait_ge(sem("rel_logits"), 1)
            A(rt[:, 1, :, :], rt[:, 0, :, :], ACT.Exp).then_inc(sem("exp_logits"), 1)
            act.wait_ge(sem("gates_T"), 1)
            A(gate_T[:, :], bank[7][0:E, 0:NTOK], ACT.Copy).then_inc(sem("gate_T"), 1)
            act.wait_ge(sem("norm_done"), NB)
            act.wait_ge(sem("att0_mm"), 1)
            for e in range(E):
                for c in range(FC):
                    act.wait_ge(sem("up_mm"), FC * e + c + 1)
                    if e >= 2 and c == 0:
                        act.wait_ge(sem("down_mm"), e - 1)
                    A(hid[e % 2][:, NTOK * c:NTOK * c + NTOK], bank[c][:, 0:NTOK], ACT.Gelu,
                      bias=la("b1")[:, FC * e + c:FC * e + c + 1]).then_inc(sem("gelu_done"), 1)

            act.wait_ge(sem("ln2_xnT"), 1)
            A(x_T[:, :], bank[MBANK][:, 0:NTOK], ACT.Copy).then_inc(sem("ln2_xT"), 1)
            act.wait_ge(sem("qp_mm"), 1)
            A(qp_T, bank[6][:, 0:NTOK], ACT.Identity, bias=la("bq1")).then_inc(sem("qp_T"), 1)
            act.wait_ge(sem("qt_mm"), 1)
            act.wait_ge(sem("qt_zero"), 1)
            A(qt_pad[:, :, 0:SQ], bank[7][:, 0:NTOK].rearrange("p (b q) -> p b q", b=NB), ACT.Copy,
              scale=float(D) ** -0.5).then_inc(sem("qt_pad"), 1)

            def evac_ctx(p):
                for bb in range(2):
                    for j in range(NCH):
                        n = 6 * p + 3 * bb + j
                        act.wait_ge(sem("t1_done"), n + 1)
                        if p >= 1 and bb == 0 and j == 0:
                            act.wait_ge(sem("s1_mm"), p)
                        A(ctx_T[:, bb, CH * j:CH * j + CH], bank[6 + n % 2][:, 0:CH], ACT.Copy).then_inc(sem("ctx1_T"), 1)

            evac_ctx(0)
            for p in range(NB // 2):
                act.wait_ge(sem("max1_done"), p + 1)
                if p >= 1:
                    act.wait_ge(sem("pt_done"), NCH * p)
                A(p_row.rearrange("p (a c) -> p a c", a=NCH), ps_all[:, 0:NCH, 0:CH], ACT.Exp, bias=den1[:, 0:1],
                  accum_out=den1[:, 1:2]).then_inc(sem("exp1_done"), 1)
                if p + 1 < NB // 2:
                    evac_ctx(p + 1)
                act.wait_ge(sem("c_tp"), p + 1)
                A(c_T[:, 2 * p:2 * p + 2, :], bank[5][:, 0:128].rearrange("p (b q) -> p b q", b=2)[:, :, 0:SQ], ACT.Copy)\
                    .then_inc(sem("c_T"), 1)
            act.wait_ge(sem("v1_mm"), 1)
            A(v1_T, bank[0][:, 0:NTOK], ACT.Identity, bias=la("bv1")).then_inc(sem("v1_T"), 1)
            act.wait_ge(sem("att1_mm"), 1)
            A(y_T[:, :], bank[1][:, 0:NTOK], ACT.Identity, bias=la("bo1")).then_inc(sem("att1_y"), 1)

            act.wait_ge(sem("xq_tp"), 1)
            A(xqT_view, bank_bf[2][:, 0:NTOK], ACT.Copy).then_inc(sem("xq_T"), 1)
            act.wait_ge(sem("xs_mm"), 1)
            A(x_T[:, :], bank[3][:, 0:NTOK], ACT.Copy).then_inc(sem("xs_row"), 1)
            for c in range(FC):
                act.wait_ge(sem("conv_done"), c + 1)
                A(hid[1][:, NTOK * c:NTOK * c + NTOK], hid[0][:, NTOK * c:NTOK * c + NTOK], ACT.Silu).then_inc(sem("silu_done"), 1)
            for c in range(FC):
                act.wait_ge(sem("hq_tp"), c + 1)
                A(hqT_view[:, NTOK * c:NTOK * c + NTOK], bank_bf[c][:, 0:NTOK], ACT.Copy).then_inc(sem("hq_T"), 1)

        @block.vector
        def _(dve):
            V = nc.vector
            chain = [0]

            def link(ins):
                chain[0] += 1
                ins.then_inc(sem("dve_chain"), 1)
                dve.wait_ge(sem("dve_chain"), chain[0])

            def layernorm(name):
                for k in range(NTT):
                    last = V.bn_stats(stats[:, k, :], x_tok[:, k, :])
                link(last)
                for k in range(NTT):
                    last = V.bn_aggr(meanvar[:, k, :], stats[:, k, :])
                last.then_inc(sem(f"{name}_var"), 1)
                dve.wait_ge(sem(f"{name}_rstd"), 1)
                for k in range(NTT):
                    last = V.tensor_scalar(xn[:, k, :], x_tok[:, k, :], meanvar[:, k, 0:1], rstd[:, k:k + 1],
                                           ALU.subtract, ALU.mult)
                last.then_inc(sem(f"{name}_xn"), 1)

            dve.wait_ge(sem("x_loaded"), 16)
            layernorm("ln0")
            for par in range(2):
                V.memset(v_aug[:, par, :, VG - 1, DH:DEN], 0.0)
                last = V.memset(v_aug[:, par, :, :, DEN:32], 0.0)
            link(last)
            for par in range(2):
                last = V.memset(v_aug[:, par, :, :, DEN], 1.0)
            last.then_inc(sem("v_const"), 1)
            dve.wait_ge(sem("early_loaded"), 16)

            def queries():
                dve.wait_ge(sem("q_mm"), 1)
                link(V.tensor_scalar(q_f[:, :], bank[OBANK][:, 0:NTOK], ea("bq"), float(DH) ** -0.5, ALU.add, ALU.mult))
                link(V.tensor_copy(q_hi[:, :], q_f[:, :]))
                V.tensor_tensor(q_lo[:, :], q_f[:, :], q_hi[:, :].bitcast(fp32), ALU.subtract).then_inc(sem("q_parts"), 1)

            def out_to_sbuf(b, par):
                dve.wait_ge(sem("pv_done"), NT * (b + 1))
                m = bank[OBANK]
                V.tensor_copy(o_cur[:, par, :], m[:, 0:OC]).then_inc(sem("o_done"), 1)

            def normalise(b, par):
                dve.wait_ge(sem("den_mm"), b + 1)
                m = bank[MBANK]
                V.reciprocal(recip[:, :], m[:, 0:OC]).then_inc(sem("recip_done"), 1)
                dve.wait_ge(sem("recip_done"), b + 1)
                V.tensor_tensor(o_all[:, b, :], o_cur[:, par, :], recip[:, :], ALU.mult).then_inc(sem("norm_done"), 1)

            def body(r, par, attn, rows, keys):
                b = 2 * r + par
                later = attn and not (isinstance(b, int) and b == 0)
                for t in range(NT):
                    if later and t == 1:
                        out_to_sbuf(b - 1, 1 - par)
                    if rows and t < len(PER_T):
                        for u in range(FIRST[t], FIRST[t] + PER_T[t]):
                            dve.wait_ge(sem("row_mm"), SROWS * (b + 1) + u + 1)
                            V.tensor_reduce(rowmax[:, u:u + 1], bank[SBANK + u % 2][:, 0:CH], AX.X, ALU.max)\
                                .then_inc(sem("row_done"), 1)
                    if t < len(PIECES):
                        kind, j = PIECES[t]
                        if kind == "K" and keys:
                            dve.wait_ge(sem("k_hi_done"), NCH * (b + 2) + j + 1)
                            V.scalar_tensor_tensor(k_lo[:, par, CH * j:CH * j + CH], bank[piece_bank(b, kind, j)][:, 0:CH], ea("bk"),
                                                   k_hi[:, par, CH * j:CH * j + CH].bitcast(fp32), ALU.add, ALU.subtract)\
                                .then_inc(sem("k_lo_done"), 1)
                    if rows and t == len(PER_T) - 1:
                        dve.wait_ge(sem("row_done"), SROWS * (b + 2))
                        V.tensor_reduce(negmax[:, :], rowmax[:, :].rearrange("p (c m) -> p c m", m=NCH), AX.X, ALU.max,
                                        negate=True).then_inc(sem("max_done"), 1)
                if later:
                    normalise(b - 1, 1 - par)

            steps(dve, body, queries)
            out_to_sbuf(NB - 1, 1)
            normalise(NB - 1, 1)

            def add_back(name, gate):
                dve.wait_ge(sem(f"{name}_yT"), 1)
                for k in range(NTT):
                    last = V.scalar_tensor_tensor(x_tok[:, k, :], bank[MBANK][0:TT, D * k:D * k + D], tgate[0:TT, gate:gate + 1],
                                                  x_tok[:, k, :], ALU.mult, ALU.add)
                link(last)

            dve.wait_ge(sem("tgate"), 1)
            add_back("att0", 0)
            layernorm("ln1")
            dve.wait_ge(sem("logits"), 1)
            lg = bank[6][0:TT, 0:NTT * E].rearrange("p (k e) -> p k e", e=E)
            bc = lambda a: a.unsqueeze(2).to_broadcast([TT, NTT, E])
            link(V.tensor_reduce(small[:, 0, :], lg, AX.X, ALU.max))
            V.tensor_tensor(rt[:, 0, :, :], lg, bc(small[:, 0, :]), ALU.subtract).then_inc(sem("rel_logits"), 1)
            dve.wait_ge(sem("rel_logits"), 1)
            link(V.tensor_scalar(rt[:, 2, :, :], rt[:, 0, :, :], 0.0, None, ALU.is_ge))
            link(V.tensor_tensor(rt[:, 2, :, :], rt[:, 2, :, :],
                                 ea("first")[0:TT, :].unsqueeze(1).to_broadcast([TT, NTT, E]), ALU.mult))
            link(V.tensor_reduce(small[:, 1, :], rt[:, 2, :, :], AX.X, ALU.max))
            link(V.tensor_tensor(rt[:, 2, :, :], rt[:, 2, :, :], bc(small[:, 1, :]), ALU.is_equal))
            dve.wait_ge(sem("exp_logits"), 1)
            link(V.tensor_reduce(small[:, 2, :], rt[:, 1, :, :], AX.X, ALU.add))
            link(V.reciprocal(small[:, 3, :], small[:, 2, :]))
            link(V.tensor_scalar(small[:, 4, :], small[:, 3, :], tgate[0:TT, 2:3], None, ALU.mult))
            V.tensor_tensor(rt[:, 3, :, :], rt[:, 2, :, :], bc(small[:, 4, :]), ALU.mult).then_inc(sem("gates"), 1)
            dve.wait_ge(sem("b2_mm"), 1)
            dve.wait_ge(sem("gates"), 1)
            x_flat = x_tok[:, :, :].rearrange("p k d -> p (k d)")
            link(V.tensor_tensor(x_flat, bank[6][0:TT, :], x_flat, ALU.add))
            for e in range(E):
                dve.wait_ge(sem("down_mm"), e + 1)
                for k in range(NTT):
                    last = V.scalar_tensor_tensor(x_tok[:, k, :], bank[4 + e % 2][0:TT, D * k:D * k + D], rt[:, 3, k, e:e + 1],
                                                  x_tok[:, k, :], ALU.mult, ALU.add)
                last.then_inc(sem("mix_done"), 1)
                dve.wait_ge(sem("mix_done"), e + 1)
            layernorm("ln2")
            V.memset(qt_pad, 0.0).then_inc(sem("qt_zero"), 1)

            def pair_max(p):
                dve.wait_ge(sem("s1_mm"), p + 1)
                V.tensor_reduce(den1[:, 0:1], ps_all[:, 0:NCH, 0:CH], AX.XY, ALU.max, negate=True).then_inc(sem("max1_done"), 1)

            for p in range(NB // 2):
                pair_max(p)
                for j in range(NCH):
                    n = NCH * p + j
                    dve.wait_ge(sem("pt_done"), n + 1)
                    if p >= 1 and j == 0:
                        dve.wait_ge(sem("pv1_done"), p)
                    V.tensor_copy(p_T[0:KT, 512 * j:512 * j + 512], bank[3 + n % 2][0:KT, :]).then_inc(sem("p_T"), 1)
                dve.wait_ge(sem("exp1_done"), p + 1)
                link(V.reciprocal(den1[:, 2:3], den1[:, 1:2]))
                dve.wait_ge(sem("pv1_done"), p + 1)
                V.tensor_scalar(c_nat, bank[5][:, 0:D], den1[:, 2:3], None, ALU.mult).then_inc(sem("c_nat"), 1)
            add_back("att1", 1)
            layernorm("ln3")

            for i, name in enumerate(("fw1", "fw2")):
                V.tensor_reduce(wsc[:, i:i + 1], la(name), AX.X, ALU.add, apply_absolute_value=True)\
                    .then_inc(sem("w_abs"), 1)
            dve.wait_ge(sem("w_mean"), 1)
            link(V.tensor_scalar(wsc[:, 4:6], wsc[:, 2:4], 1.0 / (D * F), 1e-5, ALU.mult, ALU.max))
            link(V.reciprocal(wsc[:, 6:8], wsc[:, 4:6]))
            for i, (name, q) in enumerate((("fw1", fw1_q), ("fw2", fw2_q))):
                link(V.tensor_scalar(la(name), la(name), wsc[:, 6 + i:7 + i], MAGIC, ALU.mult, ALU.add))
                link(V.tensor_scalar(la(name), la(name), MAGIC, 1.0, ALU.subtract, ALU.min))
                V.tensor_scalar(q[:, :], la(name), -1.0, None, ALU.max).then_inc(sem(f"{name}_q"), 1)
            V.tensor_copy(ident_bf[:, :], ident).then_inc(sem("ident_bf"), 1)

            def scales(src, row):
                link(V.tensor_reduce(small[:, 5, :], src, AX.X, ALU.max, apply_absolute_value=True))

            dve.wait_ge(sem("ln3_xn"), 1)
            link(V.tensor_reduce(small[:, 5, :], xn[:, :, :], AX.X, ALU.max, apply_absolute_value=True))
            link(V.tensor_scalar(small[:, 5, :], small[:, 5, :], 1e-5, None, ALU.max))
            link(V.reciprocal(small[:, 6, :], small[:, 5, :]))
            link(V.tensor_scalar(small[:, 6, :], small[:, 6, :], 127.0, None, ALU.mult))
            for k in range(NTT):
                last = V.tensor_scalar(xn[:, k, :], xn[:, k, :], small[:, 6, k:k + 1], MAGIC, ALU.mult, ALU.add)
            link(last)
            xn_flat = xn[:, :, :].rearrange("p k d -> p (k d)")
            link(V.tensor_scalar(xn_flat, xn_flat, MAGIC, 127.0, ALU.subtract, ALU.min))
            V.tensor_scalar(xq_view.rearrange("p k d -> p (k d)"), xn_flat, -128.0, None, ALU.max).then_inc(sem("xq_done"), 1)
            dve.wait_ge(sem("xq_done"), 1)
            link(V.tensor_scalar(small[:, 7, :], small[:, 5, :], wsc[0:TT, 4:5], 1.0 / 127.0, ALU.mult, ALU.mult))
            for k in range(NTT):
                last = V.tensor_scalar(xn[:, k, 0:TT], ident[0:TT, 0:TT], small[:, 7, k:k + 1], None, ALU.mult)
            last.then_inc(sem("xs_diag"), 1)
            link(V.memset(hconv, 0.0))
            dve.wait_ge(sem("xs_row"), 1)
            x_row = x_T[:, :].rearrange("p (b s) -> p b s", b=NB)
            cw, cb = la("convw"), la("convb")
            for c in range(FC):
                dve.wait_ge(sem("h1_mm"), c + 1)
                V.tensor_tensor(hconv[:, c, :, 1:1 + SQ], bank[4 + c][:, 0:NTOK].rearrange("p (b s) -> p b s", b=NB),
                                x_row, ALU.mult).then_inc(sem("h1_read"), 1)
                dve.wait_ge(sem("h1_read"), c + 1)
                y = hid[0][:, NTOK * c:NTOK * c + NTOK].rearrange("p (b s) -> p b s", b=NB)
                link(V.tensor_scalar(y, hconv[:, c, :, 0:SQ], cw[:, 3 * c:3 * c + 1], cb[:, c:c + 1], ALU.mult, ALU.add))
                link(V.scalar_tensor_tensor(y, hconv[:, c, :, 1:1 + SQ], cw[:, 3 * c + 1:3 * c + 2], y, ALU.mult, ALU.add))
                V.scalar_tensor_tensor(y, hconv[:, c, :, 2:2 + SQ], cw[:, 3 * c + 2:3 * c + 3], y, ALU.mult, ALU.add)\
                    .then_inc(sem("conv_done"), 1)
            for k in range(NTT):
                dve.wait_ge(sem("h_tok"), k + 1)
                link(V.tensor_reduce(small[:, 5, k:k + 1], bank[4 + k][0:TT, :], AX.X, ALU.max, apply_absolute_value=True))
                link(V.tensor_scalar(small[:, 5, k:k + 1], small[:, 5, k:k + 1], 1e-5, None, ALU.max))
                link(V.reciprocal(small[:, 6, k:k + 1], small[:, 5, k:k + 1]))
                link(V.tensor_scalar(small[:, 6, k:k + 1], small[:, 6, k:k + 1], 127.0, None, ALU.mult))
                t = xn[:, :, :].rearrange("p k d -> p (k d)")
                link(V.tensor_scalar(t, bank[4 + k][0:TT, :], small[:, 6, k:k + 1], MAGIC, ALU.mult, ALU.add))
                link(V.tensor_scalar(t, t, MAGIC, 127.0, ALU.subtract, ALU.min))
                V.tensor_scalar(hq_view[:, F * k:F * k + F], t, -128.0, None, ALU.max).then_inc(sem("hq_done"), 1)
                dve.wait_ge(sem("hq_done"), k + 1)
            link(V.tensor_scalar(small[:, 7, :], small[:, 5, :], wsc[0:TT, 5:6], 1.0 / 127.0, ALU.mult, ALU.mult))
            link(V.tensor_scalar(small[:, 7, :], small[:, 7, :], tgate[0:TT, 3:4], None, ALU.mult))
            dve.wait_ge(sem("y2_mm"), 1)
            for k in range(NTT):
                V.scalar_tensor_tensor(x_tok[:, k, :], bank[4][0:TT, D * k:D * k + D], small[:, 7, k:k + 1],
                                       x_tok[:, k, :], ALU.mult, ALU.add).then_inc(sem("x4_done"), 1)

        @block.gpsimd
        def _(pool):
            G = nc.gpsimd
            G.memset(minus_half[:, :], -0.5).then_inc(sem("minus_half"), 1)
            pool.wait_ge(sem("minus_half"), 1)

            def rsqrt(name):
                pool.wait_ge(sem(f"{name}_var"), 1)
                G.tensor_scalar(rstd[:, :], meanvar[:, :, 1], 1e-5, None, ALU.add).then_inc(sem(f"{name}_eps"), 1)
                pool.wait_ge(sem(f"{name}_eps"), 1)
                G.tensor_tensor(rstd[:, :], rstd[:, :], minus_half[:, :], ALU.pow).then_inc(sem(f"{name}_rstd"), 1)

            G.memset(ones[:, :], 1.0).then_inc(sem("ones"), 1)
            rsqrt("ln0")
            mask = ea("mask").unsqueeze(2).to_broadcast([128, H, SQ])
            pool.wait_ge(sem("early_loaded"), 16)
            pool.wait_ge(sem("q_parts"), 1)
            pool.dma_start(late[:, :], late_d).then_inc(sem("late_loaded"), 16)
            pool.dma_start(w1_sb[:, :].rearrange("p (e f) -> p e f", e=E), w1_v).then_inc(sem("w1_loaded"), 16)

            def body(r, par, attn, rows, keys):
                b = 2 * r + par
                o = 1 - par
                if keys:
                    if not isinstance(b, int) or b >= 0:
                        pool.wait_ge(sem("row_mm"), SROWS * (b + 1))
                        pool.wait_ge(sem(f"q_stacked{par}"), 16 * 13 * (r + 1))
                    for k, (dst, src) in enumerate(((qd_hi, q_hi), (qd_lo, q_lo))):
                        s = src[:, :].bitcast(fp32).rearrange("p (b q) -> p b q", b=NB)[:, b + 2, :]
                        last = G.tensor_tensor(dst[:, par, :].rearrange("p (h q) -> p h q", h=H),
                                               s.unsqueeze(1).to_broadcast([128, H, SQ]), mask, ALU.mult)
                    last.then_inc(sem("qd_done"), 1)

            steps(pool, body)
            rsqrt("ln1")
            rsqrt("ln2")
            pool.wait_ge(sem("ln3_var"), 1)
            G.tensor_scalar(rstd[:, :], meanvar[:, :, 1], 1e-5, None, ALU.add).then_inc(sem("ln3_eps"), 1)
            pool.wait_ge(sem("ln3_eps"), 1)
            G.tensor_tensor(rstd[:, :], rstd[:, :], minus_half[:, :], ALU.pow).then_inc(sem("ln3_rstd"), 1)
            pool.wait_ge(sem("w_abs"), 2)
            G.partition_all_reduce(wsc[:, 2:4], wsc[:, 0:2], 128, bass.bass_isa.ReduceOp.add).then_inc(sem("w_mean"), 1)


def kernel(**inputs):
    import numpy as np
    import concourse.bacc as bacc
    from concourse.bass_utils import run_bass_kernel_spmd as run

    a = {k: np.asarray(v) for k, v in inputs.items()}
    f4 = np.float32

    def pack(table, n, parts):
        out = np.zeros((128, n), f4)
        for name, arr in parts.items():
            at, w = table[name]
            out[:arr.shape[0], at:at + w] = arr
        return out

    col = lambda v: v.reshape(128, 1)
    heads = np.arange(128) // DH
    sel = np.zeros((128, 128), f4)
    for j in range(4):
        sel[32 * j + DEN, 32 * j:32 * j + 32] = 1
    sel2 = sel + np.roll(sel, 64, axis=0)
    wo = a["L0_xattn_Wo"]
    slots = np.zeros((6, 128, D), f4)
    for h in range(H):
        g, i = h // 3, h % 3
        slot = 5 if h == H - 1 else 3 * (g // 4) + i
        for row in ([32 * g + DH * i] if g < 4 else [32 * (g - 4) + DH * i, 32 * (g - 2) + DH * i]):
            slots[slot, row:row + DH] = wo[DH * h:DH * h + DH]
    gates = np.broadcast_to(np.concatenate([a["g_xattn"], a["g_ffn"]])[None], (128, 4))
    early = pack(EARLY, EARLY_N, {
        "ident": np.eye(128, dtype=f4), "sel": sel, "sel2": sel2, "mask": (heads[:, None] == np.arange(H)[None]).astype(f4),
        "first": np.broadcast_to(np.arange(E, 0, -1, dtype=f4)[None], (128, E)),
        "wq": a["L0_xattn_Wq"], "wk": a["L0_xattn_Wk"], "wv": a["L0_xattn_Wv"],
        "bq": col(a["L0_xattn_bq"]), "bk": col(a["L0_xattn_bk"]), "bv": col(a["L0_xattn_bv"]),
        "bo": col(a["L0_xattn_bo"]), "gates": gates})
    late = pack(LATE, LATE_N, {
        "wo": wo, "woslot": slots.transpose(1, 0, 2).reshape(128, 6 * D), "wr": a["L0_ffn_Wr"],
        "wq1": a["L1_xattn_Wq"].T, "wk1": a["L1_xattn_Wk"], "wv1": a["L1_xattn_Wv"].T, "wo1": a["L1_xattn_Wo"].T,
        "bq1": col(a["L1_xattn_bq"]), "bv1": col(a["L1_xattn_bv"]), "bo1": col(a["L1_xattn_bo"]),
        "convw": a["L1_ffn_conv_w"].reshape(FC, 128, 3).transpose(1, 0, 2).reshape(128, FC * 3),
        "convb": a["L1_ffn_conv_b"].reshape(FC, 128).T,
        "b1": a["L0_ffn_b1"].reshape(E * FC, 128).T, "b2": a["L0_ffn_b2"],
        "fw1": a["L1_ffn_w1"].T,
        "fw2": a["L1_ffn_w2"].reshape(D, FC, 128).transpose(2, 1, 0).reshape(128, F)})
    arrays = {"x_in": a["x"].reshape(NTOK, D), "ctx_in": a["ctx_1024"], "early_in": early, "late_in": late,
              "w1_in": a["L0_ffn_W1"], "w2_in": a["L0_ffn_W2"]}
    arrays = {k: np.ascontiguousarray(v) for k, v in arrays.items()}
    nc = bacc.Bacc("TRN2", target_bir_lowering=False, num_devices=1)
    args = [nc.dram_tensor(k, v.shape, mybir.dt.from_np(v.dtype), kind="ExternalInput").ap() for k, v in arrays.items()]
    out = nc.dram_tensor("x_out", (NTOK, D), mybir.dt.float32, kind="ExternalOutput").ap()
    flamingo_kernel(nc, *args, out)
    r = run(nc, [arrays], core_ids=[0])
    return r.results[0]["x_out"].reshape(NB, SQ, D)
```

```python
import concourse.bass as bass
from concourse import mybir
from contextlib import ExitStack

NB, SQ, D = 8, 56, 128
SK = 1500
NTOK = NB * SQ
H, DH = 16, 8
KT, NT = 125, 12
CH, NCH = 500, 3
TPC = NT // NCH
HQ = H * SQ
QG, GC = 4, 224
RT = HQ // 128
VG, VC = 6, 168
OC = 2 * VC
DEN = 24
TT, NTT = 112, 4
E, F, FC = 8, 512, 4
SP1 = SQ + 2
MAGIC = 12582912.0

EARLY = {}
LATE = {}


def _offsets(table, parts):
    at = 0
    for name, n in parts:
        table[name] = (at, n)
        at += n
    return at


EARLY_N = _offsets(EARLY, [("ident", 128), ("sel", 128), ("sel2", 128), ("mask", H), ("first", E), ("wq", D), ("wk", D),
                           ("wv", D), ("bq", 1), ("bk", 1), ("bv", 1), ("bo", 1), ("gates", 4)])
LATE_N = _offsets(LATE, [("wo", D), ("woslot", 6 * D), ("wr", E), ("wq1", D), ("wk1", D), ("wv1", D),
                         ("wo1", D), ("bq1", 1), ("bv1", 1), ("bo1", 1), ("convw", FC * 3), ("convb", FC),
                         ("b1", E * FC), ("b2", D), ("fw1", F), ("fw2", F)])


def flamingo_kernel(nc, x_d, ctx_d, early_d, late_d, w1_d, w2_d, out_d):
    fp32, f32r, bf16 = mybir.dt.float32, mybir.dt.float32r, mybir.dt.bfloat16
    ALU, ACT, AX = mybir.AluOpType, mybir.ActivationFunctionType, mybir.AxisListType

    with ExitStack() as ctx:
        def sb(name, shape, dt=fp32):
            return ctx.enter_context(nc.sbuf_tensor(name, shape, dt))

        sems = {}

        def sem(name):
            if name not in sems:
                sems[name] = ctx.enter_context(nc.semaphore(name))
            return sems[name]

        early = sb("early", [128, EARLY_N])
        late = sb("late", [128, LATE_N])

        def ea(name):
            a, n = EARLY[name]
            return early[:, a:a + n]

        def la(name):
            a, n = LATE[name]
            return late[:, a:a + n]

        ident = ea("ident")
        ctx_nat = sb("ctx_nat", [128, 2, NT * D])
        ctx_T = sb("ctx_T", [128, 2, SK])
        v_aug = sb("v_aug", [128, 2, NT, VG, 32])
        probs = sb("probs", [128, 3, HQ])
        q_f = sb("q_f", [128, NTOK])
        q_hi = sb("q_hi", [128, NTOK], f32r)
        q_lo = sb("q_lo", [128, NTOK], f32r)
        qd_hi = sb("qd_hi", [128, 2, HQ], f32r)
        qd_lo = sb("qd_lo", [128, 2, HQ], f32r)
        q_st = sb("q_st", [128, 2, HQ], f32r)
        rowmax = sb("rowmax", [128, RT * NCH])
        negmax = sb("negmax", [128, RT])
        negrow = sb("negrow", [RT, 128], f32r)
        o_all = sb("o_all", [128, NB, OC])
        recip = sb("recip", [128, OC])
        o_cur = sb("o_cur", [128, 2, OC])
        w1_sb = sb("w1_sb", [128, E * F])
        x_tok = sb("x_tok", [TT, NTT, D])
        xn = sb("xn", [TT, NTT, D])
        x_T = sb("x_T", [128, NTOK])
        stats = sb("stats", [TT, NTT, 6])
        meanvar = sb("meanvar", [TT, NTT, 2])
        rstd = sb("rstd", [TT, NTT])
        minus_half = sb("minus_half", [TT, NTT])
        tgate = sb("tgate", [128, 4])
        c0 = sb("c0", [128, 1])
        ones = sb("ones", [128, 128])
        small = sb("small", [TT, 8, NTT])
        rt = sb("rt", [TT, 4, NTT, E])
        gate_T = sb("gate_T", [E, NTOK])
        den1 = sb("den1", [128, 2, 3])
        magic = sb("magic", [128, 1])
        wsc = sb("wsc", [128, 8])
        ident_bf = sb("ident_bf", [128, 128], bf16)
        fw1_q = sb("fw1_q", [128, F], bf16)
        fw2_q = sb("fw2_q", [128, F], bf16)

        with ExitStack() as layer0:
            sb0 = lambda name, shape: layer0.enter_context(nc.sbuf_tensor(name, shape, f32r))
            k_hi = sb0("k_hi", [128, 2, SK])
            k_lo = sb0("k_lo", [128, 2, SK])
            k_st = sb0("k_st", [128, 2, QG, SK])
        ctxT_late = sb("ctxT_late", [128, 2, 2, SK])
        ctx_late = sb("ctx_late", [128, NB // 2 - 1, 2, NT * D])

        y_T = q_f
        w2_sb = v_aug[:, :, :, :, :].rearrange("p a t g c -> p (a t g c)")[:, 0:E * F]
        hid = [probs[:, 0:2, :].rearrange("p a c -> p (a c)"),
               o_all[:, :, :].rearrange("p b c -> p (b c)")[:, 0:FC * NTOK]]
        v_flat = v_aug[:, :, :, :, :].rearrange("p a t g c -> p (a t g c)")
        p_row = v_flat[:, 0:SK]
        p_T = v_flat[:, 1536:3072]
        ctx_pair = [ctx_nat[:, :, :]] + [ctx_late[:, i, :, :] for i in range(NB // 2 - 1)]
        ctxT_pair = [ctx_T[:, :, :], ctxT_late[:, 0, :, :], ctxT_late[:, 1, :, :], ctx_T[:, :, :]]
        qt_pad = hid[1][:, 0:NB * 64].rearrange("p (b q) -> p b q", q=64)
        qp_T = hid[0][:, 0:NTOK]
        c_nat = hid[0][:, 448:576]
        c_T = hid[0][:, 576:1024].rearrange("p (b q) -> p b q", q=SQ)
        v1_T = hid[0][:, 1024:1472]
        hconv = w1_sb[:, 0:FC * NB * SP1].rearrange("p (c b s) -> p c b s", c=FC, b=NB)

        ps = [ctx.enter_context(nc.psum_tensor(f"bank{i}", [128, 512], fp32)) for i in range(4, 8)]
        ps_all = ctx.enter_context(nc.psum_tensor("banks", [128, 4, 512], fp32))
        bank = [ps_all[:, i, :] for i in range(4)] + [p[:, :] for p in ps]
        SBANK, OBANK, MBANK = 4, 6, 7

        bank_bf = [b.bitcast(bf16) for b in bank]
        xq_view = ctx_nat[0:TT, 0, 0:NTT * D // 2].bitcast(bf16).rearrange("p (k d) -> p k d", k=NTT)
        xqT_view = ctx_nat[:, 0, 512:512 + NTOK // 2].bitcast(bf16)
        hq_view = ctx_T[0:TT, 0, 0:NTT * F // 2].bitcast(bf16)
        hqT_view = ctx_T[:, 1, 0:FC * NTOK // 2].bitcast(bf16)
        hq_f32 = w1_sb[0:TT, FC * NB * SP1:FC * NB * SP1 + NTT * F].rearrange("p (k f) -> p k f", k=NTT)

        x_v = x_d.rearrange("(k p) d -> p k d", p=TT)
        out_v = out_d.rearrange("(k p) d -> p k d", p=TT)
        ctx_v = ctx_d.rearrange("b (p t) d -> b p (t d)", t=NT)
        w1_v = w1_d.rearrange("e d f -> d e f")
        w2_v = w2_d.rearrange("e (c p) d -> p e c d", p=128)

        PIECES = [("T", 0), ("K", 0), ("V", 0), ("T", 1), ("K", 1), ("V", 1), ("T", 2), ("K", 2), ("V", 2)]
        PER_T = [2, 2, 3, 2, 2, 3, 2, 2, 3]
        FIRST = [sum(PER_T[:t]) for t in range(len(PER_T))]
        SROWS = RT * NCH

        def piece_bank(b, kind, j):
            if isinstance(b, int) and b < 0:
                i = PIECES.index((kind, j))
                return i % 4 if b == -1 else (2 * j + (kind == "K")) % 4
            return MBANK

        def steps(eng, body, queries=lambda: None):
            body(-1, 0, False, False, True)
            queries()
            body(-1, 1, False, True, True)
            body(0, 0, True, True, True)
            body(0, 1, True, True, True)
            with eng.Fori(1, NB // 2 - 1) as r:
                body(r, 0, True, True, True)
                body(r, 1, True, True, True)
            body(NB // 2 - 1, 0, True, True, False)
            body(NB // 2 - 1, 1, True, False, False)

        def piece1_bank(n):
            return n % 4 if n < 18 else 6 + n % 2

        def wait(eng, s, n):
            if isinstance(n, int) and n <= 0:
                return
            eng.wait_ge(s, n)

        block = ctx.enter_context(nc.Block())

        @block.sync
        def _(sp):
            sp.dma_start(x_tok[:, :, :], x_v).then_inc(sem("x_loaded"), 16)
            sp.dma_start(early[:, :], early_d).then_inc(sem("early_loaded"), 16)
            for n in range(2):
                sp.dma_start(ctx_nat[0:KT, n, :], ctx_v[n, :, :]).then_inc(sem(f"ctx_loaded{n}"), 16)
            sp.wait_ge(sem("ones"), 1)
            n = 2 * QG * SK // KT
            sp.dma_start(k_st[96:97, :, :, :].bitcast(fp32).rearrange("p a g (t k) -> p (a g t) k", k=KT), ones[0:n, 0:KT])\
                .then_inc(sem("k_ones"), 16)

            def body(r, par, attn, rows, keys):
                b = 2 * r + par
                o = 1 - par
                n = b + 4 if isinstance(b, int) else 3 * (NB // 2) + par - (NB // 2 + 2) * r
                load = keys and (not isinstance(b, int) or b + 4 < NB)
                if rows:
                    wait(sp, sem("st_done"), NT * b)
                    sp.wait_ge(sem("k_lo_done"), NCH * (b + 2))
                    for g in range(QG):
                        for blk, part in enumerate((k_hi, k_hi, k_lo)):
                            sp.dma_start(k_st[32 * blk:32 * blk + 32, o, g, :].bitcast(fp32),
                                         part[32 * g:32 * g + 32, o, :].bitcast(fp32)).then_inc(sem(f"k_stacked{o}"), 16)
                if rows:
                    sp.wait_ge(sem("qd_done"), b + 2)
                    for g in range(QG):
                        for blk, part in enumerate((qd_hi, qd_lo, qd_hi)):
                            if load and (g, blk) == (QG - 1, 2):
                                sp.wait_ge(sem("t_done"), NCH * (b + 3))
                            sp.dma_start(q_st[32 * blk:32 * blk + 32, o, GC * g:GC * g + GC].bitcast(fp32),
                                         part[32 * g:32 * g + 32, o, GC * g:GC * g + GC].bitcast(fp32))\
                                .then_inc(sem(f"q_stacked{o}"), 16)
                if load:
                    if not rows:
                        sp.wait_ge(sem("t_done"), NCH * (b + 3))
                    sp.dma_start(ctx_nat[0:KT, par, :], ctx_v[n, :, :]).then_inc(sem(f"ctx_loaded{par}"), 16)
                if rows:
                    sp.wait_ge(sem("negrow_done"), b + 2)
                    sp.dma_start(q_st[96:97, o, :].bitcast(fp32).rearrange("a (m c) -> a m c", m=RT),
                                 negrow[:, :].bitcast(fp32)).then_inc(sem(f"q_stacked{o}"), 16)

            steps(sp, body)

            sp.wait_ge(sem("pv_done"), NT * NB)
            sp.dma_start(w2_sb.rearrange("p (e c d) -> p e c d", e=E, c=FC), w2_v).then_inc(sem("w2_loaded"), 16)
            sp.wait_ge(sem("st_done"), NT * NB)
            for p in range(1, NB // 2):
                for bb in range(2):
                    sp.dma_start(ctx_pair[p][0:KT, bb, :], ctx_v[2 * p + bb, :, :]).then_inc(sem(f"pair_loaded{p}"), 16)
            sp.wait_ge(sem("x4_done"), NTT)
            sp.dma_start(out_v, x_tok[:, :, :]).then_inc(sem("stored"), 16)
            sp.wait_ge(sem("stored"), 16)

        @block.tensor
        def _(pe):
            mm, tp = nc.tensor.matmul, nc.tensor.transpose

            def transpose_x(name):
                pe.wait_ge(sem(f"{name}_xn"), 1)
                for k in range(NTT):
                    last = tp(bank[MBANK][:, TT * k:TT * k + TT], xn[:, k, :], ident[0:TT, 0:TT])
                last.then_inc(sem(f"{name}_xnT"), 1)

            def back_to_tokens(name, src):
                pe.wait_ge(sem(f"{name}_y"), 1)
                for k in range(NTT):
                    last = tp(bank[MBANK][0:TT, D * k:D * k + D], src[:, TT * k:TT * k + TT], ident)
                last.then_inc(sem(f"{name}_yT"), 1)

            pe.wait_ge(sem("early_loaded"), 16)

            def queries():
                transpose_x("ln0")
                pe.wait_ge(sem("ln0_xT"), 1)
                mm(bank[OBANK][:, 0:NTOK], ea("wq"), x_T[:, :], start=True, stop=True).then_inc(sem("q_mm"), 1)

            def piece(b, r, par, kind, j, rows, keys):
                n, rn = b + 2, r + 1
                o = 1 - par
                m = bank[piece_bank(b, kind, j)]
                early_step = isinstance(b, int) and b < 0
                if kind == "T" and keys:
                    if j == 0:
                        pe.wait_ge(sem(f"ctx_loaded{par}"), 16 * (rn + 1))
                        if not early_step:
                            wait(pe, sem("recip_done"), b - 1)
                    if not early_step:
                        wait(pe, sem("v_done"), NCH * (b + 1) + j)
                    elif b == -1 and j == 2:
                        pe.wait_ge(sem("v_done"), 1)
                    for i in range(TPC):
                        t = TPC * j + i
                        last = tp(m[:, KT * i:KT * i + KT], ctx_nat[0:KT, par, D * t:D * t + D], ident[0:KT, 0:KT])
                    last.then_inc(sem("t_done"), 1)
                if kind == "K" and keys:
                    pe.wait_ge(sem("ctx_T_done"), NCH * n + j + 1)
                    if early_step and (b, j) == (-2, 2):
                        pe.wait_ge(sem("k_lo_done"), 1)
                    if early_step and (b, j) == (-1, 0):
                        pe.wait_ge(sem("k_lo_done"), NCH)
                    mm(m[:, 0:CH], ea("wk"), ctx_T[:, par, CH * j:CH * j + CH], start=True, stop=True)\
                        .then_inc(sem("k_mm"), 1)
                if kind == "V" and rows:
                    if keys:
                        pe.wait_ge(sem("k_lo_done"), NCH * n + j + 1)
                    else:
                        wait(pe, sem("v_done"), NCH * (b + 1) + j)
                        if j == 0:
                            wait(pe, sem("recip_done"), b - 1)
                    for i in range(TPC):
                        t = TPC * j + i
                        last = mm(m[0:KT, D * i:D * i + D], ctx_T[:, o, KT * t:KT * t + KT], ea("wv"), start=True, stop=True)
                    last.then_inc(sem("v_mm"), 1)

            def values(b, par, t):
                pe.wait_ge(sem("exp_done"), NT * b + t + 1)
                if t == 0:
                    pe.wait_ge(sem("v_done"), NCH * (b + 1))
                    wait(pe, sem("o_done"), b)
                work = [(t, g, g, VC * g) for g in range(4)]
                if t % 2:
                    work += [(t + j // 2 - 1, 4 + j % 2, j, (VC * 4, HQ - VC)[j % 2]) for j in range(4)]
                for tile, g, j, at in work:
                    second = int(g >= 4)
                    last = mm(bank[OBANK][32 * j:32 * j + 32, VC * second:VC * second + VC], v_aug[0:KT, par, tile, g, :],
                              probs[0:KT, tile % 3, at:at + VC], start=(t == 0 and not second), stop=(t == NT - 1),
                              skip_group_check=True)
                last.then_inc(sem("pv_done"), 1)

            def denominators(b, par):
                pe.wait_ge(sem("o_done"), b + 1)
                mm(bank[MBANK][:, 0:VC], ea("sel"), o_cur[:, par, 0:VC], start=True, stop=True)
                mm(bank[MBANK][:, VC:OC], ea("sel2"), o_cur[:, par, VC:OC], start=True, stop=True)\
                    .then_inc(sem("den_mm"), 1)

            def body(r, par, attn, rows, keys):
                b = 2 * r + par
                o, ro = 1 - par, r + par
                later = attn and not (isinstance(b, int) and b == 0)
                for t in range(NT):
                    rows_t = iter(range(FIRST[t], FIRST[t] + PER_T[t]) if rows and t < len(PER_T) else ())

                    def row_chunk():
                        u = next(rows_t, None)
                        if u is None:
                            return
                        c, m = u // NCH, u % NCH
                        if u == 0:
                            pe.wait_ge(sem("k_hi_done"), NCH * (b + 2))
                            pe.wait_ge(sem("qd_done"), b + 2)
                            wait(pe, sem("negrow_done"), b + 1)
                        wait(pe, sem("row_done"), SROWS * (b + 1) + u - 1)
                        mm(bank[SBANK + u % 2][:, 0:CH], qd_hi[:, o, 128 * c:128 * c + 128],
                           k_hi[:, o, CH * m:CH * m + CH], start=True, stop=True).then_inc(sem("row_mm"), 1)

                    if attn:
                        if t == 0:
                            if isinstance(b, int) and b == 0:
                                pe.wait_ge(sem("k_ones"), 16)
                                pe.wait_ge(sem("v_done"), NCH)
                                pe.wait_ge(sem("k_lo_done"), 2 * NCH)
                            pe.wait_ge(sem(f"k_stacked{par}"), 16 * 12 * (r + 1))
                            pe.wait_ge(sem(f"q_stacked{par}"), 16 * 13 * (r + 1))
                        wait(pe, sem("exp_done"), NT * b + t - 1)
                        for g in range(QG):
                            last = mm(bank[2 * (t % 2) + g // 2][0:KT, GC * (g % 2):GC * (g % 2) + GC],
                                      k_st[0:97, par, g, KT * t:KT * t + KT], q_st[0:97, par, GC * g:GC * g + GC],
                                      start=True, stop=True)
                        last.then_inc(sem("st_done"), 1)
                    row_chunk()
                    if attn and t >= 1:
                        values(b, par, t - 1)
                    elif later:
                        values(b - 1, o, NT - 1)
                    row_chunk()
                    if t < len(PIECES):
                        piece(b, r, par, *PIECES[t], rows, keys)
                    row_chunk()
                    if rows and t == 9:
                        pe.wait_ge(sem("max_done"), b + 2)
                        tp(bank[SBANK][0:RT, 0:128], negmax[:, :], ident).then_inc(sem("max_T"), 1)
                    if later and t == 10:
                        if rows:
                            pe.wait_ge(sem("v_done"), NCH * (b + 2))
                        else:
                            pe.wait_ge(sem("recip_done"), b - 1)
                        denominators(b - 1, o)

            steps(pe, body, queries)

            def ctx_transposes(first, end):
                for n in range(first, end):
                    p, bb, j = n // 6, n % 6 // NCH, n % NCH
                    if n % 6 == 0:
                        if p == 0:
                            pe.wait_ge(sem("ctx_loaded0"), 16 * (NB // 2 + 1))
                            pe.wait_ge(sem("ctx_loaded1"), 16 * (NB // 2 + 1))
                        else:
                            pe.wait_ge(sem(f"pair_loaded{p}"), 32)
                    if n == 12:
                        pe.wait_ge(sem("gelu_done"), FC * E)
                    if n >= 4:
                        pe.wait_ge(sem("ctx1_T"), n - 1 if n >= 20 else n - 3)
                    for i in range(TPC):
                        t = TPC * j + i
                        last = tp(bank[piece1_bank(n)][:, KT * i:KT * i + KT], ctx_pair[p][0:KT, bb, D * t:D * t + D],
                                  ident[0:KT, 0:KT])
                    last.then_inc(sem("t1_done"), 1)

            values(NB - 1, 1, NT - 1)
            pe.wait_ge(sem("recip_done"), NB - 1)
            ctx_transposes(0, 2)
            denominators(NB - 1, 1)
            ctx_transposes(2, 6)
            pe.wait_ge(sem("late_loaded"), 16)
            mm(bank[4][:, 0:1], la("wo"), ea("bv"), start=True, stop=True).then_inc(sem("c0_mm"), 1)
            pe.wait_ge(sem("norm_done"), NB)
            for s in range(6):
                a = VC * (s // 3) + SQ * (s % 3)
                last = mm(bank[5][:, 0:NTOK], la("woslot")[:, D * s:D * s + D], o_all[:, :, a:a + SQ],
                          start=(s == 0), stop=(s == 5))
            last.then_inc(sem("att0_mm"), 1)
            back_to_tokens("att0", y_T)
            ctx_transposes(6, 12)

            transpose_x("ln1")
            pe.wait_ge(sem("ln1_xT"), 1)
            for k in range(NTT):
                last = mm(bank[6][0:TT, E * k:E * k + E], x_T[:, TT * k:TT * k + TT], la("wr"), start=True, stop=True)
            last.then_inc(sem("logits"), 1)
            pe.wait_ge(sem("w1_loaded"), 16)

            def up(e):
                for c in range(FC):
                    if e >= 1:
                        pe.wait_ge(sem("gelu_done"), FC * (e - 1) + c + 1)
                    mm(bank[c][:, 0:NTOK], w1_sb[:, F * e + 128 * c:F * e + 128 * c + 128], x_T[:, :],
                       start=True, stop=True).then_inc(sem("up_mm"), 1)

            def down(e):
                if e >= 2:
                    pe.wait_ge(sem("mix_done"), e - 1)
                pe.wait_ge(sem("gelu_done"), FC * (e + 1))
                h = hid[e % 2]
                for k in range(NTT):
                    for c in range(FC):
                        last = mm(bank[4 + e % 2][0:TT, D * k:D * k + D], h[:, NTOK * c + TT * k:NTOK * c + TT * k + TT],
                                  w2_sb[:, F * e + D * c:F * e + D * c + D], start=(c == 0), stop=(c == FC - 1))
                last.then_inc(sem("down_mm"), 1)

            pe.wait_ge(sem("ctx1_T"), 12)
            up(0)
            pe.wait_ge(sem("gates"), 1)
            for k in range(NTT):
                last = tp(bank[7][0:E, TT * k:TT * k + TT], rt[:, 3, k, :], ident[0:TT, 0:TT])
            last.then_inc(sem("gates_T"), 1)
            pe.wait_ge(sem("gate_T"), 1)
            for k in range(NTT):
                last = mm(bank[6][0:TT, D * k:D * k + D], gate_T[:, TT * k:TT * k + TT], la("b2")[0:E, :], start=True, stop=True)
            last.then_inc(sem("b2_mm"), 1)
            pe.wait_ge(sem("w2_loaded"), 16)
            for e in range(1, E):
                up(e)
                down(e - 1)
            down(E - 1)

            ctx_transposes(12, 18)
            transpose_x("ln2")
            pe.wait_ge(sem("ln2_xT"), 1)
            mm(bank[6][:, 0:NTOK], la("wq1"), x_T[:, :], start=True, stop=True).then_inc(sem("qp_mm"), 1)
            pe.wait_ge(sem("qp_T"), 1)
            mm(bank[7][:, 0:NTOK], la("wk1"), qp_T, start=True, stop=True).then_inc(sem("qt_mm"), 1)

            def pair_scores(p):
                if p >= 1:
                    pe.wait_ge(sem("exp1_done"), p)
                else:
                    pe.wait_ge(sem("qt_pad"), 1)
                    pe.wait_ge(sem("ctx1_T"), 18)
                if p == 3:
                    pe.wait_ge(sem("ctx1_T"), 24)
                for j in range(NCH):
                    for bb in range(2):
                        last = mm(bank[j][64 * bb:64 * bb + 64, 0:CH], qt_pad[:, 2 * p + bb, :],
                                  ctxT_pair[p][:, bb, CH * j:CH * j + CH], start=True, stop=True)
                last.then_inc(sem("s1_mm"), 1)

            def transpose_c(p):
                if p == 0:
                    pe.wait_ge(sem("ctx1_T"), 24)
                if p >= 2:
                    pe.wait_ge(sem("c_T"), p - 1)
                pe.wait_ge(sem("c_nat"), p + 1)
                tp(bank[6 + p % 2][:, 0:128], c_nat, ident).then_inc(sem("c_tp"), 1)

            pair_scores(0)
            ctx_transposes(18, 24)
            for p in range(NB // 2):
                if p + 1 < NB // 2:
                    pair_scores(p + 1)
                pe.wait_ge(sem("exp1_done"), p + 1)
                for j in range(NCH):
                    n = NCH * p + j
                    if n >= 2:
                        pe.wait_ge(sem("p_T"), n - 1)
                    for i in range(TPC):
                        t = TPC * j + i
                        last = tp(bank[3 + n % 2][0:KT, 128 * i:128 * i + 128], p_row[:, KT * t:KT * t + KT], ident)
                    last.then_inc(sem("pt_done"), 1)
                if p >= 1:
                    transpose_c(p - 1)
                for t in range(NT):
                    if t % TPC == 0:
                        pe.wait_ge(sem("p_T"), NCH * p + t // TPC + 1)
                    for bb in range(2):
                        last = mm(bank[5][64 * bb:64 * bb + 64, 0:D], p_T[0:KT, 128 * t + 64 * bb:128 * t + 64 * bb + 64],
                                  ctx_pair[p][0:KT, bb, D * t:D * t + D], start=(t == 0), stop=(t == NT - 1))
                last.then_inc(sem("pv1_done"), 1)
            transpose_c(NB // 2 - 1)
            pe.wait_ge(sem("c_T"), NB // 2)
            mm(bank[0][:, 0:NTOK], la("wv1"), c_T, start=True, stop=True).then_inc(sem("v1_mm"), 1)
            pe.wait_ge(sem("v1_T"), 1)
            mm(bank[1][:, 0:NTOK], la("wo1"), v1_T, start=True, stop=True).then_inc(sem("att1_mm"), 1)
            back_to_tokens("att1", y_T)

            pe.wait_ge(sem("xq_done"), 1)
            pe.wait_ge(sem("ident_bf"), 1)
            for k in range(NTT):
                last = tp(bank_bf[2][:, TT * k:TT * k + TT], xq_view[:, k, :], ident_bf[0:TT, 0:TT])
            last.then_inc(sem("xq_tp"), 1)
            pe.wait_ge(sem("xs_diag"), 1)
            pe.wait_ge(sem("ones"), 1)
            for k in range(NTT):
                last = mm(bank[3][:, TT * k:TT * k + TT], ones[0:TT, :], xn[:, k, 0:TT], start=True, stop=True)
            last.then_inc(sem("xs_mm"), 1)
            pe.wait_ge(sem("xq_T"), 1)
            pe.wait_ge(sem("fw1_q"), 1)
            for c in range(FC):
                mm(bank[4 + c][:, 0:NTOK], fw1_q[:, 128 * c:128 * c + 128], xqT_view, start=True, stop=True)\
                    .then_inc(sem("h1_mm"), 1)
            for k in range(NTT):
                if k == 0:
                    pe.wait_ge(sem("silu_done"), FC)
                    pe.wait_ge(sem("h1_read"), FC)
                for c in range(FC):
                    last = tp(bank[4 + k][0:TT, 128 * c:128 * c + 128], hid[1][:, NTOK * c + TT * k:NTOK * c + TT * k + TT], ident)
                last.then_inc(sem("h_tok"), 1)
            pe.wait_ge(sem("fw2_q"), 1)

            def hidden_transposes(k):
                pe.wait_ge(sem("hq_done"), k + 1)
                for c in range(FC):
                    last = tp(bank_bf[k][:, TT * c:TT * c + TT], hq_view[:, F * k + 128 * c:F * k + 128 * c + 128],
                              ident_bf[0:TT, 0:TT])
                last.then_inc(sem("hq_tp"), 1)

            hidden_transposes(0)
            for k in range(NTT):
                if k + 1 < NTT:
                    hidden_transposes(k + 1)
                pe.wait_ge(sem("hq_T"), k + 1)
                for c in range(FC):
                    last = mm(bank[4 + k][0:TT, 0:D], hqT_view[:, FC * TT * k + TT * c:FC * TT * k + TT * c + TT],
                              fw2_q[:, D * c:D * c + D], start=(c == 0), stop=(c == FC - 1))
                last.then_inc(sem("y2_mm"), 1)

        @block.scalar
        def _(act):
            A = nc.scalar.activation
            act.wait_ge(sem("early_loaded"), 16)
            A(tgate[:, :], ea("gates"), ACT.Tanh).then_inc(sem("tgate"), 1)

            def queries():
                act.wait_ge(sem("ln0_xnT"), 1)
                A(x_T[:, :], bank[MBANK][:, 0:NTOK], ACT.Copy).then_inc(sem("ln0_xT"), 1)

            def piece(b, r, par, kind, j, rows, keys):
                n = b + 2
                o = 1 - par
                m = bank[piece_bank(b, kind, j)]
                if kind == "T" and keys:
                    act.wait_ge(sem("t_done"), NCH * n + j + 1)
                    A(ctx_T[:, par, CH * j:CH * j + CH], m[:, 0:CH], ACT.Copy).then_inc(sem("ctx_T_done"), 1)
                if kind == "K" and keys:
                    act.wait_ge(sem("k_mm"), NCH * n + j + 1)
                    if j == 0:
                        if not isinstance(b, int) or b >= 0:
                            act.wait_ge(sem(f"k_stacked{par}"), 16 * 12 * (r + 1))
                            act.wait_ge(sem("row_mm"), SROWS * (b + 1))
                    A(k_hi[:, par, CH * j:CH * j + CH], m[:, 0:CH], ACT.Identity, bias=ea("bk")).then_inc(sem("k_hi_done"), 1)
                if kind == "V" and rows:
                    act.wait_ge(sem("v_mm"), NCH * (b + 1) + j + 1)
                    if j == 0:
                        wait(act, sem("pv_done"), NT * b)
                        if isinstance(b, int) and b == -1:
                            act.wait_ge(sem("v_const"), 1)
                    mv = m[0:KT, :].rearrange("p (t c) -> p t c", t=TPC)
                    dst = v_aug[0:KT, o, TPC * j:TPC * j + TPC, :, :]
                    A(dst[:, :, 0:5, 0:24], mv[:, :, 0:120].rearrange("p t (g c) -> p t g c", g=5), ACT.Copy)
                    A(dst[:, :, 5, 0:8], mv[:, :, 120:128], ACT.Copy).then_inc(sem("v_done"), 1)

            def body(r, par, attn, rows, keys):
                b = 2 * r + par
                for t in range(NT):
                    if attn:
                        act.wait_ge(sem("st_done"), NT * b + t + 1)
                        wait(act, sem("pv_done"), NT * b + t - 2 + t % 2)
                        A(probs[0:KT, t % 3, :].rearrange("p (a c) -> p a c", a=2),
                          ps_all[0:KT, 2 * (t % 2):2 * (t % 2) + 2, 0:2 * GC], ACT.Exp).then_inc(sem("exp_done"), 1)
                    if t < len(PIECES):
                        piece(b, r, par, *PIECES[t], rows, keys)
                    if rows and t == 9:
                        act.wait_ge(sem("max_T"), b + 2)
                        if not isinstance(b, int) or b >= 0:
                            act.wait_ge(sem(f"q_stacked{par}"), 16 * 13 * (r + 1))
                        A(negrow[:, :], bank[SBANK][0:RT, 0:128], ACT.Copy).then_inc(sem("negrow_done"), 1)

            steps(act, body, queries)

            def evac_ctx(first, end):
                for n in range(first, end):
                    act.wait_ge(sem("t1_done"), n + 1)
                    if n == 18:
                        act.wait_ge(sem("s1_mm"), 1)
                    A(ctxT_pair[n // 6][:, n % 6 // NCH, CH * (n % NCH):CH * (n % NCH) + CH],
                      bank[piece1_bank(n)][:, 0:CH], ACT.Copy).then_inc(sem("ctx1_T"), 1)

            evac_ctx(0, 6)
            act.wait_ge(sem("c0_mm"), 1)
            A(c0[:, :], bank[4][:, 0:1], ACT.Identity, bias=ea("bo")).then_inc(sem("c0_done"), 1)
            act.wait_ge(sem("c0_done"), 1)
            act.wait_ge(sem("att0_mm"), 1)
            A(y_T[:, :], bank[5][:, 0:NTOK], ACT.Identity, bias=c0[:, :]).then_inc(sem("att0_y"), 1)

            evac_ctx(6, 12)
            act.wait_ge(sem("ln1_xnT"), 1)
            A(x_T[:, :], bank[MBANK][:, 0:NTOK], ACT.Copy).then_inc(sem("ln1_xT"), 1)
            act.wait_ge(sem("rel_logits"), 1)
            A(rt[:, 1, :, :], rt[:, 0, :, :], ACT.Exp).then_inc(sem("exp_logits"), 1)
            act.wait_ge(sem("gates_T"), 1)
            A(gate_T[:, :], bank[7][0:E, 0:NTOK], ACT.Copy).then_inc(sem("gate_T"), 1)
            act.wait_ge(sem("norm_done"), NB)
            act.wait_ge(sem("att0_mm"), 1)
            for e in range(E):
                for c in range(FC):
                    act.wait_ge(sem("up_mm"), FC * e + c + 1)
                    if e >= 2 and c == 0:
                        act.wait_ge(sem("down_mm"), e - 1)
                    A(hid[e % 2][:, NTOK * c:NTOK * c + NTOK], bank[c][:, 0:NTOK], ACT.Gelu,
                      bias=la("b1")[:, FC * e + c:FC * e + c + 1]).then_inc(sem("gelu_done"), 1)

            evac_ctx(12, 18)
            act.wait_ge(sem("ln2_xnT"), 1)
            A(x_T[:, :], bank[MBANK][:, 0:NTOK], ACT.Copy).then_inc(sem("ln2_xT"), 1)
            act.wait_ge(sem("qp_mm"), 1)
            A(qp_T, bank[6][:, 0:NTOK], ACT.Identity, bias=la("bq1")).then_inc(sem("qp_T"), 1)
            act.wait_ge(sem("qt_mm"), 1)
            act.wait_ge(sem("qt_zero"), 1)
            A(qt_pad[:, :, 0:SQ], bank[7][:, 0:NTOK].rearrange("p (b q) -> p b q", b=NB), ACT.Copy,
              scale=float(D) ** -0.5).then_inc(sem("qt_pad"), 1)

            def pair_exp(p):
                act.wait_ge(sem("max1_done"), p + 1)
                if p >= 1:
                    act.wait_ge(sem("pt_done"), NCH * p)
                A(p_row.rearrange("p (a c) -> p a c", a=NCH), ps_all[:, 0:NCH, 0:CH], ACT.Exp, bias=den1[:, p % 2, 0:1],
                  accum_out=den1[:, p % 2, 1:2]).then_inc(sem("exp1_done"), 1)

            def evac_c(p):
                act.wait_ge(sem("c_tp"), p + 1)
                A(c_T[:, 2 * p:2 * p + 2, :], bank[6 + p % 2][:, 0:128].rearrange("p (b q) -> p b q", b=2)[:, :, 0:SQ], ACT.Copy)\
                    .then_inc(sem("c_T"), 1)

            pair_exp(0)
            evac_ctx(18, 24)
            for p in range(NB // 2):
                for j in range(NCH):
                    n = NCH * p + j
                    act.wait_ge(sem("pt_done"), n + 1)
                    if p >= 1 and j == 0:
                        act.wait_ge(sem("pv1_done"), p)
                    A(p_T[0:KT, 512 * j:512 * j + 512], bank[3 + n % 2][0:KT, :], ACT.Copy).then_inc(sem("p_T"), 1)
                if p >= 1:
                    evac_c(p - 1)
                if p + 1 < NB // 2:
                    pair_exp(p + 1)
            evac_c(NB // 2 - 1)
            act.wait_ge(sem("v1_mm"), 1)
            A(v1_T, bank[0][:, 0:NTOK], ACT.Identity, bias=la("bv1")).then_inc(sem("v1_T"), 1)
            act.wait_ge(sem("att1_mm"), 1)
            A(y_T[:, :], bank[1][:, 0:NTOK], ACT.Identity, bias=la("bo1")).then_inc(sem("att1_y"), 1)

            act.wait_ge(sem("xq_tp"), 1)
            A(xqT_view, bank_bf[2][:, 0:NTOK], ACT.Copy).then_inc(sem("xq_T"), 1)
            act.wait_ge(sem("xs_mm"), 1)
            A(x_T[:, :], bank[3][:, 0:NTOK], ACT.Copy).then_inc(sem("xs_row"), 1)
            def silu(c):
                act.wait_ge(sem("conv_done"), c + 1)
                A(hid[1][:, NTOK * c:NTOK * c + NTOK], hid[0][:, NTOK * c:NTOK * c + NTOK], ACT.Silu).then_inc(sem("silu_done"), 1)

            for c in range(FC):
                act.wait_ge(sem("h1_read"), c + 1)
                A(hid[0][:, NTOK * c:NTOK * c + NTOK].rearrange("p (b s) -> p b s", b=NB), hconv[:, c, :, 0:SQ], ACT.Identity,
                  scale=la("convw")[:, 3 * c:3 * c + 1], bias=la("convb")[:, c:c + 1]).then_inc(sem("tap0"), 1)
                if c >= 1:
                    silu(c - 1)
            silu(FC - 1)
            act.wait_ge(sem("h_scale"), 1)
            act.wait_ge(sem("magic"), 1)
            for k in range(NTT):
                A(hq_f32[:, k, :], bank[4 + k][0:TT, :], ACT.Identity, scale=small[:, 6, k:k + 1], bias=magic[0:TT, :]).then_inc(sem("h_round"), 1)
            for k in range(NTT):
                act.wait_ge(sem("hq_tp"), k + 1)
                A(hqT_view[:, FC * TT * k:FC * TT * (k + 1)], bank_bf[k][:, 0:FC * TT], ACT.Copy).then_inc(sem("hq_T"), 1)

        @block.vector
        def _(dve):
            V = nc.vector
            chain = [0]

            def link(ins):
                chain[0] += 1
                ins.then_inc(sem("dve_chain"), 1)
                dve.wait_ge(sem("dve_chain"), chain[0])

            def layernorm(name):
                for k in range(NTT):
                    last = V.bn_stats(stats[:, k, :], x_tok[:, k, :])
                link(last)
                for k in range(NTT):
                    last = V.bn_aggr(meanvar[:, k, :], stats[:, k, :])
                last.then_inc(sem(f"{name}_var"), 1)
                dve.wait_ge(sem(f"{name}_rstd"), 1)
                for k in range(NTT):
                    last = V.tensor_scalar(xn[:, k, :], x_tok[:, k, :], meanvar[:, k, 0:1], rstd[:, k:k + 1],
                                           ALU.subtract, ALU.mult)
                last.then_inc(sem(f"{name}_xn"), 1)

            dve.wait_ge(sem("x_loaded"), 16)
            layernorm("ln0")
            for par in range(2):
                V.memset(v_aug[:, par, :, VG - 1, DH:DEN], 0.0)
                last = V.memset(v_aug[:, par, :, :, DEN:32], 0.0)
            link(last)
            for par in range(2):
                last = V.memset(v_aug[:, par, :, :, DEN], 1.0)
            last.then_inc(sem("v_const"), 1)
            dve.wait_ge(sem("early_loaded"), 16)

            def queries():
                dve.wait_ge(sem("q_mm"), 1)
                link(V.tensor_scalar(q_f[:, :], bank[OBANK][:, 0:NTOK], ea("bq"), float(DH) ** -0.5, ALU.add, ALU.mult))
                link(V.tensor_copy(q_hi[:, :], q_f[:, :]))
                V.tensor_tensor(q_lo[:, :], q_f[:, :], q_hi[:, :].bitcast(fp32), ALU.subtract).then_inc(sem("q_parts"), 1)

            def out_to_sbuf(b, par):
                dve.wait_ge(sem("pv_done"), NT * (b + 1))
                m = bank[OBANK]
                V.tensor_copy(o_cur[:, par, :], m[:, 0:OC]).then_inc(sem("o_done"), 1)

            def normalise(b, par):
                dve.wait_ge(sem("den_mm"), b + 1)
                m = bank[MBANK]
                V.reciprocal(recip[:, :], m[:, 0:OC]).then_inc(sem("recip_done"), 1)
                dve.wait_ge(sem("recip_done"), b + 1)
                V.tensor_tensor(o_all[:, b, :], o_cur[:, par, :], recip[:, :], ALU.mult).then_inc(sem("norm_done"), 1)

            def body(r, par, attn, rows, keys):
                b = 2 * r + par
                later = attn and not (isinstance(b, int) and b == 0)
                for t in range(NT):
                    if later and t == 1:
                        out_to_sbuf(b - 1, 1 - par)
                    if rows and t < len(PER_T):
                        for u in range(FIRST[t], FIRST[t] + PER_T[t]):
                            dve.wait_ge(sem("row_mm"), SROWS * (b + 1) + u + 1)
                            V.tensor_reduce(rowmax[:, u:u + 1], bank[SBANK + u % 2][:, 0:CH], AX.X, ALU.max)\
                                .then_inc(sem("row_done"), 1)
                    if t < len(PIECES):
                        kind, j = PIECES[t]
                        if kind == "K" and keys:
                            dve.wait_ge(sem("k_hi_done"), NCH * (b + 2) + j + 1)
                            V.scalar_tensor_tensor(k_lo[:, par, CH * j:CH * j + CH], bank[piece_bank(b, kind, j)][:, 0:CH], ea("bk"),
                                                   k_hi[:, par, CH * j:CH * j + CH].bitcast(fp32), ALU.add, ALU.subtract)\
                                .then_inc(sem("k_lo_done"), 1)
                    if rows and t == len(PER_T) - 1:
                        dve.wait_ge(sem("row_done"), SROWS * (b + 2))
                        V.tensor_reduce(negmax[:, :], rowmax[:, :].rearrange("p (c m) -> p c m", m=NCH), AX.X, ALU.max,
                                        negate=True).then_inc(sem("max_done"), 1)
                if later:
                    normalise(b - 1, 1 - par)

            steps(dve, body, queries)
            out_to_sbuf(NB - 1, 1)
            normalise(NB - 1, 1)

            def add_back(name, gate):
                dve.wait_ge(sem(f"{name}_yT"), 1)
                for k in range(NTT):
                    last = V.scalar_tensor_tensor(x_tok[:, k, :], bank[MBANK][0:TT, D * k:D * k + D], tgate[0:TT, gate:gate + 1],
                                                  x_tok[:, k, :], ALU.mult, ALU.add)
                link(last)

            dve.wait_ge(sem("tgate"), 1)
            add_back("att0", 0)
            layernorm("ln1")
            dve.wait_ge(sem("logits"), 1)
            lg = bank[6][0:TT, 0:NTT * E].rearrange("p (k e) -> p k e", e=E)
            bc = lambda a: a.unsqueeze(2).to_broadcast([TT, NTT, E])
            link(V.tensor_reduce(small[:, 0, :], lg, AX.X, ALU.max))
            V.tensor_tensor(rt[:, 0, :, :], lg, bc(small[:, 0, :]), ALU.subtract).then_inc(sem("rel_logits"), 1)
            dve.wait_ge(sem("rel_logits"), 1)
            link(V.tensor_scalar(rt[:, 2, :, :], rt[:, 0, :, :], 0.0, None, ALU.is_ge))
            link(V.tensor_tensor(rt[:, 2, :, :], rt[:, 2, :, :],
                                 ea("first")[0:TT, :].unsqueeze(1).to_broadcast([TT, NTT, E]), ALU.mult))
            link(V.tensor_reduce(small[:, 1, :], rt[:, 2, :, :], AX.X, ALU.max))
            link(V.tensor_tensor(rt[:, 2, :, :], rt[:, 2, :, :], bc(small[:, 1, :]), ALU.is_equal))
            dve.wait_ge(sem("exp_logits"), 1)
            link(V.tensor_reduce(small[:, 2, :], rt[:, 1, :, :], AX.X, ALU.add))
            link(V.reciprocal(small[:, 3, :], small[:, 2, :]))
            link(V.tensor_scalar(small[:, 4, :], small[:, 3, :], tgate[0:TT, 2:3], None, ALU.mult))
            V.tensor_tensor(rt[:, 3, :, :], rt[:, 2, :, :], bc(small[:, 4, :]), ALU.mult).then_inc(sem("gates"), 1)
            dve.wait_ge(sem("b2_mm"), 1)
            dve.wait_ge(sem("gates"), 1)
            x_flat = x_tok[:, :, :].rearrange("p k d -> p (k d)")
            link(V.tensor_tensor(x_flat, bank[6][0:TT, :], x_flat, ALU.add))
            def mix(e):
                dve.wait_ge(sem("down_mm"), e + 1)
                for k in range(NTT):
                    last = V.scalar_tensor_tensor(x_tok[:, k, :], bank[4 + e % 2][0:TT, D * k:D * k + D], rt[:, 3, k, e:e + 1],
                                                  x_tok[:, k, :], ALU.mult, ALU.add)
                last.then_inc(sem("mix_done"), 1)
                dve.wait_ge(sem("mix_done"), e + 1)

            def ternary(i, name, q):
                link(V.tensor_scalar(la(name), la(name), wsc[:, 6 + i:7 + i], MAGIC, ALU.mult, ALU.add))
                link(V.tensor_scalar(la(name), la(name), MAGIC, 1.0, ALU.subtract, ALU.min))
                V.tensor_scalar(q[:, :], la(name), -1.0, None, ALU.max).then_inc(sem(f"{name}_q"), 1)

            mix(0)
            for i, name in enumerate(("fw1", "fw2")):
                V.tensor_reduce(wsc[:, i:i + 1], la(name), AX.X, ALU.add, apply_absolute_value=True)\
                    .then_inc(sem("w_abs"), 1)
            V.tensor_copy(ident_bf[:, :], ident).then_inc(sem("ident_bf"), 1)
            mix(1)
            dve.wait_ge(sem("w_mean"), 1)
            link(V.tensor_scalar(wsc[:, 4:6], wsc[:, 2:4], 1.0 / (D * F), 1e-5, ALU.mult, ALU.max))
            link(V.reciprocal(wsc[:, 6:8], wsc[:, 4:6]))
            mix(2)
            ternary(0, "fw1", fw1_q)
            mix(3)
            ternary(1, "fw2", fw2_q)
            for e in range(4, E):
                mix(e)
            layernorm("ln2")

            for p in range(NB // 2 + 1):
                if p < NB // 2:
                    dve.wait_ge(sem("s1_mm"), p + 1)
                    V.tensor_reduce(den1[:, p % 2, 0:1], ps_all[:, 0:NCH, 0:CH], AX.XY, ALU.max, negate=True)\
                        .then_inc(sem("max1_done"), 1)
                if p >= 1:
                    den = den1[:, (p - 1) % 2, :]
                    dve.wait_ge(sem("exp1_done"), p)
                    link(V.reciprocal(den[:, 2:3], den[:, 1:2]))
                    dve.wait_ge(sem("pv1_done"), p)
                    V.tensor_scalar(c_nat, bank[5][:, 0:D], den[:, 2:3], None, ALU.mult).then_inc(sem("c_nat"), 1)
            add_back("att1", 1)
            layernorm("ln3")

            dve.wait_ge(sem("ln3_xn"), 1)
            link(V.tensor_reduce(small[:, 5, :], xn[:, :, :], AX.X, ALU.max, apply_absolute_value=True))
            link(V.tensor_scalar(small[:, 5, :], small[:, 5, :], 1e-5, None, ALU.max))
            link(V.reciprocal(small[:, 6, :], small[:, 5, :]))
            link(V.tensor_scalar(small[:, 6, :], small[:, 6, :], 127.0, None, ALU.mult))
            for k in range(NTT):
                last = V.tensor_scalar(xn[:, k, :], xn[:, k, :], small[:, 6, k:k + 1], MAGIC, ALU.mult, ALU.add)
            link(last)
            xn_flat = xn[:, :, :].rearrange("p k d -> p (k d)")
            link(V.tensor_scalar(xn_flat, xn_flat, MAGIC, 127.0, ALU.subtract, ALU.min))
            V.tensor_scalar(xq_view.rearrange("p k d -> p (k d)"), xn_flat, -128.0, None, ALU.max).then_inc(sem("xq_done"), 1)
            dve.wait_ge(sem("xq_done"), 1)
            link(V.tensor_scalar(small[:, 7, :], small[:, 5, :], wsc[0:TT, 4:5], 1.0 / 127.0, ALU.mult, ALU.mult))
            for k in range(NTT):
                last = V.tensor_scalar(xn[:, k, 0:TT], ident[0:TT, 0:TT], small[:, 7, k:k + 1], None, ALU.mult)
            last.then_inc(sem("xs_diag"), 1)
            dve.wait_ge(sem("xs_row"), 1)
            dve.wait_ge(sem("conv_edges"), 1)
            x_row = x_T[:, :].rearrange("p (b s) -> p b s", b=NB)
            cw, cb = la("convw"), la("convb")
            for c in range(FC):
                dve.wait_ge(sem("h1_mm"), c + 1)
                V.tensor_tensor(hconv[:, c, :, 1:1 + SQ], bank[4 + c][:, 0:NTOK].rearrange("p (b s) -> p b s", b=NB),
                                x_row, ALU.mult).then_inc(sem("h1_read"), 1)
            for c in range(FC):
                y = hid[0][:, NTOK * c:NTOK * c + NTOK].rearrange("p (b s) -> p b s", b=NB)
                dve.wait_ge(sem("tap0"), c + 1)
                link(V.scalar_tensor_tensor(y, hconv[:, c, :, 1:1 + SQ], cw[:, 3 * c + 1:3 * c + 2], y, ALU.mult, ALU.add))
                V.scalar_tensor_tensor(y, hconv[:, c, :, 2:2 + SQ], cw[:, 3 * c + 2:3 * c + 3], y, ALU.mult, ALU.add)\
                    .then_inc(sem("conv_done"), 1)
            for k in range(NTT):
                dve.wait_ge(sem("h_tok"), k + 1)
                last = V.tensor_reduce(small[:, 5, k:k + 1], bank[4 + k][0:TT, :], AX.X, ALU.max, apply_absolute_value=True)
            link(last)
            link(V.tensor_scalar(small[:, 5, :], small[:, 5, :], 1e-5, None, ALU.max))
            link(V.reciprocal(small[:, 6, :], small[:, 5, :]))
            V.tensor_scalar(small[:, 6, :], small[:, 6, :], 127.0, None, ALU.mult).then_inc(sem("h_scale"), 1)
            link(V.tensor_scalar(small[:, 7, :], small[:, 5, :], wsc[0:TT, 5:6], 1.0 / 127.0, ALU.mult, ALU.mult))
            link(V.tensor_scalar(small[:, 7, :], small[:, 7, :], tgate[0:TT, 3:4], None, ALU.mult))
            for k in range(NTT):
                dve.wait_ge(sem("h_round"), k + 1)
                link(V.tensor_scalar(hq_f32[:, k, :], hq_f32[:, k, :], MAGIC, 127.0, ALU.subtract, ALU.min))
                V.tensor_scalar(hq_view[:, F * k:F * k + F], hq_f32[:, k, :], -128.0, None, ALU.max).then_inc(sem("hq_done"), 1)
            for k in range(NTT):
                dve.wait_ge(sem("y2_mm"), k + 1)
                V.scalar_tensor_tensor(x_tok[:, k, :], bank[4 + k][0:TT, 0:D], small[:, 7, k:k + 1],
                                       x_tok[:, k, :], ALU.mult, ALU.add).then_inc(sem("x4_done"), 1)

        @block.gpsimd
        def _(pool):
            G = nc.gpsimd
            G.memset(minus_half[:, :], -0.5).then_inc(sem("minus_half"), 1)
            pool.wait_ge(sem("minus_half"), 1)

            def rsqrt(name):
                pool.wait_ge(sem(f"{name}_var"), 1)
                G.tensor_scalar(rstd[:, :], meanvar[:, :, 1], 1e-5, None, ALU.add).then_inc(sem(f"{name}_eps"), 1)
                pool.wait_ge(sem(f"{name}_eps"), 1)
                G.tensor_tensor(rstd[:, :], rstd[:, :], minus_half[:, :], ALU.pow).then_inc(sem(f"{name}_rstd"), 1)

            G.memset(ones[:, :], 1.0).then_inc(sem("ones"), 1)
            G.memset(magic[:, :], MAGIC).then_inc(sem("magic"), 1)
            rsqrt("ln0")
            mask = ea("mask").unsqueeze(2).to_broadcast([128, H, SQ])
            pool.wait_ge(sem("early_loaded"), 16)
            pool.wait_ge(sem("q_parts"), 1)
            pool.dma_start(late[:, :], late_d).then_inc(sem("late_loaded"), 16)
            pool.dma_start(w1_sb[:, :].rearrange("p (e f) -> p e f", e=E), w1_v).then_inc(sem("w1_loaded"), 16)

            def body(r, par, attn, rows, keys):
                b = 2 * r + par
                o = 1 - par
                if keys:
                    if not isinstance(b, int) or b >= 0:
                        pool.wait_ge(sem("row_mm"), SROWS * (b + 1))
                        pool.wait_ge(sem(f"q_stacked{par}"), 16 * 13 * (r + 1))
                    for k, (dst, src) in enumerate(((qd_hi, q_hi), (qd_lo, q_lo))):
                        s = src[:, :].bitcast(fp32).rearrange("p (b q) -> p b q", b=NB)[:, b + 2, :]
                        last = G.tensor_tensor(dst[:, par, :].rearrange("p (h q) -> p h q", h=H),
                                               s.unsqueeze(1).to_broadcast([128, H, SQ]), mask, ALU.mult)
                    last.then_inc(sem("qd_done"), 1)

            steps(pool, body)
            rsqrt("ln1")
            pool.wait_ge(sem("w_abs"), 2)
            G.partition_all_reduce(wsc[:, 2:4], wsc[:, 0:2], 128, bass.bass_isa.ReduceOp.add).then_inc(sem("w_mean"), 1)
            pool.wait_ge(sem("up_mm"), FC * E)
            G.memset(hconv[:, :, :, 0], 0.0)
            G.memset(hconv[:, :, :, SP1 - 1], 0.0).then_inc(sem("conv_edges"), 1)
            pool.wait_ge(sem("down_mm"), E)
            G.memset(qt_pad, 0.0).then_inc(sem("qt_zero"), 1)
            rsqrt("ln2")
            rsqrt("ln3")


def kernel(**inputs):
    import numpy as np
    import concourse.bacc as bacc
    from concourse.bass_utils import run_bass_kernel_spmd as run

    a = {k: np.asarray(v) for k, v in inputs.items()}
    f4 = np.float32

    def pack(table, n, parts):
        out = np.zeros((128, n), f4)
        for name, arr in parts.items():
            at, w = table[name]
            out[:arr.shape[0], at:at + w] = arr
        return out

    col = lambda v: v.reshape(128, 1)
    heads = np.arange(128) // DH
    sel = np.zeros((128, 128), f4)
    for j in range(4):
        sel[32 * j + DEN, 32 * j:32 * j + 32] = 1
    sel2 = sel + np.roll(sel, 64, axis=0)
    wo = a["L0_xattn_Wo"]
    slots = np.zeros((6, 128, D), f4)
    for h in range(H):
        g, i = h // 3, h % 3
        slot = 5 if h == H - 1 else 3 * (g // 4) + i
        for row in ([32 * g + DH * i] if g < 4 else [32 * (g - 4) + DH * i, 32 * (g - 2) + DH * i]):
            slots[slot, row:row + DH] = wo[DH * h:DH * h + DH]
    gates = np.broadcast_to(np.concatenate([a["g_xattn"], a["g_ffn"]])[None], (128, 4))
    early = pack(EARLY, EARLY_N, {
        "ident": np.eye(128, dtype=f4), "sel": sel, "sel2": sel2, "mask": (heads[:, None] == np.arange(H)[None]).astype(f4),
        "first": np.broadcast_to(np.arange(E, 0, -1, dtype=f4)[None], (128, E)),
        "wq": a["L0_xattn_Wq"], "wk": a["L0_xattn_Wk"], "wv": a["L0_xattn_Wv"],
        "bq": col(a["L0_xattn_bq"]), "bk": col(a["L0_xattn_bk"]), "bv": col(a["L0_xattn_bv"]),
        "bo": col(a["L0_xattn_bo"]), "gates": gates})
    late = pack(LATE, LATE_N, {
        "wo": wo, "woslot": slots.transpose(1, 0, 2).reshape(128, 6 * D), "wr": a["L0_ffn_Wr"],
        "wq1": a["L1_xattn_Wq"].T, "wk1": a["L1_xattn_Wk"], "wv1": a["L1_xattn_Wv"].T, "wo1": a["L1_xattn_Wo"].T,
        "bq1": col(a["L1_xattn_bq"]), "bv1": col(a["L1_xattn_bv"]), "bo1": col(a["L1_xattn_bo"]),
        "convw": a["L1_ffn_conv_w"].reshape(FC, 128, 3).transpose(1, 0, 2).reshape(128, FC * 3),
        "convb": a["L1_ffn_conv_b"].reshape(FC, 128).T,
        "b1": a["L0_ffn_b1"].reshape(E * FC, 128).T, "b2": a["L0_ffn_b2"],
        "fw1": a["L1_ffn_w1"].T,
        "fw2": a["L1_ffn_w2"].reshape(D, FC, 128).transpose(2, 1, 0).reshape(128, F)})
    arrays = {"x_in": a["x"].reshape(NTOK, D), "ctx_in": a["ctx_1024"], "early_in": early, "late_in": late,
              "w1_in": a["L0_ffn_W1"], "w2_in": a["L0_ffn_W2"]}
    arrays = {k: np.ascontiguousarray(v) for k, v in arrays.items()}
    nc = bacc.Bacc("TRN2", target_bir_lowering=False, num_devices=1)
    args = [nc.dram_tensor(k, v.shape, mybir.dt.from_np(v.dtype), kind="ExternalInput").ap() for k, v in arrays.items()]
    out = nc.dram_tensor("x_out", (NTOK, D), mybir.dt.float32, kind="ExternalOutput").ap()
    flamingo_kernel(nc, *args, out)
    r = run(nc, [arrays], core_ids=[0])
    return r.results[0]["x_out"].reshape(NB, SQ, D)
```

```python
import concourse.bass as bass
from concourse import mybir
from contextlib import ExitStack

NB, SQ, D = 8, 56, 128
SK = 1500
NTOK = NB * SQ
H, DH = 16, 8
KT, NT = 125, 12
CH, NCH = 500, 3
TPC = NT // NCH
HQ = H * SQ
QG, GC = 4, 224
RT = HQ // 128
VG, VC = 6, 168
OC = 2 * VC
DEN = 24
TT, NTT = 112, 4
E, F, FC = 8, 512, 4
SP1 = SQ + 2
LAG = 4
MAGIC = 12582912.0

EARLY = {}
LATE = {}


def _offsets(table, parts):
    at = 0
    for name, n in parts:
        table[name] = (at, n)
        at += n
    return at


EARLY_N = _offsets(EARLY, [("ident", 128), ("sel", 128), ("sel2", 128), ("mask", H), ("first", E), ("wq", D), ("wk", D),
                           ("wv", D), ("bq", 1), ("bk", 1), ("bv", 1), ("bo", 1), ("gates", 4)])
LATE_N = _offsets(LATE, [("wo", D), ("woslot", 6 * D), ("wr", E), ("wq1", D), ("wk1", D), ("wv1", D),
                         ("wo1", D), ("bq1", 1), ("bv1", 1), ("bo1", 1), ("convw", FC * 3), ("convb", FC),
                         ("b1", E * FC), ("b2", D), ("fw1", F), ("fw2", F)])


def flamingo_kernel(nc, x_d, ctx_d, early_d, late_d, w1_d, w2_d, out_d):
    fp32, f32r, bf16 = mybir.dt.float32, mybir.dt.float32r, mybir.dt.bfloat16
    ALU, ACT, AX = mybir.AluOpType, mybir.ActivationFunctionType, mybir.AxisListType

    with ExitStack() as ctx:
        def sb(name, shape, dt=fp32):
            return ctx.enter_context(nc.sbuf_tensor(name, shape, dt))

        sems = {}

        def sem(name):
            if name not in sems:
                sems[name] = ctx.enter_context(nc.semaphore(name))
            return sems[name]

        early = sb("early", [128, EARLY_N])
        late = sb("late", [128, LATE_N])

        def ea(name):
            a, n = EARLY[name]
            return early[:, a:a + n]

        def la(name):
            a, n = LATE[name]
            return late[:, a:a + n]

        ident = ea("ident")
        ctx_nat = sb("ctx_nat", [128, 2, NT * D])
        ctx_T = sb("ctx_T", [128, 2, SK])
        v_aug = sb("v_aug", [128, 2, NT, VG, 32])
        probs = sb("probs", [128, 3, HQ])
        q_f = sb("q_f", [128, NTOK])
        q_hi = sb("q_hi", [128, NTOK], f32r)
        q_lo = sb("q_lo", [128, NTOK], f32r)
        qd_hi = sb("qd_hi", [128, 2, HQ], f32r)
        qd_lo = sb("qd_lo", [128, 2, HQ], f32r)
        q_st = sb("q_st", [128, 2, HQ], f32r)
        rowmax = sb("rowmax", [128, RT * NCH])
        negmax = sb("negmax", [128, RT])
        negrow = sb("negrow", [RT, 128], f32r)
        o_all = sb("o_all", [128, NB, OC])
        recip = sb("recip", [128, OC])
        o_cur = sb("o_cur", [128, 2, OC])
        w1_sb = sb("w1_sb", [128, E * F])
        x_tok = sb("x_tok", [TT, NTT, D])
        xn = sb("xn", [TT, NTT, D])
        x_T = sb("x_T", [128, NTOK])
        stats = sb("stats", [TT, NTT, 6])
        meanvar = sb("meanvar", [TT, NTT, 2])
        rstd = sb("rstd", [TT, NTT])
        minus_half = sb("minus_half", [TT, NTT])
        tgate = sb("tgate", [128, 4])
        c0 = sb("c0", [128, 3])
        wqk1 = sb("wqk1", [128, D])
        wvo1 = sb("wvo1", [128, D])
        ones = sb("ones", [128, 128])
        small = sb("small", [TT, 8, NTT])
        rt = sb("rt", [TT, 4, NTT, E])
        chosen_T = sb("chosen_T", [E, NTOK], f32r)
        pick = sb("pick", [E, E], f32r)
        den1 = sb("den1", [128, 2, 3])
        magic = sb("magic", [128, 1])
        wsc = sb("wsc", [128, 8])
        ident_bf = sb("ident_bf", [128, 128], bf16)
        fw1_q = sb("fw1_q", [128, F], bf16)
        fw2_q = sb("fw2_q", [128, F], bf16)

        with ExitStack() as layer0:
            sb0 = lambda name, shape: layer0.enter_context(nc.sbuf_tensor(name, shape, f32r))
            k_hi = sb0("k_hi", [128, 2, SK])
            k_lo = sb0("k_lo", [128, 2, SK])
            k_st = sb0("k_st", [128, 2, QG, SK])
        ctxT_1 = sb("ctxT_1", [128, 2, SK])
        ctx_late = sb("ctx_late", [128, NB // 2 - 1, 2, NT * D])

        with ExitStack() as experts:
            sbe = lambda name, shape: experts.enter_context(nc.sbuf_tensor(name, shape, f32r))
            w2_lo = sbe("w2_lo", [128, 3, F])
            h_hi = sbe("h_hi", [128, LAG + 1, NTOK])
            h_lo = sbe("h_lo", [128, LAG + 1, NTOK])
        ctxT_2 = sb("ctxT_2", [128, 2, SK])
        three = lambda a: a[:, :, :].rearrange("p a c -> p (a c)")[:, 0:3 * F].rearrange("p (a c) -> p a c", a=3)
        w1_hi, w1_lo, w2_hi = three(qd_hi), three(qd_lo), three(q_st)
        x_hi, x_lo = q_hi, q_lo

        y_T = q_f
        w2_sb = v_aug[:, :, :, :, :].rearrange("p a t g c -> p (a t g c)")[:, 0:E * F]
        hid = [probs[:, 0:2, :].rearrange("p a c -> p (a c)"),
               o_all[:, :, :].rearrange("p b c -> p (b c)")[:, 0:FC * NTOK]]
        v_flat = v_aug[:, :, :, :, :].rearrange("p a t g c -> p (a t g c)")
        p_row = v_flat[:, 0:SK]
        p_T = v_flat[:, 1536:3072]
        ctx_pair = [ctx_nat[:, :, :]] + [ctx_late[:, i, :, :] for i in range(NB // 2 - 1)]
        ctxT_pair = [ctx_T[:, :, :], ctxT_1[:, :, :], ctxT_2[:, :, :], ctx_T[:, :, :]]
        o_flat = o_all[:, :, :].rearrange("p b c -> p (b c)")
        qt_pad = o_flat[:, FC * NTOK:FC * NTOK + NB * 64].rearrange("p (b q) -> p b q", q=64)
        chosen_y = hid[1][:, 0:NTOK]
        chosen_sb = hid[1][:, NTOK:3 * NTOK].rearrange("p (a c) -> p a c", a=2)
        h_f = hid[0].rearrange("p (a c) -> p a c", a=4)
        c_nat = probs[:, 2, 0:128]
        c_T = probs[:, 2, 128:128 + NTOK].rearrange("p (b q) -> p b q", q=SQ)
        hconv = w1_sb[:, 0:FC * NB * SP1].rearrange("p (c b s) -> p c b s", c=FC, b=NB)

        ps = [ctx.enter_context(nc.psum_tensor(f"bank{i}", [128, 512], fp32)) for i in range(4, 8)]
        ps_all = ctx.enter_context(nc.psum_tensor("banks", [128, 4, 512], fp32))
        bank = [ps_all[:, i, :] for i in range(4)] + [p[:, :] for p in ps]
        SBANK, OBANK, MBANK = 4, 6, 7

        bank_bf = [b.bitcast(bf16) for b in bank]
        xq_view = ctx_nat[0:TT, 0, 0:NTT * D // 2].bitcast(bf16).rearrange("p (k d) -> p k d", k=NTT)
        xqT_view = ctx_nat[:, 0, 512:512 + NTOK // 2].bitcast(bf16)
        hq_view = ctx_T[0:TT, 0, 0:NTT * F // 2].bitcast(bf16)
        hqT_view = ctx_T[:, 1, 0:FC * NTOK // 2].bitcast(bf16)
        hq_f32 = w1_sb[0:TT, FC * NB * SP1:FC * NB * SP1 + NTT * F].rearrange("p (k f) -> p k f", k=NTT)

        x_v = x_d.rearrange("(k p) d -> p k d", p=TT)
        out_v = out_d.rearrange("(k p) d -> p k d", p=TT)
        ctx_v = ctx_d.rearrange("b (p t) d -> b p (t d)", t=NT)
        w1_v = w1_d.rearrange("e d f -> d e f")
        w2_v = w2_d.rearrange("e (c p) d -> p e c d", p=128)

        PIECES = [("T", 0), ("K", 0), ("V", 0), ("T", 1), ("K", 1), ("V", 1), ("T", 2), ("K", 2), ("V", 2)]
        PER_T = [2, 2, 3, 2, 2, 3, 2, 2, 3]
        FIRST = [sum(PER_T[:t]) for t in range(len(PER_T))]
        SROWS = RT * NCH

        FIRST_PIECES = {-2: [("T", 0), ("T", 1), ("T", 2), ("K", 0), ("K", 1), ("K", 2)],
                        -1: [("T", 0), ("T", 1), ("T", 2), ("V", 0), ("V", 1), ("V", 2), ("K", 0), ("K", 1), ("K", 2)]}

        def pieces(b):
            return FIRST_PIECES[b] if isinstance(b, int) and b < 0 else PIECES

        def piece_bank(b, kind, j):
            if isinstance(b, int) and b < 0:
                return pieces(b).index((kind, j)) % 4
            return MBANK

        def steps(eng, body, queries=lambda: None):
            queries()
            body(-1, 0, False, False, True)
            body(-1, 1, False, True, True)
            body(0, 0, True, True, True)
            body(0, 1, True, True, True)
            with eng.Fori(1, NB // 2 - 1) as r:
                body(r, 0, True, True, True)
                body(r, 1, True, True, True)
            body(NB // 2 - 1, 0, True, True, False)
            body(NB // 2 - 1, 1, True, False, False)

        EARLY_TILES = NTT - 1
        EB = EARLY_TILES * TT // SQ

        TURNS = [("P", p, j) if j < NCH else ("C", p - 1, 0) for p in range(NB // 2) for j in range(NCH + (p > 0))]
        TURNS.append(("C", NB // 2 - 1, 0))

        def turn_bank(item):
            return 3 + TURNS.index(item) % 2

        HB, HT = NB // 2, NTT // 2
        HN = HT * TT
        HALF_BANKS = [(6, 7), (0, 1)]

        def q_count(r, par):
            return 16 * 13 * (r + 1) - (0 if par else 16 * 12)

        def act_rounds(n):
            return n % 4 != 0

        def dve_rounds(name, e):
            return name == "w1_parts" or e < 3

        def piece1_bank(n):
            return n % 4 if n < 18 else 6 + n % 2

        def wait(eng, s, n):
            if isinstance(n, int) and n <= 0:
                return
            eng.wait_ge(s, n)

        block = ctx.enter_context(nc.Block())

        @block.sync
        def _(sp):
            sp.dma_start(x_tok[:, :, :], x_v).then_inc(sem("x_loaded"), 16)
            sp.dma_start(early[:, :], early_d).then_inc(sem("early_loaded"), 16)
            for n in range(2):
                sp.dma_start(ctx_nat[0:KT, n, :], ctx_v[n, :, :]).then_inc(sem(f"ctx_loaded{n}"), 16)
            sp.wait_ge(sem("ones"), 1)
            n = 2 * QG * SK // KT
            sp.dma_start(k_st[96:97, :, :, :].bitcast(fp32).rearrange("p a g (t k) -> p (a g t) k", k=KT), ones[0:n, 0:KT])\
                .then_inc(sem("k_ones"), 16)

            def body(r, par, attn, rows, keys):
                b = 2 * r + par
                o = 1 - par
                n = b + 4 if isinstance(b, int) else 3 * (NB // 2) + par - (NB // 2 + 2) * r
                load = keys and (not isinstance(b, int) or b + 4 < NB)
                first = isinstance(b, int) and b == -1
                if rows:
                    wait(sp, sem("st_done"), NT * b)
                    sp.wait_ge(sem("k_lo_done"), NCH * (b + 2))
                    for g in range(QG):
                        for blk, part in enumerate((k_hi, k_hi, k_lo)):
                            sp.dma_start(k_st[32 * blk:32 * blk + 32, o, g, :].bitcast(fp32),
                                         part[32 * g:32 * g + 32, o, :].bitcast(fp32)).then_inc(sem(f"k_stacked{o}"), 16)
                if rows and not first:
                    sp.wait_ge(sem("qd_done"), b + 2)
                    for g in range(QG):
                        for blk, part in enumerate((qd_hi, qd_lo, qd_hi)):
                            if load and (g, blk) == (QG - 1, 2):
                                sp.wait_ge(sem("t_done"), NCH * (b + 3))
                            sp.dma_start(q_st[32 * blk:32 * blk + 32, o, GC * g:GC * g + GC].bitcast(fp32),
                                         part[32 * g:32 * g + 32, o, GC * g:GC * g + GC].bitcast(fp32))\
                                .then_inc(sem(f"q_stacked{o}"), 16)
                if load:
                    if not rows or first:
                        sp.wait_ge(sem("t_done"), NCH * (b + 3))
                    sp.dma_start(ctx_nat[0:KT, par, :], ctx_v[n, :, :]).then_inc(sem(f"ctx_loaded{par}"), 16)
                if rows:
                    sp.wait_ge(sem("negrow_done"), b + 2)
                    sp.dma_start(q_st[96:97, o, :].bitcast(fp32).rearrange("a (m c) -> a m c", m=RT),
                                 negrow[:, :].bitcast(fp32)).then_inc(sem(f"q_stacked{o}"), 16)

            steps(sp, body)

            def load_pair(p):
                for bb in range(2):
                    sp.dma_start(ctx_pair[p][0:KT, bb, :], ctx_v[2 * p + bb, :, :]).then_inc(sem(f"pair_loaded{p}"), 16)

            sp.wait_ge(sem("k_stacked1"), 16 * 12 * NB // 2)
            sp.wait_ge(sem("st_done"), NT * (NB - 1))
            load_pair(1)
            load_pair(2)
            sp.wait_ge(sem("pv_done"), NT * NB)
            sp.dma_start(w2_sb.rearrange("p (e c d) -> p e c d", e=E, c=FC), w2_v).then_inc(sem("w2_loaded"), 16)
            sp.wait_ge(sem("st_done"), NT * NB)
            load_pair(3)
            for hf in range(2):
                half = slice(HT * hf, HT * hf + HT)
                sp.wait_ge(sem("x4_done"), HT * (hf + 1))
                sp.dma_start(out_v[:, half, :], x_tok[:, half, :]).then_inc(sem("stored"), 16)
            sp.wait_ge(sem("stored"), 32)

        @block.tensor
        def _(pe):
            mm, tp = nc.tensor.matmul, nc.tensor.transpose

            def transpose_x(name):
                pe.wait_ge(sem(f"{name}_xn"), 1)
                for k in range(NTT):
                    last = tp(bank[MBANK][:, TT * k:TT * k + TT], xn[:, k, :], ident[0:TT, 0:TT])
                last.then_inc(sem(f"{name}_xnT"), 1)

            def back_to_tokens(name, src):
                pe.wait_ge(sem(f"{name}_y"), 1)
                for k in range(NTT):
                    last = tp(bank[MBANK][0:TT, D * k:D * k + D], src[:, TT * k:TT * k + TT], ident)
                last.then_inc(sem(f"{name}_yT"), 1)

            pe.wait_ge(sem("ones"), 1)
            for _ in range(13):
                mm(bank[0][:, 0:128], ones[:, :], ones[:, :], start=True, stop=True)
            pe.wait_ge(sem("early_loaded"), 16)

            def queries():
                transpose_x("ln0")
                pe.wait_ge(sem("ln0_xT"), 1)
                mm(bank[OBANK][:, 0:NTOK], ea("wq"), x_T[:, :], start=True, stop=True).then_inc(sem("q_mm"), 1)

            def piece(b, r, par, kind, j, rows, keys):
                n, rn = b + 2, r + 1
                o = 1 - par
                m = bank[piece_bank(b, kind, j)]
                early_step = isinstance(b, int) and b < 0
                held = {(-1, "T", 0): ("k_lo_done", 2), (-1, "T", 1): ("k_lo_done", 3), (-1, "V", 1): ("ctx_T_done", 4),
                        (-1, "V", 2): ("ctx_T_done", 5), (-1, "K", 0): ("ctx_T_done", 6), (-1, "K", 1): ("v_done", 1),
                        (-1, "K", 2): ("v_done", 2)}.get((b, kind, j) if early_step else None)
                if held:
                    pe.wait_ge(sem(held[0]), held[1])
                if kind == "T" and keys:
                    if j == 0:
                        pe.wait_ge(sem(f"ctx_loaded{par}"), 16 * (rn + 1))
                        if not early_step:
                            wait(pe, sem("recip_done"), b - 1)
                    if not early_step:
                        wait(pe, sem("v_done"), NCH * (b + 1) + j)
                    for i in range(TPC):
                        t = TPC * j + i
                        last = tp(m[:, KT * i:KT * i + KT], ctx_nat[0:KT, par, D * t:D * t + D], ident[0:KT, 0:KT])
                    last.then_inc(sem("t_done"), 1)
                if kind == "K" and keys:
                    pe.wait_ge(sem("ctx_T_done"), NCH * n + j + 1)
                    mm(m[:, 0:CH], ea("wk"), ctx_T[:, par, CH * j:CH * j + CH], start=True, stop=True)\
                        .then_inc(sem("k_mm"), 1)
                if kind == "V" and rows:
                    if keys and not early_step:
                        pe.wait_ge(sem("k_lo_done"), NCH * n + j + 1)
                    elif not keys:
                        wait(pe, sem("v_done"), NCH * (b + 1) + j)
                        if j == 0:
                            wait(pe, sem("recip_done"), b - 1)
                    for i in range(TPC):
                        t = TPC * j + i
                        last = mm(m[0:KT, D * i:D * i + D], ctx_T[:, o, KT * t:KT * t + KT], ea("wv"), start=True, stop=True)
                    last.then_inc(sem("v_mm"), 1)

            def values(b, par, t):
                pe.wait_ge(sem("exp_done"), NT * b + t + 1)
                if t == 0:
                    pe.wait_ge(sem("v_done"), NCH * (b + 1))
                    wait(pe, sem("o_done"), b)
                work = [(t, g, g, VC * g) for g in range(4)]
                if t % 2:
                    work += [(t + j // 2 - 1, 4 + j % 2, j, (VC * 4, HQ - VC)[j % 2]) for j in range(4)]
                for tile, g, j, at in work:
                    second = int(g >= 4)
                    last = mm(bank[OBANK][32 * j:32 * j + 32, VC * second:VC * second + VC], v_aug[0:KT, par, tile, g, :],
                              probs[0:KT, tile % 3, at:at + VC], start=(t == 0 and not second), stop=(t == NT - 1),
                              skip_group_check=True)
                last.then_inc(sem("pv_done"), 1)

            def denominators(b, par):
                pe.wait_ge(sem("o_done"), b + 1)
                mm(bank[MBANK][:, 0:VC], ea("sel"), o_cur[:, par, 0:VC], start=True, stop=True)
                mm(bank[MBANK][:, VC:OC], ea("sel2"), o_cur[:, par, VC:OC], start=True, stop=True)\
                    .then_inc(sem("den_mm"), 1)

            def folded_weights():
                pe.wait_ge(sem("late_loaded"), 16)
                pe.wait_ge(sem("negrow_done"), NB)
                mm(bank[4][:, 0:1], la("wo"), ea("bv"), start=True, stop=True)
                mm(bank[4][:, 1:2], la("wk1"), la("bq1"), start=True, stop=True)
                mm(bank[4][:, 2:3], la("wo1"), la("bv1"), start=True, stop=True)
                mm(bank[4][:, 128:256], la("wq1"), la("wk1"), start=True, stop=True)
                mm(bank[4][:, 256:384], la("wv1"), la("wo1"), start=True, stop=True).then_inc(sem("folded_mm"), 1)

            def output_slot(s, b0, b1):
                a = VC * (s // 3) + SQ * (s % 3)
                ins = mm(bank[5][:, SQ * b0:SQ * b1], la("woslot")[:, D * s:D * s + D], o_all[:, b0:b1, a:a + SQ],
                         start=(s == 0), stop=(s == 5), skip_group_check=True)
                if s == 5:
                    ins.then_inc(sem("att0_mm"), 1)

            def attention_to_tokens(ks, m, part):
                pe.wait_ge(sem("att0_y"), part)
                for k in ks:
                    last = tp(m[0:TT, D * k:D * k + D], y_T[:, TT * k:TT * k + TT], ident)
                last.then_inc(sem("att0_yT"), 1)

            def beside_last_batch(t):
                if t == 1:
                    folded_weights()
                if t == 2:
                    pe.wait_ge(sem("row_done"), SROWS * NB)
                    pe.wait_ge(sem("norm_done"), EB)
                if 2 <= t < 8:
                    output_slot(t - 2, 0, EB)
                if t == 9:
                    attention_to_tokens(range(EARLY_TILES), bank[4], 1)

            def body(r, par, attn, rows, keys):
                b = 2 * r + par
                o = 1 - par
                later = attn and not (isinstance(b, int) and b == 0)
                for t in range(NT):
                    rows_t = iter(range(FIRST[t], FIRST[t] + PER_T[t]) if rows and t < len(PER_T) else ())

                    def row_chunk():
                        u = next(rows_t, None)
                        if u is None:
                            return
                        c, m = u // NCH, u % NCH
                        if u == 0:
                            pe.wait_ge(sem("k_hi_done"), NCH * (b + 2))
                            pe.wait_ge(sem("qd_hi_done"), b + 2)
                            wait(pe, sem("negrow_done"), b + 1)
                        wait(pe, sem("row_done"), SROWS * (b + 1) + u - 1)
                        mm(bank[SBANK + u % 2][:, 0:CH], qd_hi[:, o, 128 * c:128 * c + 128],
                           k_hi[:, o, CH * m:CH * m + CH], start=True, stop=True).then_inc(sem("row_mm"), 1)

                    if attn:
                        if t == 0:
                            if isinstance(b, int) and b == 0:
                                pe.wait_ge(sem("k_ones"), 16)
                                pe.wait_ge(sem("q_first"), 16 * 12)
                                pe.wait_ge(sem("v_done"), NCH)
                                pe.wait_ge(sem("k_lo_done"), 2 * NCH)
                            pe.wait_ge(sem(f"k_stacked{par}"), 16 * 12 * (r + 1))
                            pe.wait_ge(sem(f"q_stacked{par}"), q_count(r, par))
                        wait(pe, sem("exp_done"), NT * b + t - 1)
                        for g in range(QG):
                            last = mm(bank[2 * (t % 2) + g // 2][0:KT, GC * (g % 2):GC * (g % 2) + GC],
                                      k_st[0:97, par, g, KT * t:KT * t + KT], q_st[0:97, par, GC * g:GC * g + GC],
                                      start=True, stop=True)
                        last.then_inc(sem("st_done"), 1)
                    row_chunk()
                    if attn and t >= 1:
                        values(b, par, t - 1)
                    elif later:
                        values(b - 1, o, NT - 1)
                    now = pieces(b)[t] if t < len(pieces(b)) else None
                    if now and now[0] == "K":
                        piece(b, r, par, *now, rows, keys)
                    row_chunk()
                    if now and now[0] != "K":
                        piece(b, r, par, *now, rows, keys)
                    row_chunk()
                    if rows and t == 9:
                        pe.wait_ge(sem("max_done"), b + 2)
                        tp(bank[SBANK][0:RT, 0:128], negmax[:, :], ident).then_inc(sem("max_T"), 1)
                    if later and t == 10:
                        if rows:
                            pe.wait_ge(sem("v_done"), NCH * (b + 2))
                        else:
                            pe.wait_ge(sem("recip_done"), b - 1)
                        denominators(b - 1, o)
                    if isinstance(b, int) and b == NB - 1:
                        beside_last_batch(t)

            steps(pe, body, queries)

            def ctx_transposes(first, end):
                for n in range(first, end):
                    p, bb, j = n // 6, n % 6 // NCH, n % NCH
                    if n % 6 == 0:
                        if p == 0:
                            pe.wait_ge(sem("ctx_loaded0"), 16 * (NB // 2 + 1))
                            pe.wait_ge(sem("ctx_loaded1"), 16 * (NB // 2 + 1))
                        else:
                            pe.wait_ge(sem(f"pair_loaded{p}"), 32)
                    if n == 12:
                        pe.wait_ge(sem("gelu_done"), FC * E)
                    if n >= 4:
                        pe.wait_ge(sem("ctx1_T"), n - 1 if n >= 20 else n - 3)
                    for i in range(TPC):
                        t = TPC * j + i
                        last = tp(bank[piece1_bank(n)][:, KT * i:KT * i + KT], ctx_pair[p][0:KT, bb, D * t:D * t + D],
                                  ident[0:KT, 0:KT])
                    last.then_inc(sem("t1_done"), 1)

            values(NB - 1, 1, NT - 1)
            pe.wait_ge(sem("recip_done"), NB - 1)
            ctx_transposes(0, 2)
            denominators(NB - 1, 1)
            ctx_transposes(2, 6)
            ctx_transposes(6, 8)
            pe.wait_ge(sem("norm_done"), NB)
            for s in range(6):
                output_slot(s, EB, NB)
            attention_to_tokens(range(EARLY_TILES, NTT), bank[MBANK], 2)
            ctx_transposes(8, 12)

            transpose_x("ln1")
            pe.wait_ge(sem("ln1_xT"), 1)
            for k in range(NTT):
                last = mm(bank[6][0:TT, E * k:E * k + E], x_T[:, TT * k:TT * k + TT], la("wr"), start=True, stop=True)
            last.then_inc(sem("logits"), 1)

            def up(n):
                e, c = n // FC, n % FC
                if n >= 4:
                    pe.wait_ge(sem("gelu_done"), n - 3)
                if c == 0:
                    pe.wait_ge(sem("w1_parts"), e + 1)
                bk = bank[n % 4][:, 0:NTOK]
                hi, lo = (w[:, e % 3, 128 * c:128 * c + 128] for w in (w1_hi, w1_lo))
                mm(bk, hi, x_hi[:, :], start=True, stop=False)
                mm(bk, hi, x_lo[:, :], start=False, stop=False)
                mm(bk, lo, x_hi[:, :], start=False, stop=True).then_inc(sem("up_mm"), 1)

            def down(n):
                e, c = n // FC, n % FC
                pe.wait_ge(sem("h_parts"), n + 1)
                if c == 0:
                    pe.wait_ge(sem("w2_parts"), e + 1)
                    if e == 1:
                        pe.wait_ge(sem("acc_b2"), 1)
                    if e >= 2:
                        pe.wait_ge(sem("mul_done"), e - 1)
                if c == 2:
                    if e >= 2:
                        pe.wait_ge(sem("chosen_sb"), e - 1)
                    mm(bank[6 + e % 2][:, 0:NTOK], pick[:, e:e + 1].to_broadcast([E, 128]), chosen_T[:, :],
                       start=True, stop=True).then_inc(sem("chosen_mm"), 1)
                bk = bank[4 + e % 2][:, 0:NTOK]
                hi, lo = (w[:, e % 3, D * c:D * c + D] for w in (w2_hi, w2_lo))
                mm(bk, hi, h_hi[:, n % (LAG + 1), :], start=(c == 0), stop=False)
                mm(bk, hi, h_lo[:, n % (LAG + 1), :], start=False, stop=False)
                mm(bk, lo, h_hi[:, n % (LAG + 1), :], start=False, stop=(c == FC - 1)).then_inc(sem("down_mm"), 1)

            pe.wait_ge(sem("att0_added"), 2)
            pe.wait_ge(sem("ctx1_T"), 12)
            pe.wait_ge(sem("ln1_parts"), 1)
            for n in range(FC):
                up(n)
            pe.wait_ge(sem("chosen"), 1)
            for k in range(NTT):
                last = tp(bank[7][0:E, TT * k:TT * k + TT], rt[:, 2, k, :], ident[0:TT, 0:TT])
            last.then_inc(sem("chosen_tp"), 1)
            for n in range(FC, FC * E + LAG):
                if n < FC * E:
                    up(n)
                if n == FC + 1:
                    pe.wait_ge(sem("chosen_T"), 1)
                    mm(bank[5][:, 0:NTOK], la("b2")[0:E, :], chosen_T[:, :].bitcast(fp32), start=True, stop=True)\
                        .then_inc(sem("b2_mm"), 1)
                if n >= LAG:
                    down(n - LAG)
            back_to_tokens("moe", y_T)

            ctx_transposes(12, 18)
            transpose_x("ln2")
            pe.wait_ge(sem("ln2_xT"), 1)
            pe.wait_ge(sem("folded"), 1)
            mm(bank[6][:, 0:NTOK], wqk1[:, :], x_T[:, :], start=True, stop=True).then_inc(sem("qt_mm"), 1)

            def pair_scores(p):
                if p >= 1:
                    pe.wait_ge(sem("exp1_done"), p)
                else:
                    pe.wait_ge(sem("qt_pad"), 1)
                    pe.wait_ge(sem("ctx1_T"), 18)
                if p == 3:
                    pe.wait_ge(sem("ctx1_T"), 24)
                for j in range(NCH):
                    for bb in range(2):
                        last = mm(bank[j][64 * bb:64 * bb + 64, 0:CH], qt_pad[:, 2 * p + bb, :],
                                  ctxT_pair[p][:, bb, CH * j:CH * j + CH], start=True, stop=True)
                last.then_inc(sem("s1_mm"), 1)

            def turn(item):
                i = TURNS.index(item)
                if i >= 2:
                    kind, p, j = TURNS[i - 2]
                    if kind == "P":
                        pe.wait_ge(sem("p_T"), NCH * p + j + 1)
                    else:
                        pe.wait_ge(sem("c_T"), p + 1)
                return bank[turn_bank(item)]

            def transpose_c(p):
                m = turn(("C", p, 0))
                pe.wait_ge(sem("c_nat"), p + 1)
                tp(m[:, 0:128], c_nat, ident).then_inc(sem("c_tp"), 1)

            def output_projection(hf):
                if hf == 0:
                    pe.wait_ge(sem("ctx1_T"), 24)
                pe.wait_ge(sem("c_T"), HB // 2 * (hf + 1))
                mm(bank[HALF_BANKS[hf][0]][:, 0:HN], wvo1[:, :], c_T[:, HB * hf:HB * hf + HB, :], start=True, stop=True)\
                    .then_inc(sem("att1_mm"), 1)

            def half_to_tokens(hf):
                pe.wait_ge(sem("att1_y"), hf + 1)
                for i in range(HT):
                    k = HT * hf + i
                    last = tp(bank[HALF_BANKS[hf][1]][0:TT, D * i:D * i + D], y_T[:, TT * k:TT * k + TT], ident)
                last.then_inc(sem("att1_yT"), 1)

            def xq_transposes(hf):
                pe.wait_ge(sem("xq_done"), hf + 1)
                pe.wait_ge(sem("ident_bf"), 1)
                for i in range(HT):
                    last = tp(bank_bf[HALF_BANKS[hf][0]][:, TT * i:TT * i + TT], xq_view[:, HT * hf + i, :], ident_bf[0:TT, 0:TT])
                last.then_inc(sem("xq_tp"), 1)

            def spread_scales(hf):
                pe.wait_ge(sem("xs_diag"), hf + 1)
                pe.wait_ge(sem("ones"), 1)
                for i in range(HT):
                    last = mm(bank[HALF_BANKS[hf][1]][:, TT * i:TT * i + TT], ones[0:TT, :], xn[:, HT * hf + i, 0:TT],
                              start=True, stop=True)
                last.then_inc(sem("xs_mm"), 1)

            def hidden_products(hf):
                pe.wait_ge(sem("xq_T"), hf + 1)
                pe.wait_ge(sem("xs_row"), hf + 1)
                pe.wait_ge(sem("fw1_q"), 1)
                for c in range(FC):
                    last = mm(bank[HALF_BANKS[hf][c // 2]][:, HN * (c % 2):HN * (c % 2) + HN], fw1_q[:, 128 * c:128 * c + 128],
                              xqT_view[:, HN * hf:HN * hf + HN], start=True, stop=True)
                    if c % 2:
                        last.then_inc(sem("h1_mm"), 1)

            def hidden_to_tokens(hf):
                pe.wait_ge(sem("silu_done"), FC * (hf + 1))
                pe.wait_ge(sem("h1_read"), FC * (hf + 1))
                for i in range(HT):
                    k = HT * hf + i
                    for c in range(FC):
                        last = tp(bank[HALF_BANKS[hf][i]][0:TT, 128 * c:128 * c + 128],
                                  hid[1][:, NTOK * c + TT * k:NTOK * c + TT * k + TT], ident)
                    last.then_inc(sem("h_tok"), 1)

            def hq_transposes(hf):
                for i in range(HT):
                    k = HT * hf + i
                    pe.wait_ge(sem("hq_done"), k + 1)
                    for c in range(FC):
                        last = tp(bank_bf[HALF_BANKS[hf][i]][:, TT * c:TT * c + TT], hq_view[:, F * k + 128 * c:F * k + 128 * c + 128],
                                  ident_bf[0:TT, 0:TT])
                    last.then_inc(sem("hq_tp"), 1)

            def output_products(hf):
                pe.wait_ge(sem("fw2_q"), 1)
                for i in range(HT):
                    k = HT * hf + i
                    pe.wait_ge(sem("hq_T"), k + 1)
                    for c in range(FC):
                        last = mm(bank[HALF_BANKS[hf][i]][0:TT, 0:D], hqT_view[:, FC * TT * k + TT * c:FC * TT * k + TT * c + TT],
                                  fw2_q[:, D * c:D * c + D], start=(c == 0), stop=(c == FC - 1))
                    last.then_inc(sem("y2_mm"), 1)

            pair_scores(0)
            ctx_transposes(18, 24)
            for p in range(NB // 2):
                if p + 1 < NB // 2:
                    pair_scores(p + 1)
                pe.wait_ge(sem("exp1_done"), p + 1)
                for j in range(NCH):
                    m = turn(("P", p, j))
                    for i in range(TPC):
                        t = TPC * j + i
                        last = tp(m[0:KT, 128 * i:128 * i + 128], p_row[:, KT * t:KT * t + KT], ident)
                    last.then_inc(sem("pt_done"), 1)
                if p >= 1:
                    transpose_c(p - 1)
                for t in range(NT):
                    if t % TPC == 0:
                        pe.wait_ge(sem("p_T"), NCH * p + t // TPC + 1)
                    for bb in range(2):
                        last = mm(bank[5][64 * bb:64 * bb + 64, 0:D], p_T[0:KT, 128 * t + 64 * bb:128 * t + 64 * bb + 64],
                                  ctx_pair[p][0:KT, bb, D * t:D * t + D], start=(t == 0), stop=(t == NT - 1))
                    if (p, t) == (2, 5):
                        output_projection(0)
                last.then_inc(sem("pv1_done"), 1)
                if p == 2:
                    half_to_tokens(0)
            xq_transposes(0)
            transpose_c(NB // 2 - 1)
            spread_scales(0)
            output_projection(1)
            hidden_products(0)
            half_to_tokens(1)
            hidden_to_tokens(0)
            xq_transposes(1)
            spread_scales(1)
            hidden_products(1)
            hidden_to_tokens(1)
            hq_transposes(0)
            output_products(0)
            hq_transposes(1)
            output_products(1)

        @block.scalar
        def _(act):
            A = nc.scalar.activation
            act.wait_ge(sem("early_loaded"), 16)
            A(tgate[:, :], ea("gates"), ACT.Tanh).then_inc(sem("tgate"), 1)

            def queries():
                act.wait_ge(sem("ln0_xnT"), 1)
                A(x_T[:, :], bank[MBANK][:, 0:NTOK], ACT.Copy).then_inc(sem("ln0_xT"), 1)

            def piece(b, r, par, kind, j, rows, keys):
                n = b + 2
                o = 1 - par
                m = bank[piece_bank(b, kind, j)]
                if kind == "T" and keys:
                    act.wait_ge(sem("t_done"), NCH * n + j + 1)
                    A(ctx_T[:, par, CH * j:CH * j + CH], m[:, 0:CH], ACT.Copy).then_inc(sem("ctx_T_done"), 1)
                if kind == "K" and keys:
                    act.wait_ge(sem("k_mm"), NCH * n + j + 1)
                    if j == 0:
                        if not isinstance(b, int) or b >= 0:
                            act.wait_ge(sem(f"k_stacked{par}"), 16 * 12 * (r + 1))
                            act.wait_ge(sem("row_mm"), SROWS * (b + 1))
                    A(k_hi[:, par, CH * j:CH * j + CH], m[:, 0:CH], ACT.Identity, bias=ea("bk")).then_inc(sem("k_hi_done"), 1)
                if kind == "V" and rows:
                    act.wait_ge(sem("v_mm"), NCH * (b + 1) + j + 1)
                    if j == 0:
                        wait(act, sem("pv_done"), NT * b)
                        if isinstance(b, int) and b == -1:
                            act.wait_ge(sem("v_const"), 1)
                    mv = m[0:KT, :].rearrange("p (t c) -> p t c", t=TPC)
                    dst = v_aug[0:KT, o, TPC * j:TPC * j + TPC, :, :]
                    A(dst[:, :, 0:5, 0:24], mv[:, :, 0:120].rearrange("p t (g c) -> p t g c", g=5), ACT.Copy)
                    A(dst[:, :, 5, 0:8], mv[:, :, 120:128], ACT.Copy).then_inc(sem("v_done"), 1)

            def body(r, par, attn, rows, keys):
                b = 2 * r + par
                for t in range(NT):
                    if attn:
                        act.wait_ge(sem("st_done"), NT * b + t + 1)
                        wait(act, sem("pv_done"), NT * b + t - 2 + t % 2)
                        A(probs[0:KT, t % 3, :].rearrange("p (a c) -> p a c", a=2),
                          ps_all[0:KT, 2 * (t % 2):2 * (t % 2) + 2, 0:2 * GC], ACT.Exp).then_inc(sem("exp_done"), 1)
                    if t < len(pieces(b)):
                        piece(b, r, par, *pieces(b)[t], rows, keys)
                    if rows and t == 9:
                        act.wait_ge(sem("max_T"), b + 2)
                        if not isinstance(b, int) or b >= 0:
                            act.wait_ge(sem(f"q_stacked{par}"), q_count(r, par))
                        A(negrow[:, :], bank[SBANK][0:RT, 0:128], ACT.Copy).then_inc(sem("negrow_done"), 1)

            steps(act, body, queries)

            def evac_ctx(first, end):
                for n in range(first, end):
                    act.wait_ge(sem("t1_done"), n + 1)
                    A(ctxT_pair[n // 6][:, n % 6 // NCH, CH * (n % NCH):CH * (n % NCH) + CH],
                      bank[piece1_bank(n)][:, 0:CH], ACT.Copy).then_inc(sem("ctx1_T"), 1)

            evac_ctx(0, 6)
            evac_ctx(6, 12)
            act.wait_ge(sem("ln1_xnT"), 1)
            A(x_T[:, :], bank[MBANK][:, 0:NTOK], ACT.Copy).then_inc(sem("ln1_xT"), 1)
            A(x_hi[:, :], bank[MBANK][:, 0:NTOK], ACT.Copy).then_inc(sem("ln1_hi"), 1)
            def copy_mask(e):
                act.wait_ge(sem("chosen_mm"), e + 1)
                if e >= 2:
                    act.wait_ge(sem("mul_done"), e - 1)
                A(chosen_sb[:, e % 2, :], bank[6 + e % 2][:, 0:NTOK], ACT.Copy).then_inc(sem("chosen_sb"), 1)

            for n in range(E * FC):
                act.wait_ge(sem("up_mm"), n + 1)
                b1 = la("b1")[:, n:n + 1]
                if act_rounds(n):
                    if n > LAG:
                        act.wait_ge(sem("down_mm"), n - LAG)
                    A(h_hi[:, n % (LAG + 1), :], bank[n % 4][:, 0:NTOK], ACT.Gelu, bias=b1).then_inc(sem("h_hi"), 1)
                if n >= 4:
                    act.wait_ge(sem("h_parts"), n - 3)
                A(h_f[:, n % 4, :], bank[n % 4][:, 0:NTOK], ACT.Gelu, bias=b1).then_inc(sem("gelu_done"), 1)
                if n >= LAG + 2 and (n - LAG) % FC == 3:
                    copy_mask((n - LAG) // FC)
                if n == FC - 1:
                    act.wait_ge(sem("chosen_tp"), 1)
                    A(chosen_T[:, :], bank[7][0:E, 0:NTOK], ACT.Copy).then_inc(sem("chosen_T"), 1)
            copy_mask(E - 1)
            act.wait_ge(sem("rel_logits"), 1)
            A(rt[:, 1, :, :], rt[:, 0, :, :], ACT.Exp).then_inc(sem("exp_logits"), 1)

            evac_ctx(12, 18)
            act.wait_ge(sem("ln2_xnT"), 1)
            A(x_T[:, :], bank[MBANK][:, 0:NTOK], ACT.Copy).then_inc(sem("ln2_xT"), 1)
            act.wait_ge(sem("qt_mm"), 1)
            act.wait_ge(sem("qt_zero"), 1)
            A(qt_pad[:, :, 0:SQ], bank[6][:, 0:NTOK].rearrange("p (b q) -> p b q", b=NB), ACT.Identity,
              scale=float(D) ** -0.5, bias=c0[:, 1:2]).then_inc(sem("qt_pad"), 1)

            def pair_exp(p):
                act.wait_ge(sem("max1_done"), p + 1)
                if p >= 1:
                    act.wait_ge(sem("pt_done"), NCH * p)
                A(p_row.rearrange("p (a c) -> p a c", a=NCH), ps_all[:, 0:NCH, 0:CH], ACT.Exp, bias=den1[:, p % 2, 0:1],
                  accum_out=den1[:, p % 2, 1:2]).then_inc(sem("exp1_done"), 1)

            def evac_c(p):
                act.wait_ge(sem("c_tp"), p + 1)
                A(c_T[:, 2 * p:2 * p + 2, :], bank[turn_bank(("C", p, 0))][:, 0:128].rearrange("p (b q) -> p b q", b=2)[:, :, 0:SQ], ACT.Copy)\
                    .then_inc(sem("c_T"), 1)

            def half_y(hf):
                act.wait_ge(sem("att1_mm"), hf + 1)
                A(y_T[:, HN * hf:HN * hf + HN], bank[HALF_BANKS[hf][0]][:, 0:HN], ACT.Identity, bias=c0[:, 2:3]).then_inc(sem("att1_y"), 1)

            def evac_xq(hf):
                act.wait_ge(sem("xq_tp"), hf + 1)
                A(xqT_view[:, HN * hf:HN * hf + HN], bank_bf[HALF_BANKS[hf][0]][:, 0:HN], ACT.Copy).then_inc(sem("xq_T"), 1)

            def evac_scales(hf):
                act.wait_ge(sem("xs_mm"), hf + 1)
                A(x_T[:, HN * hf:HN * hf + HN], bank[HALF_BANKS[hf][1]][:, 0:HN], ACT.Copy).then_inc(sem("xs_row"), 1)

            def taps_and_silu(hf):
                def silu(c):
                    act.wait_ge(sem("conv_done"), FC * hf + c + 1)
                    at = NTOK * c + HN * hf
                    A(hid[1][:, at:at + HN], hid[0][:, at:at + HN], ACT.Silu).then_inc(sem("silu_done"), 1)

                for c in range(FC):
                    act.wait_ge(sem("h1_read"), FC * hf + c + 1)
                    A(hid[0][:, NTOK * c + HN * hf:NTOK * c + HN * hf + HN].rearrange("p (b s) -> p b s", b=HB),
                      hconv[:, c, HB * hf:HB * hf + HB, 0:SQ], ACT.Identity,
                      scale=la("convw")[:, 3 * c:3 * c + 1], bias=la("convb")[:, c:c + 1]).then_inc(sem("tap0"), 1)
                    if c >= 1:
                        silu(c - 1)
                silu(FC - 1)

            def round_hidden(hf):
                act.wait_ge(sem("h_scale"), hf + 1)
                act.wait_ge(sem("magic"), 1)
                for i in range(HT):
                    k = HT * hf + i
                    A(hq_f32[:, k, :], bank[HALF_BANKS[hf][i]][0:TT, :], ACT.Identity,
                      scale=small[:, 6, k:k + 1], bias=magic[0:TT, :]).then_inc(sem("h_round"), 1)

            def evac_hq(hf):
                for i in range(HT):
                    k = HT * hf + i
                    act.wait_ge(sem("hq_tp"), k + 1)
                    A(hqT_view[:, FC * TT * k:FC * TT * (k + 1)], bank_bf[HALF_BANKS[hf][i]][:, 0:FC * TT], ACT.Copy).then_inc(sem("hq_T"), 1)

            act.wait_ge(sem("s1_mm"), 1)
            evac_ctx(18, 21)
            pair_exp(0)
            evac_ctx(21, 24)
            for p in range(NB // 2):
                for j in range(NCH):
                    n = NCH * p + j
                    act.wait_ge(sem("pt_done"), n + 1)
                    if p >= 1 and j == 0:
                        act.wait_ge(sem("pv1_done"), p)
                    A(p_T[0:KT, 512 * j:512 * j + 512], bank[turn_bank(("P", p, j))][0:KT, :], ACT.Copy).then_inc(sem("p_T"), 1)
                if p >= 1:
                    evac_c(p - 1)
                if p + 1 < NB // 2:
                    pair_exp(p + 1)
                if p == 2:
                    half_y(0)
            evac_xq(0)
            evac_c(NB // 2 - 1)
            evac_scales(0)
            half_y(1)
            taps_and_silu(0)
            evac_xq(1)
            evac_scales(1)
            round_hidden(0)
            taps_and_silu(1)
            evac_hq(0)
            round_hidden(1)
            evac_hq(1)

        @block.vector
        def _(dve):
            V = nc.vector
            chain = [0]

            def link(ins):
                chain[0] += 1
                ins.then_inc(sem("dve_chain"), 1)
                dve.wait_ge(sem("dve_chain"), chain[0])

            def row_stats(ks):
                for k in ks:
                    last = V.bn_stats(stats[:, k, :], x_tok[:, k, :])
                link(last)

            def variances(name, ks, fresh=None):
                row_stats(ks if fresh is None else range(fresh, NTT))
                for k in ks:
                    last = V.bn_aggr(meanvar[:, k, :], stats[:, k, :])
                last.then_inc(sem(f"{name}_var"), 1)

            def normalise_rows(name, ks, part=1):
                dve.wait_ge(sem(f"{name}_rstd"), part)
                for k in ks:
                    last = V.tensor_scalar(xn[:, k, :], x_tok[:, k, :], meanvar[:, k, 0:1], rstd[:, k:k + 1],
                                           ALU.subtract, ALU.mult)
                if name == "ln3":
                    link(last)
                elif ks[-1] == NTT - 1:
                    last.then_inc(sem(f"{name}_xn"), 1)

            def layernorm(name, ks=range(NTT), part=1, fresh=None):
                variances(name, ks, fresh)
                normalise_rows(name, ks, part)

            dve.wait_ge(sem("x_loaded"), 16)
            layernorm("ln0")
            for par in range(2):
                V.memset(v_aug[:, par, :, VG - 1, DH:DEN], 0.0)
                last = V.memset(v_aug[:, par, :, :, DEN:32], 0.0)
            link(last)
            for par in range(2):
                last = V.memset(v_aug[:, par, :, :, DEN], 1.0)
            last.then_inc(sem("v_const"), 1)
            dve.wait_ge(sem("early_loaded"), 16)

            def queries():
                dve.wait_ge(sem("q_mm"), 1)
                link(V.tensor_scalar(q_f[:, :], bank[OBANK][:, 0:NTOK], ea("bq"), float(DH) ** -0.5, ALU.add, ALU.mult))
                link(V.tensor_copy(q_hi[:, :], q_f[:, :]))
                V.tensor_tensor(q_lo[:, :], q_f[:, :], q_hi[:, :].bitcast(fp32), ALU.subtract).then_inc(sem("q_parts"), 1)

            def out_to_sbuf(b, par):
                dve.wait_ge(sem("pv_done"), NT * (b + 1))
                m = bank[OBANK]
                V.tensor_copy(o_cur[:, par, :], m[:, 0:OC]).then_inc(sem("o_done"), 1)

            def normalise(b, par):
                dve.wait_ge(sem("den_mm"), b + 1)
                m = bank[MBANK]
                V.reciprocal(recip[:, :], m[:, 0:OC]).then_inc(sem("recip_done"), 1)
                dve.wait_ge(sem("recip_done"), b + 1)
                V.tensor_tensor(o_all[:, b, :], o_cur[:, par, :], recip[:, :], ALU.mult).then_inc(sem("norm_done"), 1)

            def attention_y(b0, b1, part):
                dve.wait_ge(sem("att0_mm"), part)
                V.tensor_scalar(y_T[:, SQ * b0:SQ * b1], bank[5][:, SQ * b0:SQ * b1], c0[:, 0:1], None, ALU.add)\
                    .then_inc(sem("att0_y"), 1)

            def add_attention0(ks, m, part):
                dve.wait_ge(sem("tgate"), 1)
                dve.wait_ge(sem("att0_yT"), part)
                for k in ks:
                    last = V.scalar_tensor_tensor(x_tok[:, k, :], m[0:TT, D * k:D * k + D], tgate[0:TT, 0:1],
                                                  x_tok[:, k, :], ALU.mult, ALU.add)
                last.then_inc(sem("att0_added"), 1)
                dve.wait_ge(sem("att0_added"), part)

            def beside_last_batch(t):
                if t == 2:
                    dve.wait_ge(sem("folded_mm"), 1)
                    V.tensor_tensor(c0[:, 0:1], bank[4][:, 0:1], ea("bo"), ALU.add)
                    V.tensor_scalar(c0[:, 1:2], bank[4][:, 1:2], float(D) ** -0.5, None, ALU.mult)
                    V.tensor_tensor(c0[:, 2:3], bank[4][:, 2:3], la("bo1"), ALU.add)
                    V.tensor_copy(wqk1[:, :], bank[4][:, 128:256])
                    V.tensor_copy(wvo1[:, :], bank[4][:, 256:384]).then_inc(sem("folded"), 1)
                    dve.wait_ge(sem("folded"), 1)
                if t == 8:
                    attention_y(0, EB, 1)
                if t == 10:
                    add_attention0(range(EARLY_TILES), bank[4], 1)

            def body(r, par, attn, rows, keys):
                b = 2 * r + par
                later = attn and not (isinstance(b, int) and b == 0)
                for t in range(NT):
                    if rows and t < len(PER_T):
                        for u in range(FIRST[t], FIRST[t] + PER_T[t]):
                            dve.wait_ge(sem("row_mm"), SROWS * (b + 1) + u + 1)
                            V.tensor_reduce(rowmax[:, u:u + 1], bank[SBANK + u % 2][:, 0:CH], AX.X, ALU.max)\
                                .then_inc(sem("row_done"), 1)
                            if later and u == 0:
                                out_to_sbuf(b - 1, 1 - par)
                    if later and not rows and t == 1:
                        out_to_sbuf(b - 1, 1 - par)
                    if isinstance(b, int) and b == NB - 1:
                        beside_last_batch(t)
                    if t < len(pieces(b)):
                        kind, j = pieces(b)[t]
                        if kind == "K" and keys:
                            dve.wait_ge(sem("k_hi_done"), NCH * (b + 2) + j + 1)
                            V.scalar_tensor_tensor(k_lo[:, par, CH * j:CH * j + CH], bank[piece_bank(b, kind, j)][:, 0:CH], ea("bk"),
                                                   k_hi[:, par, CH * j:CH * j + CH].bitcast(fp32), ALU.add, ALU.subtract)\
                                .then_inc(sem("k_lo_done"), 1)
                    if rows and t == len(PER_T) - 1:
                        dve.wait_ge(sem("row_done"), SROWS * (b + 2))
                        V.tensor_reduce(negmax[:, :], rowmax[:, :].rearrange("p (c m) -> p c m", m=NCH), AX.X, ALU.max,
                                        negate=True).then_inc(sem("max_done"), 1)
                if later:
                    normalise(b - 1, 1 - par)

            steps(dve, body, queries)
            out_to_sbuf(NB - 1, 1)

            def round_weights(e, src, hi, name, used):
                if e >= 3:
                    dve.wait_ge(sem(used), FC * (e - 2))
                V.tensor_copy(hi[:, e % 3, :], src[:, F * e:F * e + F]).then_inc(sem(name + "_hi"), 1)

            dve.wait_ge(sem("w1_loaded"), 16)
            dve.wait_ge(sem("q_stacked1"), 16 * 13 * NB // 2)
            for e in range(3):
                round_weights(e, w1_sb[:, :], w1_hi, "w1_parts", "up_mm")
            row_stats(range(EARLY_TILES))
            normalise(NB - 1, 1)

            attention_y(EB, NB, 2)
            dve.wait_ge(sem("w2_loaded"), 16)
            for e in range(3):
                round_weights(e, w2_sb, w2_hi, "w2_parts", "down_mm")
            add_attention0(range(EARLY_TILES, NTT), bank[MBANK], 2)
            layernorm("ln1", fresh=EARLY_TILES)
            dve.wait_ge(sem("ln1_xT"), 1)
            dve.wait_ge(sem("ln1_hi"), 1)
            V.tensor_tensor(x_lo[:, :], x_T[:, :], x_hi[:, :].bitcast(fp32), ALU.subtract).then_inc(sem("ln1_parts"), 1)
            dve.wait_ge(sem("logits"), 1)
            lg = bank[6][0:TT, 0:NTT * E].rearrange("p (k e) -> p k e", e=E)
            bc = lambda a: a.unsqueeze(2).to_broadcast([TT, NTT, E])
            link(V.tensor_reduce(small[:, 0, :], lg, AX.X, ALU.max))
            V.tensor_tensor(rt[:, 0, :, :], lg, bc(small[:, 0, :]), ALU.subtract).then_inc(sem("rel_logits"), 1)
            dve.wait_ge(sem("rel_logits"), 1)
            link(V.tensor_scalar(rt[:, 2, :, :], rt[:, 0, :, :], 0.0, None, ALU.is_ge))
            link(V.tensor_tensor(rt[:, 2, :, :], rt[:, 2, :, :],
                                 ea("first")[0:TT, :].unsqueeze(1).to_broadcast([TT, NTT, E]), ALU.mult))
            link(V.tensor_reduce(small[:, 1, :], rt[:, 2, :, :], AX.X, ALU.max))
            V.tensor_tensor(rt[:, 2, :, :], rt[:, 2, :, :], bc(small[:, 1, :]), ALU.is_equal).then_inc(sem("chosen"), 1)

            def split_hidden(n):
                if not act_rounds(n):
                    if n > LAG:
                        dve.wait_ge(sem("down_mm"), n - LAG)
                    dve.wait_ge(sem("gelu_done"), n + 1)
                    link(V.tensor_copy(h_hi[:, n % (LAG + 1), :], h_f[:, n % 4, :]))
                else:
                    dve.wait_ge(sem("h_hi"), sum(act_rounds(m) for m in range(n + 1)))
                    dve.wait_ge(sem("gelu_done"), n + 1)
                V.tensor_tensor(h_lo[:, n % (LAG + 1), :], h_f[:, n % 4, :], h_hi[:, n % (LAG + 1), :].bitcast(fp32), ALU.subtract)\
                    .then_inc(sem("h_parts"), 1)

            def split_hiddens(first, end):
                for n in range(first, end):
                    split_hidden(n)

            def hidden_and_weights(e):
                first = FC * e + LAG + 1
                if e + 3 < E:
                    split_hidden(first)
                    round_weights(e + 3, w1_sb[:, :], w1_hi, "w1_parts", "up_mm")
                    first += 1
                split_hiddens(first, min(FC * (e + 1) + LAG + 1, FC * E))

            def mix(e):
                dve.wait_ge(sem("down_mm"), FC * (e + 1))
                dve.wait_ge(sem("chosen_sb"), e + 1)
                V.tensor_tensor(chosen_y, bank[4 + e % 2][:, 0:NTOK], chosen_sb[:, e % 2, :], ALU.mult)\
                    .then_inc(sem("mul_done"), 1)
                dve.wait_ge(sem("mul_done"), e + 1)
                last = V.tensor_tensor(y_T[:, :], y_T[:, :], chosen_y, ALU.add)
                if e == E - 1:
                    last.then_inc(sem("moe_y"), 1)
                else:
                    link(last)

            split_hiddens(0, 5)
            dve.wait_ge(sem("b2_mm"), 1)
            V.tensor_copy(y_T[:, :], bank[5][:, 0:NTOK]).then_inc(sem("acc_b2"), 1)
            dve.wait_ge(sem("acc_b2"), 1)

            def ternary(i, name, q):
                link(V.tensor_scalar(la(name), la(name), wsc[:, 6 + i:7 + i], MAGIC, ALU.mult, ALU.add))
                link(V.tensor_scalar(la(name), la(name), MAGIC, 1.0, ALU.subtract, ALU.min))
                V.tensor_scalar(q[:, :], la(name), -1.0, None, ALU.max).then_inc(sem(f"{name}_q"), 1)

            hidden_and_weights(0)
            mix(0)
            for i, name in enumerate(("fw1", "fw2")):
                V.tensor_reduce(wsc[:, i:i + 1], la(name), AX.X, ALU.add, apply_absolute_value=True)\
                    .then_inc(sem("w_abs"), 1)
            V.tensor_copy(ident_bf[:, :], ident).then_inc(sem("ident_bf"), 1)
            hidden_and_weights(1)
            mix(1)
            dve.wait_ge(sem("w_mean"), 1)
            link(V.tensor_scalar(wsc[:, 4:6], wsc[:, 2:4], 1.0 / (D * F), 1e-5, ALU.mult, ALU.max))
            link(V.reciprocal(wsc[:, 6:8], wsc[:, 4:6]))
            hidden_and_weights(2)
            for e in range(2, E):
                if e > 2:
                    hidden_and_weights(e)
                mix(e)
                if e == 5:
                    ternary(0, "fw1", fw1_q)
                if e == 6:
                    ternary(1, "fw2", fw2_q)
            dve.wait_ge(sem("exp_logits"), 1)
            link(V.tensor_reduce(small[:, 2, :], rt[:, 1, :, :], AX.X, ALU.add))
            link(V.reciprocal(small[:, 3, :], small[:, 2, :]))
            link(V.tensor_scalar(small[:, 4, :], small[:, 3, :], tgate[0:TT, 2:3], None, ALU.mult))
            dve.wait_ge(sem("moe_yT"), 1)
            for k in range(NTT):
                last = V.scalar_tensor_tensor(x_tok[:, k, :], bank[MBANK][0:TT, D * k:D * k + D], small[:, 4, k:k + 1],
                                              x_tok[:, k, :], ALU.mult, ALU.add)
            link(last)
            layernorm("ln2")

            def tiles(hf):
                return range(HT * hf, HT * hf + HT)

            def half_rows(row, hf):
                return small[:, row, HT * hf:HT * hf + HT]

            def add_attention(hf):
                dve.wait_ge(sem("att1_yT"), hf + 1)
                for i, k in enumerate(tiles(hf)):
                    last = V.scalar_tensor_tensor(x_tok[:, k, :], bank[HALF_BANKS[hf][1]][0:TT, D * i:D * i + D], tgate[0:TT, 1:2],
                                                  x_tok[:, k, :], ALU.mult, ALU.add)
                link(last)

            def quantise_x(hf):
                k0, k1 = HT * hf, HT * hf + HT
                link(V.tensor_reduce(half_rows(5, hf), xn[:, k0:k1, :], AX.X, ALU.max, apply_absolute_value=True))
                link(V.tensor_scalar(half_rows(5, hf), half_rows(5, hf), 1e-5, None, ALU.max))
                link(V.reciprocal(half_rows(6, hf), half_rows(5, hf)))
                link(V.tensor_scalar(half_rows(6, hf), half_rows(6, hf), 127.0, None, ALU.mult))
                for k in tiles(hf):
                    last = V.tensor_scalar(xn[:, k, :], xn[:, k, :], small[:, 6, k:k + 1], MAGIC, ALU.mult, ALU.add)
                link(last)
                xf = xn[:, k0:k1, :].rearrange("p k d -> p (k d)")
                link(V.tensor_scalar(xf, xf, MAGIC, 127.0, ALU.subtract, ALU.min))
                V.tensor_scalar(xq_view[:, k0:k1, :].rearrange("p k d -> p (k d)"), xf, -128.0, None, ALU.max)\
                    .then_inc(sem("xq_done"), 1)

            def diagonal_scales(hf):
                dve.wait_ge(sem("xq_done"), hf + 1)
                link(V.tensor_scalar(half_rows(7, hf), half_rows(5, hf), wsc[0:TT, 4:5], 1.0 / 127.0, ALU.mult, ALU.mult))
                for k in tiles(hf):
                    last = V.tensor_scalar(xn[:, k, 0:TT], ident[0:TT, 0:TT], small[:, 7, k:k + 1], None, ALU.mult)
                last.then_inc(sem("xs_diag"), 1)

            def convolution(hf):
                dve.wait_ge(sem("xs_row"), hf + 1)
                dve.wait_ge(sem("conv_edges"), 1)
                x_row = x_T[:, HN * hf:HN * hf + HN].rearrange("p (b s) -> p b s", b=HB)
                batches = slice(HB * hf, HB * hf + HB)
                cw = la("convw")
                for c in range(FC):
                    if c % 2 == 0:
                        dve.wait_ge(sem("h1_mm"), 2 * hf + c // 2 + 1)
                    V.tensor_tensor(hconv[:, c, batches, 1:1 + SQ],
                                    bank[HALF_BANKS[hf][c // 2]][:, HN * (c % 2):HN * (c % 2) + HN].rearrange("p (b s) -> p b s", b=HB),
                                    x_row, ALU.mult).then_inc(sem("h1_read"), 1)
                for c in range(FC):
                    y = hid[0][:, NTOK * c + HN * hf:NTOK * c + HN * hf + HN].rearrange("p (b s) -> p b s", b=HB)
                    dve.wait_ge(sem("tap0"), FC * hf + c + 1)
                    link(V.scalar_tensor_tensor(y, hconv[:, c, batches, 1:1 + SQ], cw[:, 3 * c + 1:3 * c + 2], y, ALU.mult, ALU.add))
                    V.scalar_tensor_tensor(y, hconv[:, c, batches, 2:2 + SQ], cw[:, 3 * c + 2:3 * c + 3], y, ALU.mult, ALU.add)\
                        .then_inc(sem("conv_done"), 1)

            def hidden_scales(hf):
                for i, k in enumerate(tiles(hf)):
                    dve.wait_ge(sem("h_tok"), k + 1)
                    last = V.tensor_reduce(small[:, 5, k:k + 1], bank[HALF_BANKS[hf][i]][0:TT, :], AX.X, ALU.max,
                                           apply_absolute_value=True)
                link(last)
                link(V.tensor_scalar(half_rows(5, hf), half_rows(5, hf), 1e-5, None, ALU.max))
                link(V.reciprocal(half_rows(6, hf), half_rows(5, hf)))
                V.tensor_scalar(half_rows(6, hf), half_rows(6, hf), 127.0, None, ALU.mult).then_inc(sem("h_scale"), 1)
                link(V.tensor_scalar(half_rows(7, hf), half_rows(5, hf), wsc[0:TT, 5:6], 1.0 / 127.0, ALU.mult, ALU.mult))
                link(V.tensor_scalar(half_rows(7, hf), half_rows(7, hf), tgate[0:TT, 3:4], None, ALU.mult))

            def clip_hidden(hf):
                for k in tiles(hf):
                    dve.wait_ge(sem("h_round"), k + 1)
                    link(V.tensor_scalar(hq_f32[:, k, :], hq_f32[:, k, :], MAGIC, 127.0, ALU.subtract, ALU.min))
                    V.tensor_scalar(hq_view[:, F * k:F * k + F], hq_f32[:, k, :], -128.0, None, ALU.max).then_inc(sem("hq_done"), 1)

            def add_output(hf):
                for i, k in enumerate(tiles(hf)):
                    dve.wait_ge(sem("y2_mm"), k + 1)
                    V.scalar_tensor_tensor(x_tok[:, k, :], bank[HALF_BANKS[hf][i]][0:TT, 0:D], small[:, 7, k:k + 1],
                                           x_tok[:, k, :], ALU.mult, ALU.add).then_inc(sem("x4_done"), 1)

            def pair_max(p):
                dve.wait_ge(sem("s1_mm"), p + 1)
                V.tensor_reduce(den1[:, p % 2, 0:1], ps_all[:, 0:NCH, 0:CH], AX.XY, ALU.max, negate=True)\
                    .then_inc(sem("max1_done"), 1)

            def pair_output(p):
                den = den1[:, p % 2, :]
                dve.wait_ge(sem("exp1_done"), p + 1)
                link(V.reciprocal(den[:, 2:3], den[:, 1:2]))
                dve.wait_ge(sem("pv1_done"), p + 1)
                V.tensor_scalar(c_nat, bank[5][:, 0:D], den[:, 2:3], None, ALU.mult).then_inc(sem("c_nat"), 1)

            pair_max(0)
            for p in range(NB // 2 - 1):
                pair_max(p + 1)
                pair_output(p)
            add_attention(0)
            layernorm("ln3", tiles(0), 1)
            quantise_x(0)
            pair_output(NB // 2 - 1)
            diagonal_scales(0)
            add_attention(1)
            variances("ln3", tiles(1))
            convolution(0)
            normalise_rows("ln3", tiles(1), 2)
            quantise_x(1)
            diagonal_scales(1)
            hidden_scales(0)
            convolution(1)
            clip_hidden(0)
            hidden_scales(1)
            clip_hidden(1)
            add_output(0)
            add_output(1)

        @block.gpsimd
        def _(pool):
            G = nc.gpsimd
            G.memset(minus_half[:, :], -0.5).then_inc(sem("minus_half"), 1)
            pool.wait_ge(sem("minus_half"), 1)

            def rsqrt(name, ks=range(NTT), part=1):
                k = slice(ks[0], ks[-1] + 1)
                pool.wait_ge(sem(f"{name}_var"), part)
                G.tensor_scalar(rstd[:, k], meanvar[:, k, 1], 1e-5, None, ALU.add).then_inc(sem(f"{name}_eps"), 1)
                pool.wait_ge(sem(f"{name}_eps"), part)
                G.tensor_tensor(rstd[:, k], rstd[:, k], minus_half[:, k], ALU.pow).then_inc(sem(f"{name}_rstd"), 1)

            G.memset(ones[:, :], 1.0).then_inc(sem("ones"), 1)
            G.memset(magic[:, :], MAGIC).then_inc(sem("magic"), 1)
            rsqrt("ln0")
            mask = ea("mask").unsqueeze(2).to_broadcast([128, H, SQ])
            pool.wait_ge(sem("early_loaded"), 16)
            pool.wait_ge(sem("q_parts"), 1)

            def body(r, par, attn, rows, keys):
                b = 2 * r + par
                o = 1 - par
                if keys:
                    if isinstance(b, int) and b == 0:
                        pool.wait_ge(sem("q_first"), 16 * 12)
                    if not isinstance(b, int) or b >= 0:
                        pool.wait_ge(sem("row_mm"), SROWS * (b + 1))
                        pool.wait_ge(sem(f"q_stacked{par}"), q_count(r, par))
                    for k, (dst, src) in enumerate(((qd_hi, q_hi), (qd_lo, q_lo))):
                        s = src[:, :].bitcast(fp32).rearrange("p (b q) -> p b q", b=NB)[:, b + 2, :]
                        G.tensor_tensor(dst[:, par, :].rearrange("p (h q) -> p h q", h=H),
                                        s.unsqueeze(1).to_broadcast([128, H, SQ]), mask, ALU.mult)\
                            .then_inc(sem(("qd_hi_done", "qd_done")[k]), 1)

            def body_and_weights(r, par, attn, rows, keys):
                body(r, par, attn, rows, keys)
                if isinstance(r, int) and (r, par) == (-1, 0):
                    pool.wait_ge(sem("qd_done"), 1)
                    for g in range(QG):
                        for blk, part in enumerate((qd_hi, qd_lo, qd_hi)):
                            pool.dma_start(q_st[32 * blk:32 * blk + 32, 0, GC * g:GC * g + GC].bitcast(fp32),
                                           part[32 * g:32 * g + 32, 0, GC * g:GC * g + GC].bitcast(fp32))\
                                .then_inc(sem("q_first"), 16)
                if isinstance(r, int) and (r, par) == (0, 0):
                    pool.dma_start(late[:, :], late_d).then_inc(sem("late_loaded"), 16)
                if isinstance(r, int) and (r, par) == (0, 1):
                    pool.dma_start(w1_sb[:, :].rearrange("p (e f) -> p e f", e=E), w1_v).then_inc(sem("w1_loaded"), 16)

            steps(pool, body_and_weights)
            pool.wait_ge(sem("w1_loaded"), 16)
            pool.wait_ge(sem("q_stacked1"), 16 * 13 * NB // 2)
            pool.wait_ge(sem("st_done"), NT * NB)
            pool.wait_ge(sem("row_mm"), SROWS * NB)
            G.tensor_copy(pick[:, :], ident[0:E, 0:E])

            def split(e, src, hi, lo, name, used):
                if e >= 3:
                    pool.wait_ge(sem(used), FC * (e - 2))
                w = src[:, F * e:F * e + F]
                if not dve_rounds(name, e):
                    G.tensor_copy(hi[:, e % 3, :], w).then_inc(sem(name + "_hi"), 1)
                pool.wait_ge(sem(name + "_hi"), e + 1)
                G.tensor_tensor(lo[:, e % 3, :], w, hi[:, e % 3, :].bitcast(fp32), ALU.subtract).then_inc(sem(name), 1)

            def split_w1(e):
                split(e, w1_sb[:, :], w1_hi, w1_lo, "w1_parts", "up_mm")

            def split_w2(e):
                split(e, w2_sb, w2_hi, w2_lo, "w2_parts", "down_mm")

            for e in range(3):
                split_w1(e)
            pool.wait_ge(sem("w2_loaded"), 16)
            split_w2(0)
            rsqrt("ln1")
            split_w2(1)
            split_w2(2)
            for e in range(3, E):
                split_w1(e)
                if e == 4:
                    pool.wait_ge(sem("w_abs"), 2)
                    G.partition_all_reduce(wsc[:, 2:4], wsc[:, 0:2], 128, bass.bass_isa.ReduceOp.add).then_inc(sem("w_mean"), 1)
                split_w2(e)
            pool.wait_ge(sem("up_mm"), FC * E)
            G.memset(hconv[:, :, :, 0], 0.0)
            G.memset(hconv[:, :, :, SP1 - 1], 0.0).then_inc(sem("conv_edges"), 1)
            pool.wait_ge(sem("moe_y"), 1)
            G.memset(qt_pad, 0.0).then_inc(sem("qt_zero"), 1)
            rsqrt("ln2")
            for hf in range(2):
                rsqrt("ln3", range(HT * hf, HT * hf + HT), hf + 1)


def kernel(**inputs):
    import numpy as np
    import concourse.bacc as bacc
    from concourse.bass_utils import run_bass_kernel_spmd as run

    a = {k: np.asarray(v) for k, v in inputs.items()}
    f4 = np.float32

    def pack(table, n, parts):
        out = np.zeros((128, n), f4)
        for name, arr in parts.items():
            at, w = table[name]
            out[:arr.shape[0], at:at + w] = arr
        return out

    col = lambda v: v.reshape(128, 1)
    heads = np.arange(128) // DH
    sel = np.zeros((128, 128), f4)
    for j in range(4):
        sel[32 * j + DEN, 32 * j:32 * j + 32] = 1
    sel2 = sel + np.roll(sel, 64, axis=0)
    wo = a["L0_xattn_Wo"]
    slots = np.zeros((6, 128, D), f4)
    for h in range(H):
        g, i = h // 3, h % 3
        slot = 5 if h == H - 1 else 3 * (g // 4) + i
        for row in ([32 * g + DH * i] if g < 4 else [32 * (g - 4) + DH * i, 32 * (g - 2) + DH * i]):
            slots[slot, row:row + DH] = wo[DH * h:DH * h + DH]
    gates = np.broadcast_to(np.concatenate([a["g_xattn"], a["g_ffn"]])[None], (128, 4))
    early = pack(EARLY, EARLY_N, {
        "ident": np.eye(128, dtype=f4), "sel": sel, "sel2": sel2, "mask": (heads[:, None] == np.arange(H)[None]).astype(f4),
        "first": np.broadcast_to(np.arange(E, 0, -1, dtype=f4)[None], (128, E)),
        "wq": a["L0_xattn_Wq"], "wk": a["L0_xattn_Wk"], "wv": a["L0_xattn_Wv"],
        "bq": col(a["L0_xattn_bq"]), "bk": col(a["L0_xattn_bk"]), "bv": col(a["L0_xattn_bv"]),
        "bo": col(a["L0_xattn_bo"]), "gates": gates})
    late = pack(LATE, LATE_N, {
        "wo": wo, "woslot": slots.transpose(1, 0, 2).reshape(128, 6 * D), "wr": a["L0_ffn_Wr"],
        "wq1": a["L1_xattn_Wq"], "wk1": a["L1_xattn_Wk"], "wv1": a["L1_xattn_Wv"], "wo1": a["L1_xattn_Wo"].T,
        "bq1": col(a["L1_xattn_bq"]), "bv1": col(a["L1_xattn_bv"]), "bo1": col(a["L1_xattn_bo"]),
        "convw": a["L1_ffn_conv_w"].reshape(FC, 128, 3).transpose(1, 0, 2).reshape(128, FC * 3),
        "convb": a["L1_ffn_conv_b"].reshape(FC, 128).T,
        "b1": a["L0_ffn_b1"].reshape(E * FC, 128).T, "b2": a["L0_ffn_b2"],
        "fw1": a["L1_ffn_w1"].T,
        "fw2": a["L1_ffn_w2"].reshape(D, FC, 128).transpose(2, 1, 0).reshape(128, F)})
    arrays = {"x_in": a["x"].reshape(NTOK, D), "ctx_in": a["ctx_1024"], "early_in": early, "late_in": late,
              "w1_in": a["L0_ffn_W1"], "w2_in": a["L0_ffn_W2"]}
    arrays = {k: np.ascontiguousarray(v) for k, v in arrays.items()}
    nc = bacc.Bacc("TRN2", target_bir_lowering=False, num_devices=1)
    args = [nc.dram_tensor(k, v.shape, mybir.dt.from_np(v.dtype), kind="ExternalInput").ap() for k, v in arrays.items()]
    out = nc.dram_tensor("x_out", (NTOK, D), mybir.dt.float32, kind="ExternalOutput").ap()
    flamingo_kernel(nc, *args, out)
    r = run(nc, [arrays], core_ids=[0])
    return r.results[0]["x_out"].reshape(NB, SQ, D)
```
